# Optimizing a Trainium2 kernel written in Bass

```python
import numpy as np
import jax
import jax.numpy as jnp

def _softmax(x, axis=-1):
    return jax.nn.softmax(x, axis=axis)

def _gelu(x):
    return jax.nn.gelu(x, approximate=True)

def _silu(x):
    return jax.nn.silu(x)

def _sigmoid(x):
    return jax.nn.sigmoid(x)

def _layernorm(x, axis=-1, eps=1e-05):
    m = jnp.mean(x, axis=axis, keepdims=True)
    v = jnp.var(x, axis=axis, keepdims=True)
    return (x - m) / jnp.sqrt(v + eps)

def _scatter_add(tgt, idx, src, axis=0):
    return tgt.at[idx].add(src)

def _segment_sum(src, seg, n):
    return jax.ops.segment_sum(src, seg, n)
kernel_name = 'mk_flamingo_gated_d4_seqx_r4_675da3'

def setup_inputs(seed: int=0):
    np.random.seed(seed)
    _w = jnp.asarray

    def _rec_inputs():
        import jax
        import jax.numpy as jnp
        _rk = jax.random.key(seed)
        x = -0.0003929 + 0.9999 * jax.random.normal(jax.random.fold_in(_rk, 1), (8, 112, 512), jnp.float32)
        _lenS = 112 - jax.random.randint(jax.random.fold_in(_rk, 7), (8,), 0, max(1, 112 // 4) + 1, jnp.int32)
        _lenS2 = 375 - jax.random.randint(jax.random.fold_in(_rk, 8), (8,), 0, max(1, 375 // 4) + 1, jnp.int32)
        _ctx_2048P = jax.random.normal(jax.random.fold_in(_rk, 11), (8, 16, 512), jnp.float32)
        _ctx_2048c = jax.random.dirichlet(jax.random.fold_in(_rk, 511), 0.3 * jnp.ones((16,), jnp.float32), (8, 375))
        _ctx_2048t = jnp.einsum('bsk,bkd->bsd', _ctx_2048c, _ctx_2048P)
        _ctx_2048t = _ctx_2048t * jax.lax.rsqrt(jnp.mean(jnp.square(_ctx_2048t)) + 1e-12) * 0.953939
        ctx_2048 = -1.39393e-06 + 0.999914 * (_ctx_2048t + 0.3 * jax.random.normal(jax.random.fold_in(_rk, 611), (8, 375, 512), jnp.float32))
        itok_BxS_0_1023 = jax.random.randint(jax.random.fold_in(_rk, 12), (8, 112), 0, 256, jnp.int32)
        _validS = jnp.arange(112)[None, :] < _lenS[:, None]
        _validS2 = jnp.arange(375)[None, :] < _lenS2[:, None]
        _causal = jnp.tril(jnp.ones((112, 112), dtype=bool))
        mask_BxSx4224_bf0 = jnp.logical_not(jnp.ones((8, 112, 1056), dtype=bool))
        _g = jax.random.normal(jax.random.fold_in(_rk, 9001), (2, 4), jnp.float32)
        _g = jnp.sign(_g) * jnp.maximum(jnp.abs(_g), 1.0) + (_g == 0) * 1.0
        g_xattn = _g[0]
        g_ffn = _g[1]
        return (x, ctx_2048, itok_BxS_0_1023, mask_BxSx4224_bf0, g_xattn, g_ffn)
    x, ctx_2048, itok_BxS_0_1023, mask_BxSx4224_bf0, g_xattn, g_ffn = _rec_inputs()

    def _L0_xattn_setup():
        import jax, jax.numpy as jnp
        import numpy as np
        B, Lq, Lk = (2, 1024, 256)
        Q_DIM, KV_DIM = (512, 512)
        H, HD = (16, 128)
        KVC, QC, R = (128, 192, 64)
        LOOKBACK = 8
        NEG = -1e+30

        def _rope(x, L):
            half = x.shape[-1] // 2
            inv_freq = 1.0 / 10000.0 ** (jnp.arange(half, dtype=jnp.float32) / half)
            ang = jnp.arange(L, dtype=jnp.float32)[:, None] * inv_freq
            cos, sin = (jnp.cos(ang), jnp.sin(ang))
            x1, x2 = (x[..., :half], x[..., half:])
            return jnp.concatenate([x1 * cos - x2 * sin, x1 * sin + x2 * cos], axis=-1)
        key = jax.random.key(seed)
        ks = jax.random.split(key, 11)

        def w(k, shape, fan_in):
            return jax.random.normal(k, shape, jnp.float32) / np.sqrt(fan_in).astype(np.float32)
        return {'q': jax.random.normal(ks[0], (B, Lq, Q_DIM), jnp.float32), 'kv': jax.random.normal(ks[1], (B, Lk, KV_DIM), jnp.float32), 'seg_id': jnp.sort(jax.random.randint(ks[2], (B, Lq), 0, Lk), axis=-1), 'W_kvc': w(ks[3], (KV_DIM, KVC), KV_DIM), 'W_dq': w(ks[4], (Q_DIM, QC), Q_DIM), 'W_uq': w(ks[5], (QC, H * HD), QC), 'W_qr': w(ks[6], (QC, H * R), QC), 'W_uk': w(ks[7], (KVC, H * HD), KVC), 'W_kr': w(ks[8], (KVC, R), KVC), 'W_uv': w(ks[9], (KVC, H * HD), KVC), 'W_o': w(ks[10], (H * HD, Q_DIM), H * HD)}
    _L0_xattn_all = _L0_xattn_setup()
    _L0_xattn_in = {k: v for k, v in _L0_xattn_all.items() if k in ('W_kvc', 'W_dq', 'W_uq', 'W_qr', 'W_uk', 'W_kr', 'W_uv', 'W_o')}
    del _L0_xattn_all

    def _L0_ffn_setup():
        import jax, jax.numpy as jnp
        import numpy as np
        B, S, D, F, E, SH, K = (2, 512, 512, 256, 16, 2, 2)

        def _experts_all(x, g, gb, w1, b1, w2, b2):
            y = jax.nn.gelu(jnp.einsum('bsd,edf->bsef', x, g) + gb, approximate=False)
            y = y * (jnp.einsum('bsd,edf->bsef', x, w1) + b1)
            return jnp.einsum('bsef,efd->bsed', y, w2) + b2
        key = jax.random.key(seed)
        ks = jax.random.split(key, 8)
        std = 0.02
        mk = lambda k, sh: jax.random.normal(k, sh, jnp.float32) * std
        return {'x': jax.random.normal(ks[0], (B, S, D), jnp.float32), 'wa': mk(ks[1], (D, E)), 'rg': mk(ks[2], (E, D, F)), 'rgb': jnp.zeros((E, F), jnp.float32), 'rw1': mk(ks[3], (E, D, F)), 'rb1': jnp.zeros((E, F), jnp.float32), 'rw2': mk(ks[4], (E, F, D)), 'rb2': jnp.zeros((E, D), jnp.float32), 'sg': mk(ks[5], (SH, D, F)), 'sgb': jnp.zeros((SH, F), jnp.float32), 'sw1': mk(ks[6], (SH, D, F)), 'sb1': jnp.zeros((SH, F), jnp.float32), 'sw2': mk(ks[7], (SH, F, D)), 'sb2': jnp.zeros((SH, D), jnp.float32)}
    _L0_ffn_all = _L0_ffn_setup()
    _L0_ffn_in = {k: v for k, v in _L0_ffn_all.items() if k in ('wa', 'rg', 'rgb', 'rw1', 'rb1', 'rw2', 'rb2', 'sg', 'sgb', 'sw1', 'sb1', 'sw2', 'sb2')}
    del _L0_ffn_all

    def _L1_xattn_setup():
        import jax, jax.numpy as jnp
        import numpy as np
        D_MODEL = 512
        NUM_HEADS = 16
        HEAD_DIM = D_MODEL // NUM_HEADS
        key = jax.random.key(seed)
        ks = jax.random.split(key, 10)
        B, S, T = (4, 1024, 256)
        s = 1.0 / np.sqrt(D_MODEL)
        inp = {'query': jax.random.normal(ks[0], (B, S, D_MODEL), jnp.float32), 'key_value': jax.random.normal(ks[1], (B, T, D_MODEL), jnp.float32), 'Wq': jax.random.normal(ks[2], (D_MODEL, D_MODEL), jnp.float32) * s, 'bq': jnp.zeros((D_MODEL,), jnp.float32), 'Wk': jax.random.normal(ks[3], (D_MODEL, D_MODEL), jnp.float32) * s, 'bk': jnp.zeros((D_MODEL,), jnp.float32), 'Wv': jax.random.normal(ks[4], (D_MODEL, D_MODEL), jnp.float32) * s, 'bv': jnp.zeros((D_MODEL,), jnp.float32), 'Wo': jax.random.normal(ks[5], (D_MODEL, D_MODEL), jnp.float32) * s, 'bo': jnp.zeros((D_MODEL,), jnp.float32)}
        return inp
    _L1_xattn_all = _L1_xattn_setup()
    _L1_xattn_in = {k: v for k, v in _L1_xattn_all.items() if k in ('Wq', 'bq', 'Wk', 'bk', 'Wv', 'bv', 'Wo', 'bo')}
    del _L1_xattn_all

    def _L1_ffn_setup():
        import jax, jax.numpy as jnp
        import numpy as np
        B, S, H = (1, 512, 512)
        E, K, I = (16, 4, 352)
        IS = 704
        CAP = 256
        key = jax.random.key(seed)
        ks = jax.random.split(key, 8)
        sc = 0.02
        return {'hidden_states': jax.random.normal(ks[0], (B, S, H), jnp.float32), 'gate_w': jax.random.normal(ks[1], (E, H), jnp.float32) * sc, 'w_gate': jax.random.normal(ks[2], (E, H, I), jnp.float32) * sc, 'w_up': jax.random.normal(ks[3], (E, H, I), jnp.float32) * sc, 'w_down': jax.random.normal(ks[4], (E, I, H), jnp.float32) * sc, 'sw_gate': jax.random.normal(ks[5], (H, IS), jnp.float32) * sc, 'sw_up': jax.random.normal(ks[6], (H, IS), jnp.float32) * sc, 'sw_down': jax.random.normal(ks[7], (IS, H), jnp.float32) * sc}
    _L1_ffn_all = _L1_ffn_setup()
    _L1_ffn_in = {k: v for k, v in _L1_ffn_all.items() if k in ('gate_w', 'w_gate', 'w_up', 'w_down', 'sw_gate', 'sw_up', 'sw_down')}
    del _L1_ffn_all

    def _L2_xattn_setup():
        import jax, jax.numpy as jnp
        import numpy as np
        from jax import lax
        LN_EPS = 1e-05
        key = jax.random.key(seed)
        ks = jax.random.split(key, 8)
        B, S, T, D = (4, 128, 512, 512)
        scale = 0.02
        return {'Z': jax.random.normal(ks[0], (B, S, D), dtype=jnp.float32), 'kv': jax.random.normal(ks[1], (B, T, D), dtype=jnp.float32), 'decay': jnp.float32(0.9), 'W_in': jax.random.normal(ks[2], (D, D), dtype=jnp.float32) * scale, 'b_in': jnp.zeros((D,), dtype=jnp.float32), 'W_out': jax.random.normal(ks[3], (D, D), dtype=jnp.float32) * scale, 'b_out': jnp.zeros((D,), dtype=jnp.float32), 'gamma': jnp.ones((D,), dtype=jnp.float32), 'beta': jnp.zeros((D,), dtype=jnp.float32)}
    _L2_xattn_all = _L2_xattn_setup()
    _L2_xattn_in = {k: v for k, v in _L2_xattn_all.items() if k in ('decay', 'W_in', 'b_in', 'W_out', 'b_out', 'gamma', 'beta')}
    del _L2_xattn_all

    def _L2_ffn_setup():
        import jax, jax.numpy as jnp
        import numpy as np
        from jax import lax
        H = 512
        I = 352
        E = 16
        TOP_K = 6
        IS = 2 * I

        def _swiglu(x, w13_, w2_):
            gu = x @ w13_.T
            g, u = jnp.split(gu, 2, axis=-1)
            return jax.nn.silu(g) * u @ w2_.T
        key = jax.random.key(seed)
        ks = jax.random.split(key, 6)
        return {'hidden_states': jax.random.normal(ks[0], (1, 512, H), jnp.float32), 'gate_w': jax.random.normal(ks[1], (E, H), jnp.float32) * 0.02, 'w13': jax.random.normal(ks[2], (E, 2 * I, H), jnp.float32) * 0.02, 'w2': jax.random.normal(ks[3], (E, H, I), jnp.float32) * 0.02, 'sw13': jax.random.normal(ks[4], (2 * IS, H), jnp.float32) * 0.02, 'sw2': jax.random.normal(ks[5], (H, IS), jnp.float32) * 0.02}
    _L2_ffn_all = _L2_ffn_setup()
    _L2_ffn_in = {k: v for k, v in _L2_ffn_all.items() if k in ('gate_w', 'w13', 'w2', 'sw13', 'sw2')}
    del _L2_ffn_all

    def _L3_xattn_setup():
        import jax, jax.numpy as jnp
        import numpy as np
        import math
        DIM = 512
        B, Q_LEN, KV_LEN = (8, 128, 1024)
        key = jax.random.key(seed)
        ks = jax.random.split(key, 8)
        x = jax.random.normal(ks[0], (B, Q_LEN, DIM), dtype=jnp.float32)
        mask = jnp.zeros((B, Q_LEN, KV_LEN + Q_LEN), dtype=bool)
        k_cache = jax.random.normal(ks[1], (B, KV_LEN, DIM), dtype=jnp.float32)
        v_cache = jax.random.normal(ks[2], (B, KV_LEN, DIM), dtype=jnp.float32)
        scale = 1.0 / math.sqrt(DIM)
        wq = jax.random.normal(ks[3], (DIM, DIM), dtype=jnp.float32) * scale
        wk = jax.random.normal(ks[4], (DIM, DIM), dtype=jnp.float32) * scale
        wv = jax.random.normal(ks[5], (DIM, DIM), dtype=jnp.float32) * scale
        wo = jax.random.normal(ks[6], (DIM, DIM), dtype=jnp.float32) * scale
        return {'x': x, 'mask': mask, 'k_cache': k_cache, 'v_cache': v_cache, 'wq': wq, 'wk': wk, 'wv': wv, 'wo': wo}
    _L3_xattn_all = _L3_xattn_setup()
    _L3_xattn_in = {k: v for k, v in _L3_xattn_all.items() if k in ('wq', 'wk', 'wv', 'wo')}
    del _L3_xattn_all

    def _L3_ffn_setup():
        import jax, jax.numpy as jnp
        import numpy as np
        D_MODEL = 512
        HIDDEN = int(2 * D_MODEL * 4 / 3)

        def ternary_quant(w):
            s = jnp.mean(jnp.abs(w))
            q = jnp.clip(jnp.round(w / s), -1.0, 1.0) * s
            return w + jax.lax.stop_gradient(q - w)
        key = jax.random.key(seed)
        k0, k1, k2, k3 = jax.random.split(key, 4)
        x = jax.random.normal(k0, (4, 1024, D_MODEL), dtype=jnp.float32)
        std_in = 1.0 / np.sqrt(D_MODEL)
        std_h = 1.0 / np.sqrt(HIDDEN)
        w1 = jax.random.uniform(k1, (HIDDEN, D_MODEL), jnp.float32, -std_in, std_in)
        w3 = jax.random.uniform(k2, (HIDDEN, D_MODEL), jnp.float32, -std_in, std_in)
        w2 = jax.random.uniform(k3, (D_MODEL, HIDDEN), jnp.float32, -std_h, std_h)
        return {'x': x, 'w1': w1, 'w3': w3, 'w2': w2}
    _L3_ffn_all = _L3_ffn_setup()
    _L3_ffn_in = {k: v for k, v in _L3_ffn_all.items() if k in ('w1', 'w3', 'w2')}
    del _L3_ffn_all
    return {'x': x, 'ctx_2048': ctx_2048, 'itok_BxS_0_1023': itok_BxS_0_1023, 'mask_BxSx4224_bf0': mask_BxSx4224_bf0, 'g_xattn': g_xattn, 'g_ffn': g_ffn, 'L0_xattn_W_kvc': _L0_xattn_in['W_kvc'], 'L0_xattn_W_dq': _L0_xattn_in['W_dq'], 'L0_xattn_W_uq': _L0_xattn_in['W_uq'], 'L0_xattn_W_qr': _L0_xattn_in['W_qr'], 'L0_xattn_W_uk': _L0_xattn_in['W_uk'], 'L0_xattn_W_kr': _L0_xattn_in['W_kr'], 'L0_xattn_W_uv': _L0_xattn_in['W_uv'], 'L0_xattn_W_o': _L0_xattn_in['W_o'], 'L0_ffn_wa': _L0_ffn_in['wa'], 'L0_ffn_rg': _L0_ffn_in['rg'], 'L0_ffn_rgb': _L0_ffn_in['rgb'], 'L0_ffn_rw1': _L0_ffn_in['rw1'], 'L0_ffn_rb1': _L0_ffn_in['rb1'], 'L0_ffn_rw2': _L0_ffn_in['rw2'], 'L0_ffn_rb2': _L0_ffn_in['rb2'], 'L0_ffn_sg': _L0_ffn_in['sg'], 'L0_ffn_sgb': _L0_ffn_in['sgb'], 'L0_ffn_sw1': _L0_ffn_in['sw1'], 'L0_ffn_sb1': _L0_ffn_in['sb1'], 'L0_ffn_sw2': _L0_ffn_in['sw2'], 'L0_ffn_sb2': _L0_ffn_in['sb2'], 'L1_xattn_Wq': _L1_xattn_in['Wq'], 'L1_xattn_bq': _L1_xattn_in['bq'], 'L1_xattn_Wk': _L1_xattn_in['Wk'], 'L1_xattn_bk': _L1_xattn_in['bk'], 'L1_xattn_Wv': _L1_xattn_in['Wv'], 'L1_xattn_bv': _L1_xattn_in['bv'], 'L1_xattn_Wo': _L1_xattn_in['Wo'], 'L1_xattn_bo': _L1_xattn_in['bo'], 'L1_ffn_gate_w': _L1_ffn_in['gate_w'], 'L1_ffn_w_gate': _L1_ffn_in['w_gate'], 'L1_ffn_w_up': _L1_ffn_in['w_up'], 'L1_ffn_w_down': _L1_ffn_in['w_down'], 'L1_ffn_sw_gate': _L1_ffn_in['sw_gate'], 'L1_ffn_sw_up': _L1_ffn_in['sw_up'], 'L1_ffn_sw_down': _L1_ffn_in['sw_down'], 'L2_xattn_decay': _L2_xattn_in['decay'], 'L2_xattn_W_in': _L2_xattn_in['W_in'], 'L2_xattn_b_in': _L2_xattn_in['b_in'], 'L2_xattn_W_out': _L2_xattn_in['W_out'], 'L2_xattn_b_out': _L2_xattn_in['b_out'], 'L2_xattn_gamma': _L2_xattn_in['gamma'], 'L2_xattn_beta': _L2_xattn_in['beta'], 'L2_ffn_gate_w': _L2_ffn_in['gate_w'], 'L2_ffn_w13': _L2_ffn_in['w13'], 'L2_ffn_w2': _L2_ffn_in['w2'], 'L2_ffn_sw13': _L2_ffn_in['sw13'], 'L2_ffn_sw2': _L2_ffn_in['sw2'], 'L3_xattn_wq': _L3_xattn_in['wq'], 'L3_xattn_wk': _L3_xattn_in['wk'], 'L3_xattn_wv': _L3_xattn_in['wv'], 'L3_xattn_wo': _L3_xattn_in['wo'], 'L3_ffn_w1': _L3_ffn_in['w1'], 'L3_ffn_w3': _L3_ffn_in['w3'], 'L3_ffn_w2': _L3_ffn_in['w2']}

def reference(x, ctx_2048, itok_BxS_0_1023, mask_BxSx4224_bf0, g_xattn, g_ffn, L0_xattn_W_kvc, L0_xattn_W_dq, L0_xattn_W_uq, L0_xattn_W_qr, L0_xattn_W_uk, L0_xattn_W_kr, L0_xattn_W_uv, L0_xattn_W_o, L0_ffn_wa, L0_ffn_rg, L0_ffn_rgb, L0_ffn_rw1, L0_ffn_rb1, L0_ffn_rw2, L0_ffn_rb2, L0_ffn_sg, L0_ffn_sgb, L0_ffn_sw1, L0_ffn_sb1, L0_ffn_sw2, L0_ffn_sb2, L1_xattn_Wq, L1_xattn_bq, L1_xattn_Wk, L1_xattn_bk, L1_xattn_Wv, L1_xattn_bv, L1_xattn_Wo, L1_xattn_bo, L1_ffn_gate_w, L1_ffn_w_gate, L1_ffn_w_up, L1_ffn_w_down, L1_ffn_sw_gate, L1_ffn_sw_up, L1_ffn_sw_down, L2_xattn_decay, L2_xattn_W_in, L2_xattn_b_in, L2_xattn_W_out, L2_xattn_b_out, L2_xattn_gamma, L2_xattn_beta, L2_ffn_gate_w, L2_ffn_w13, L2_ffn_w2, L2_ffn_sw13, L2_ffn_sw2, L3_xattn_wq, L3_xattn_wk, L3_xattn_wv, L3_xattn_wo, L3_ffn_w1, L3_ffn_w3, L3_ffn_w2):
    import jax
    import jax.numpy as jnp

    def _L0_xattn_ref(q, kv, seg_id, W_kvc, W_dq, W_uq, W_qr, W_uk, W_kr, W_uv, W_o):
        import jax, jax.numpy as jnp
        import numpy as np
        B, Lq, Lk = (2, 1024, 256)
        Q_DIM, KV_DIM = (512, 512)
        H, HD = (16, 128)
        KVC, QC, R = (128, 192, 64)
        LOOKBACK = 8
        NEG = -1e+30

        def _rope(x, L):
            half = x.shape[-1] // 2
            inv_freq = 1.0 / 10000.0 ** (jnp.arange(half, dtype=jnp.float32) / half)
            ang = jnp.arange(L, dtype=jnp.float32)[:, None] * inv_freq
            cos, sin = (jnp.cos(ang), jnp.sin(ang))
            x1, x2 = (x[..., :half], x[..., half:])
            return jnp.concatenate([x1 * cos - x2 * sin, x1 * sin + x2 * cos], axis=-1)
        b, lq, _ = q.shape
        lk = kv.shape[1]
        kv_c = kv @ W_kvc
        q_c = q @ W_dq
        q_nope = (q_c @ W_uq).reshape(b, lq, H, HD).transpose(0, 2, 1, 3)
        q_rope = (q_c @ W_qr).reshape(b, lq, H, R).transpose(0, 2, 1, 3)
        k_nope = (kv_c @ W_uk).reshape(b, lk, H, HD)
        v = (kv_c @ W_uv).reshape(b, lk, H, HD)
        k_rope = kv_c @ W_kr
        q_rope = _rope(q_rope, lq)
        k_rope = _rope(k_rope, lk)
        scale = 1.0 / np.sqrt(HD + R).astype(np.float32)
        scores = (jnp.einsum('bhqd,bkhd->bhqk', q_nope, k_nope) + jnp.einsum('bhqr,bkr->bhqk', q_rope, k_rope)) * scale
        k_ids = jnp.arange(lk)[None, None, :]
        qs = seg_id[:, :, None]
        good = (k_ids <= qs) & (k_ids >= qs - LOOKBACK)
        scores = jnp.where(good[:, None, :, :], scores, NEG)
        attn = jax.nn.softmax(scores, axis=-1)
        out = jnp.einsum('bhqk,bkhd->bqhd', attn, v).reshape(b, lq, H * HD)
        return out @ W_o

    def _L0_ffn_ref(x, wa, rg, rgb, rw1, rb1, rw2, rb2, sg, sgb, sw1, sb1, sw2, sb2):
        import jax, jax.numpy as jnp
        import numpy as np
        B, S, D, F, E, SH, K = (2, 512, 512, 256, 16, 2, 2)

        def _experts_all(x, g, gb, w1, b1, w2, b2):
            y = jax.nn.gelu(jnp.einsum('bsd,edf->bsef', x, g) + gb, approximate=False)
            y = y * (jnp.einsum('bsd,edf->bsef', x, w1) + b1)
            return jnp.einsum('bsef,efd->bsed', y, w2) + b2
        aff = jax.nn.sigmoid(jnp.einsum('bsd,de->bse', x, wa))
        topk_p, topk_i = jax.lax.top_k(aff, K)
        topk_p = topk_p / jnp.sum(topk_p, axis=-1, keepdims=True)
        combine = jnp.sum(jax.nn.one_hot(topk_i, E, dtype=x.dtype) * topk_p[..., None], axis=2)
        routed = jnp.einsum('bsed,bse->bsd', _experts_all(x, rg, rgb, rw1, rb1, rw2, rb2), combine)
        shared = jnp.sum(_experts_all(x, sg, sgb, sw1, sb1, sw2, sb2), axis=2)
        return x + shared + routed

    def _L1_xattn_ref(query, key_value, Wq, bq, Wk, bk, Wv, bv, Wo, bo):
        import jax, jax.numpy as jnp
        import numpy as np
        D_MODEL = 512
        NUM_HEADS = 16
        HEAD_DIM = D_MODEL // NUM_HEADS
        B, S, _ = query.shape
        T = key_value.shape[1]
        Q = query @ Wq.T + bq
        K = key_value @ Wk.T + bk
        V = key_value @ Wv.T + bv
        Q = Q.reshape(B, S, NUM_HEADS, HEAD_DIM).transpose(0, 2, 1, 3)
        K = K.reshape(B, T, NUM_HEADS, HEAD_DIM).transpose(0, 2, 1, 3)
        V = V.reshape(B, T, NUM_HEADS, HEAD_DIM).transpose(0, 2, 1, 3)
        scale = 1.0 / np.sqrt(HEAD_DIM).astype(np.float32)
        scores = jnp.einsum('bhsd,bhtd->bhst', Q, K) * scale
        attn = jax.nn.softmax(scores, axis=-1)
        ctx = jnp.einsum('bhst,bhtd->bhsd', attn, V)
        ctx = ctx.transpose(0, 2, 1, 3).reshape(B, S, D_MODEL)
        return ctx @ Wo.T + bo

    def _L1_ffn_ref(hidden_states, gate_w, w_gate, w_up, w_down, sw_gate, sw_up, sw_down):
        import jax, jax.numpy as jnp
        import numpy as np
        B, S, H = (1, 512, 512)
        E, K, I = (16, 4, 352)
        IS = 704
        CAP = 256
        b, s, h = hidden_states.shape
        x = hidden_states.reshape(-1, h)
        T = x.shape[0]
        scores = jax.nn.softmax(x @ gate_w.T, axis=-1)
        topk_w, topk_i = jax.lax.top_k(scores, K)
        topk_w = topk_w / (topk_w.sum(-1, keepdims=True) + 1e-20)
        flat_i = topk_i.reshape(-1)
        flat_w = topk_w.reshape(-1)
        order = jnp.argsort(flat_i)
        se = flat_i[order]
        counts = jax.ops.segment_sum(jnp.ones_like(flat_i), flat_i, num_segments=E)
        starts = jnp.cumsum(counts) - counts
        rank = jnp.arange(T * K) - starts[se]
        tok = order // K
        slot = jnp.where(rank < CAP, rank, CAP)
        buf = jnp.full((E, CAP + 1), T, dtype=jnp.int32).at[se, slot].set(tok)[:, :CAP]
        wbuf = jnp.zeros((E, CAP + 1), x.dtype).at[se, slot].set(flat_w[order])[:, :CAP]
        xpad = jnp.concatenate([x, jnp.zeros((1, h), x.dtype)], axis=0)
        xg = xpad[buf]
        gact = jax.nn.silu(jnp.einsum('ech,ehi->eci', xg, w_gate))
        mid = gact * jnp.einsum('ech,ehi->eci', xg, w_up)
        eout = jnp.einsum('eci,eih->ech', mid, w_down) * wbuf[..., None]
        y = jnp.zeros((T + 1, h), x.dtype).at[buf.reshape(-1)].add(eout.reshape(-1, h))[:T]
        shared = jax.nn.silu(x @ sw_gate) * (x @ sw_up) @ sw_down
        return (y + shared).reshape(b, s, h)

    def _L2_xattn_ref(Z, kv, decay, W_in, b_in, W_out, b_out, gamma, beta):
        import jax, jax.numpy as jnp
        import numpy as np
        from jax import lax
        LN_EPS = 1e-05
        B, T, D = kv.shape
        K = jax.nn.sigmoid(decay)
        x = jnp.einsum('btd,ed->bte', kv, W_in) + b_in

        def scan_fn(s, xt):
            s = K * s + xt
            return (s, s)
        s0 = jnp.zeros((B, D), dtype=kv.dtype)
        _, states = lax.scan(scan_fn, s0, jnp.swapaxes(x, 0, 1))
        states = jnp.swapaxes(states, 0, 1)
        proj = jnp.einsum('btd,ed->bte', states, W_out) + b_out
        summary = jnp.mean(proj, axis=1, keepdims=True)
        y = Z + summary
        mu = jnp.mean(y, axis=-1, keepdims=True)
        var = jnp.mean((y - mu) ** 2, axis=-1, keepdims=True)
        return (y - mu) / jnp.sqrt(var + LN_EPS) * gamma + beta

    def _L2_ffn_ref(hidden_states, gate_w, w13, w2, sw13, sw2):
        import jax, jax.numpy as jnp
        import numpy as np
        from jax import lax
        H = 512
        I = 352
        E = 16
        TOP_K = 6
        IS = 2 * I

        def _swiglu(x, w13_, w2_):
            gu = x @ w13_.T
            g, u = jnp.split(gu, 2, axis=-1)
            return jax.nn.silu(g) * u @ w2_.T
        B, S, Hd = hidden_states.shape
        x = hidden_states.reshape(-1, Hd)
        T = x.shape[0]
        scores = jax.nn.softmax(x @ gate_w.T, axis=-1)
        topk_w, topk_ids = lax.top_k(scores, TOP_K)
        topk_w = topk_w / (topk_w.sum(-1, keepdims=True) + 1e-20)
        combine = jnp.einsum('tk,tke->te', topk_w, jax.nn.one_hot(topk_ids, E, dtype=topk_w.dtype))

        def body(acc, ew):
            w13_e, w2_e, c_e = ew
            y = _swiglu(x, w13_e, w2_e)
            return (acc + c_e[:, None] * y, None)
        out, _ = lax.scan(body, jnp.zeros_like(x), (w13, w2, combine.T))
        out = out + _swiglu(x, sw13, sw2)
        return out.reshape(B, S, Hd)

    def _L3_xattn_ref(x, mask, k_cache, v_cache, wq, wk, wv, wo):
        import jax, jax.numpy as jnp
        import numpy as np
        import math
        DIM = 512
        B, Q_LEN, KV_LEN = (8, 128, 1024)
        q = jnp.einsum('bsd,ed->bse', x, wq)
        k_new = jnp.einsum('bsd,ed->bse', x, wk)
        v_new = jnp.einsum('bsd,ed->bse', x, wv)
        k = jnp.concatenate([k_cache, k_new], axis=1)
        v = jnp.concatenate([v_cache, v_new], axis=1)
        scale = 1.0 / math.sqrt(q.shape[-1])
        scores = jnp.einsum('bqd,bkd->bqk', q, k) * scale
        attn = jax.nn.softmax(scores, axis=-1)
        out = jnp.einsum('bqk,bkd->bqd', attn, v)
        return jnp.einsum('bqd,ed->bqe', out, wo)

    def _L3_ffn_ref(x, w1, w3, w2):
        import jax, jax.numpy as jnp
        import numpy as np
        D_MODEL = 512
        HIDDEN = int(2 * D_MODEL * 4 / 3)

        def ternary_quant(w):
            s = jnp.mean(jnp.abs(w))
            q = jnp.clip(jnp.round(w / s), -1.0, 1.0) * s
            return w + jax.lax.stop_gradient(q - w)
        w1q = ternary_quant(w1)
        w3q = ternary_quant(w3)
        w2q = ternary_quant(w2)
        h1 = jnp.einsum('bsd,hd->bsh', x, w1q)
        h3 = jnp.einsum('bsd,hd->bsh', x, w3q)
        g = jax.nn.silu(h1) * h3
        return jnp.einsum('bsh,dh->bsd', g, w2q)
    x = x + jnp.tanh(g_xattn[0]) * _L0_xattn_ref(_layernorm(x, axis=-1), ctx_2048, itok_BxS_0_1023, L0_xattn_W_kvc, L0_xattn_W_dq, L0_xattn_W_uq, L0_xattn_W_qr, L0_xattn_W_uk, L0_xattn_W_kr, L0_xattn_W_uv, L0_xattn_W_o)
    x = x + jnp.tanh(g_ffn[0]) * _L0_ffn_ref(_layernorm(x, axis=-1), L0_ffn_wa, L0_ffn_rg, L0_ffn_rgb, L0_ffn_rw1, L0_ffn_rb1, L0_ffn_rw2, L0_ffn_rb2, L0_ffn_sg, L0_ffn_sgb, L0_ffn_sw1, L0_ffn_sb1, L0_ffn_sw2, L0_ffn_sb2)
    x = x + jnp.tanh(g_xattn[1]) * _L1_xattn_ref(_layernorm(x, axis=-1), ctx_2048, L1_xattn_Wq, L1_xattn_bq, L1_xattn_Wk, L1_xattn_bk, L1_xattn_Wv, L1_xattn_bv, L1_xattn_Wo, L1_xattn_bo)
    x = x + jnp.tanh(g_ffn[1]) * _L1_ffn_ref(_layernorm(x, axis=-1), L1_ffn_gate_w, L1_ffn_w_gate, L1_ffn_w_up, L1_ffn_w_down, L1_ffn_sw_gate, L1_ffn_sw_up, L1_ffn_sw_down)
    x = x + jnp.tanh(g_xattn[2]) * _L2_xattn_ref(_layernorm(x, axis=-1), ctx_2048, L2_xattn_decay, L2_xattn_W_in, L2_xattn_b_in, L2_xattn_W_out, L2_xattn_b_out, L2_xattn_gamma, L2_xattn_beta)
    x = x + jnp.tanh(g_ffn[2]) * _L2_ffn_ref(_layernorm(x, axis=-1), L2_ffn_gate_w, L2_ffn_w13, L2_ffn_w2, L2_ffn_sw13, L2_ffn_sw2)
    x = x + jnp.tanh(g_xattn[3]) * _L3_xattn_ref(_layernorm(x, axis=-1), mask_BxSx4224_bf0, ctx_2048, ctx_2048, L3_xattn_wq, L3_xattn_wk, L3_xattn_wv, L3_xattn_wo)
    x = x + jnp.tanh(g_ffn[3]) * _L3_ffn_ref(_layernorm(x, axis=-1), L3_ffn_w1, L3_ffn_w3, L3_ffn_w2)
    return x

_drawn_inputs = setup_inputs


def setup_inputs(seed=0):
    import zlib

    import numpy as np

    out = dict(_drawn_inputs(seed))
    spreads = {'L0_ffn_rgb': (0.0, 0.8),
     'L0_ffn_rb1': (0.0, 0.8),
     'L0_ffn_rb2': (0.0, 0.1),
     'L0_ffn_sgb': (0.0, 0.8),
     'L0_ffn_sb1': (0.0, 0.8),
     'L0_ffn_sb2': (0.0, 0.1),
     'L1_xattn_bq': (0.0, 0.557),
     'L1_xattn_bk': (0.0, 2.0),
     'L1_xattn_bv': (0.0, 0.1),
     'L1_xattn_bo': (0.0, 0.1),
     'L2_xattn_b_in': (0.0, 0.1),
     'L2_xattn_b_out': (0.0, 0.338),
     'L2_xattn_gamma': (1.0, 0.2),
     'L2_xattn_beta': (0.0, 0.354)}
    factors = {'g_ffn': 8.0,
     'L0_ffn_rg': 3.911,
     'L0_ffn_rw1': 3.698,
     'L0_ffn_rw2': 3.601,
     'L1_ffn_gate_w': 5.116,
     'L1_ffn_w_gate': 4.608,
     'L1_ffn_w_up': 4.62,
     'L1_ffn_w_down': 4.604,
     'L1_ffn_sw_gate': 4.044,
     'L1_ffn_sw_up': 3.954,
     'L1_ffn_sw_down': 3.954,
     'L2_ffn_gate_w': 8.0,
     'L2_ffn_w13': 8.0,
     'L2_ffn_w2': 8.0,
     'L2_ffn_sw13': 3.04,
     'L2_ffn_sw2': 2.864,
     'L3_xattn_wk': 5.2,
     'L3_xattn_wv': 3.091,
     'L3_ffn_w1': 4.411,
     'L3_ffn_w3': 4.334,
     'L3_ffn_w2': 4.317}
    for name, (base, spread) in spreads.items():
        noise = np.random.default_rng([zlib.crc32(name.encode()), seed]).standard_normal(out[name].shape)
        drawn = base * np.exp(spread * noise) if base else spread * noise
        out[name] = jnp.asarray(drawn.astype(out[name].dtype))
    for name, factor in factors.items():
        out[name] = (out[name] * factor).astype(out[name].dtype)
    return out
```

```python
from contextlib import ExitStack

import numpy as np

import concourse.bass as bass
from concourse import mybir

F32 = mybir.dt.float32
I32 = mybir.dt.int32
U32 = mybir.dt.uint32
ALU = mybir.AluOpType
ACT = mybir.ActivationFunctionType
AX_X = mybir.AxisListType.X

B, TOK, D = 8, 112, 512
NT = B * TOK
HALF = NT // 2
KD = D // 128
T = 375
KT, TT = 3, 125
NEG = -1e30
LN_EPS = 1e-5

H, HD, KVC, QC, R = 16, 128, 128, 192, 64
QC1 = QC - 128
LOOKBACK = 8
SCALE0 = 1.0 / float(np.sqrt(np.float32(HD + R)))
GH = 4
NG = H // GH
HD1 = D // H
SCALE1 = 1.0 / float(np.sqrt(np.float32(HD1)))
SCALE3 = 1.0 / float(np.sqrt(D))
E = 16
CAP = 256
L3_HIDDEN = int(2 * D * 4 / 3)


class Chip:

    def __init__(self, nc, ctx):
        self.nc = nc
        self.used = []

        def sb(name, shape, dt=F32):
            return ctx.enter_context(nc.sbuf_tensor(name, shape, dt))

        self.x = sb("x", [TOK, B, D])
        self.xn = sb("xn", [TOK, B, D])
        self.xnT = sb("xnT", [128, KD, NT])
        self.ctxT = sb("ctxT", [128, KD, B * T])
        self.ident = sb("ident", [128, 128])
        self.ones = sb("ones", [128, 128])
        self.before = sb("before", [TOK, TOK])
        self.tanh_g = sb("tanh_g", [128, 8])
        self.raw_g = sb("raw_g", [128, 8])
        self.eps = sb("eps", [128, 1])
        self.expert_ids = sb("expert_ids", [TOK, E])
        self.gates = sb("gates", [TOK, E + 2, B])
        self.gate_w = sb("gate_w", [128, KD, E])
        self.bank = [ctx.enter_context(nc.psum_tensor(f"bank{i}", [128, 512], F32)) for i in range(8)]
        self.iota_i = sb("iota_i", [TOK, T], I32)
        self.key_ids = sb("key_ids", [TOK, T])
        self.stats = sb("stats", [TOK, B, 6])
        self.mv = sb("mv", [TOK, B, 2])
        self.sd = sb("sd", [TOK, B])
        self.rstd = sb("rstd", [TOK, B])

    def sems(self, stage, *names):
        own = [self.nc.alloc_semaphore(f"{stage}_{n}") for n in names]
        self.used += own
        return own

    def clear_semaphores(self):
        self.nc.clear_and_free_semaphores(self.used)
        self.used = []
        self.nc.all_engine_barrier()


def setup_stage(nc, s, d):
    with ExitStack() as ctx:
        loaded, made, masked, const_done = s.sems("setup", "loaded", "made", "masked", "const")
        block = ctx.enter_context(nc.Block())

        @block.sync
        def _(sp):
            sp.dma_start(s.x[:, :, :], d["x"].rearrange("b p d -> p b d")).then_inc(loaded, 16)
            sp.dma_start(s.raw_g[:, 0:4], d["g_xattn"].partition_broadcast(128)).then_inc(loaded, 16)
            sp.dma_start(s.raw_g[:, 4:8], d["g_ffn"].partition_broadcast(128)).then_inc(loaded, 16)
            for k in range(KD):
                sp.dma_start(s.ctxT[:, k, :], d["ctxT"][:, k, :]).then_inc(loaded, 16)
            sp.wait_ge(loaded, 16 * (3 + KD))

        @block.scalar
        def _(act):
            act.wait_ge(loaded, 16 * (3 + KD))
            act.activation(s.tanh_g[:, :], s.raw_g[:, :], ACT.Tanh)

        @block.gpsimd
        def _(pool):
            pool.memset(s.ident[:, :], 0.0).then_inc(made, 1)
            pool.memset(s.before[:, :], 1.0).then_inc(made, 1)
            pool.memset(s.ones[:, :], 1.0)
            pool.memset(s.eps[:, :], LN_EPS)
            pool.iota(s.iota_i[:, :], pattern=[[1, T]], base=0, channel_multiplier=0).then_inc(made, 1)
            pool.wait_ge(made, 3)
            pool.affine_select(out=s.ident[:, :], in_=s.ident[:, :], compare_op=ALU.not_equal, fill=1.0,
                               base=0, pattern=[[-1, 128]], channel_multiplier=1)
            pool.affine_select(out=s.before[:, :], in_=s.before[:, :], compare_op=ALU.is_gt, fill=0.0,
                               base=0, pattern=[[1, TOK]], channel_multiplier=-1)
            pool.tensor_copy(s.key_ids[:, :], s.iota_i[:, :]).then_inc(masked, 1)
            pool.wait_ge(masked, 1)
            pool.tensor_copy(s.expert_ids[:, :], s.key_ids[:, 0:E])


def layernorm_stage(nc, s, name):
    with ExitStack() as ctx:
        stats_done, mv_done, sd_done, rstd_done, norm_done, tr_done = s.sems(name, "stats_done", "mv_done", "sd_done", "rstd_done", "norm_done", "tr_done")
        block = ctx.enter_context(nc.Block())

        @block.vector
        def _(dve):
            for b in range(B):
                dve.bn_stats(s.stats[:, b, :], s.x[:, b, :]).then_inc(stats_done, 1)
            for b in range(B):
                dve.wait_ge(stats_done, b + 1)
                dve.bn_aggr(s.mv[:, b, :], s.stats[:, b, :]).then_inc(mv_done, 1)
            dve.wait_ge(sd_done, 1)
            dve.reciprocal(s.rstd[:, :], s.sd[:, :]).then_inc(rstd_done, 1)
            dve.wait_ge(rstd_done, 1)
            for b in range(B):
                dve.tensor_scalar(s.xn[:, b, :], s.x[:, b, :], s.mv[:, b, 0:1], s.rstd[:, b:b + 1],
                                  ALU.subtract, ALU.mult).then_inc(norm_done, 1)

        @block.scalar
        def _(act):
            act.wait_ge(mv_done, B)
            act.activation(s.sd[:, :], s.mv[:, :, 1], ACT.Sqrt, bias=s.eps[0:TOK, :]).then_inc(sd_done, 1)
            for b in range(B):
                act.wait_ge(tr_done, b + 1)
                act.activation(s.xnT[:, :, b * TOK:(b + 1) * TOK],
                               s.bank[b][:, 0:KD * TOK].rearrange("p (k t) -> p k t", k=KD), ACT.Copy)

        @block.tensor
        def _(pe):
            for b in range(B):
                pe.wait_ge(norm_done, b + 1)
                for k in range(KD):
                    mm = pe.transpose(s.bank[b][:, k * TOK:(k + 1) * TOK],
                                      s.xn[:, b, k * 128:(k + 1) * 128], s.ident[0:TOK, 0:TOK])
                mm.then_inc(tr_done, 1)


def router_stage(nc, s, name, gate_dram, top_k, layer, softmax, eps, capacity=None):
    with ExitStack() as ctx:
        def sb(n, shape, dt=F32):
            return ctx.enter_context(nc.sbuf_tensor(f"{name}_{n}", shape, dt))

        (loaded, logits_done, act_done, step, hot_done, rank_done) = s.sems(name, "loaded", "logits_done", "act_done", "step", "hot_done", "rank_done")
        lmax = sb("lmax", [TOK, B])
        shifted = sb("shifted", [TOK, B, E])
        expd = sb("expd", [TOK, B, E])
        denom = sb("denom", [TOK, B, E])
        esum = sb("esum", [TOK, B])
        einv = sb("einv", [TOK, B])
        scores = sb("scores", [TOK, B, E])
        top = sb("top", [TOK, B, 8])
        top_i = sb("top_i", [TOK, B, 8], U32)
        top_f = sb("top_f", [TOK, B, 8])
        wsum = sb("wsum", [TOK, B])
        winv = sb("winv", [TOK, B])
        hot = sb("hot", [TOK, 2, B, E])
        mix = sb("mix", [TOK, B, E])
        keep = sb("keep", [TOK, B, E])
        logits = s.bank[0][0:TOK, 0:B * E].rearrange("p (b e) -> p b e", b=B)
        rank = s.bank[1][0:TOK, 0:B * E].rearrange("p (b e) -> p b e", b=B)
        block = ctx.enter_context(nc.Block())

        @block.sync
        def _(sp):
            sp.dma_start(s.gate_w[:, :, :], gate_dram.rearrange("(k p) e -> p k e", p=128)).then_inc(loaded, 16)
            sp.wait_ge(loaded, 16)

        @block.tensor
        def _(pe):
            pe.wait_ge(loaded, 16)
            for b in range(B):
                for k in range(KD):
                    mm = pe.matmul(logits[:, b, :], s.xnT[:, k, b * TOK:(b + 1) * TOK], s.gate_w[:, k, :],
                                   start=(k == 0), stop=(k == KD - 1))
            mm.then_inc(logits_done, 1)
            if capacity:
                pe.wait_ge(hot_done, 1)
                for b in range(B):
                    for c in range(b + 1):
                        mm = pe.matmul(rank[:, b, :], s.before[:, :] if c == b else s.ones[0:TOK, 0:TOK],
                                       keep[:, c, :], start=(c == 0), stop=(c == b))
                mm.then_inc(rank_done, 1)

        @block.scalar
        def _(act):
            if softmax:
                act.wait_ge(step, 2)
                act.activation(expd[:, :, :], shifted[:, :, :], ACT.Exp).then_inc(act_done, 1)
            else:
                act.wait_ge(logits_done, 1)
                act.activation(expd[:, :, :], logits, ACT.Exp, scale=-1.0).then_inc(act_done, 1)

        @block.vector
        def _(dve):
            chain = [0]

            def then(instruction):
                chain[0] += 1
                instruction.then_inc(step, 1)
                dve.wait_ge(step, chain[0])

            def over(ap):
                return ap.unsqueeze(2).to_broadcast([TOK, B, E])

            dve.wait_ge(logits_done, 1)
            if softmax:
                then(dve.tensor_reduce(lmax[:, :], logits, AX_X, ALU.max))
                then(dve.tensor_tensor(shifted[:, :, :], logits, over(lmax[:, :]), ALU.subtract))
                dve.wait_ge(act_done, 1)
                then(dve.tensor_reduce(esum[:, :], expd[:, :, :], AX_X, ALU.add))
                then(dve.reciprocal(einv[:, :], esum[:, :]))
                then(dve.tensor_tensor(scores[:, :, :], expd[:, :, :], over(einv[:, :]), ALU.mult))
            else:
                dve.wait_ge(act_done, 1)
                then(dve.tensor_scalar(denom[:, :, :], expd[:, :, :], 1.0, None, ALU.add))
                then(dve.reciprocal(scores[:, :, :], denom[:, :, :]))
            for b in range(B):
                then(dve.max(top[:, b, :], scores[:, b, :]))
                then(dve.max_index(top_i[:, b, :], top[:, b, :], scores[:, b, :]))
            then(dve.tensor_copy(top_f[:, :, :], top_i[:, :, :]))
            then(dve.tensor_reduce(wsum[:, :], top[:, :, 0:top_k], AX_X, ALU.add))
            if eps:
                then(dve.tensor_scalar(wsum[:, :], wsum[:, :], eps, None, ALU.add))
            then(dve.reciprocal(winv[:, :], wsum[:, :]))
            then(dve.tensor_scalar(winv[:, :], winv[:, :], s.tanh_g[0:TOK, 4 + layer:5 + layer], None, ALU.mult))
            then(dve.tensor_tensor(top[:, :, 0:top_k], top[:, :, 0:top_k],
                                   winv[:, :].unsqueeze(2).to_broadcast([TOK, B, top_k]), ALU.mult))
            ids = s.expert_ids[:, :].unsqueeze(1).to_broadcast([TOK, B, E])
            for k in range(top_k):
                then(dve.tensor_tensor(hot[:, 0, :, :], ids, over(top_f[:, :, k]), ALU.is_equal))
                if capacity:
                    if k == 0:
                        then(dve.tensor_copy(keep[:, :, :], hot[:, 0, :, :]))
                    else:
                        then(dve.tensor_tensor(keep[:, :, :], keep[:, :, :], hot[:, 0, :, :], ALU.add))
                dst = mix if k == 0 else hot[:, 1, :, :]
                then(dve.tensor_tensor(dst[:, :, :], hot[:, 0, :, :], over(top[:, :, k]), ALU.mult))
                if k:
                    then(dve.tensor_tensor(mix[:, :, :], mix[:, :, :], hot[:, 1, :, :], ALU.add))
            if capacity:
                dve.sem_inc(hot_done, 1)
                dve.wait_ge(rank_done, 1)
                then(dve.tensor_scalar(keep[:, :, :], rank, float(capacity), None, ALU.is_lt))
                then(dve.tensor_tensor(mix[:, :, :], mix[:, :, :], keep[:, :, :], ALU.mult))
            dve.tensor_copy(s.gates[:, 0:E, :].rearrange("p e b -> p b e"), mix[:, :, :])
            dve.tensor_scalar(s.gates[:, E:E + 2, :], s.ones[0:TOK, 0:2 * B].rearrange("p (u b) -> p u b", u=2),
                              s.tanh_g[0:TOK, 4 + layer:5 + layer], None, ALU.mult)


def gated_units_stage(nc, s, name, units, width, func, w_gate, w_up, w_down, layer,
                      biases=None, ternary=None):
    chunks = [(c * 128, min(128, width - c * 128)) for c in range((width + 127) // 128)]
    FC = len(chunks)
    whole = width // 128
    DMAS = 3 + (whole < FC)
    HMULS = 2 * FC
    with ExitStack() as ctx:
        def sb(n, shape, dt=F32):
            return ctx.enter_context(nc.sbuf_tensor(f"{name}_{n}", shape, dt))

        loaded, g_done, u_done, act_done, h_done, y_done, y_added, xn_added, extra, gT_done, gT_copied, b2_done = s.sems(name, "loaded", "g_done", "u_done", "act_done", "h_done", "y_done", "y_added",
            "xn_added", "extra", "gT_done", "gT_copied", "b2_done")
        if ternary:
            wg, wu, wd = ternary[2]
        else:
            wg = [sb(f"wg{i}", [128, KD, width]) for i in range(2)]
            wu = [sb(f"wu{i}", [128, KD, width]) for i in range(2)]
            wd = [sb(f"wd{i}", [128, FC, D]) for i in range(2)]

        def over_units(eng, unit):
            if ternary:
                for u in range(units):
                    unit(u, u)
            else:
                with eng.Fori(0, units // 2) as i:
                    for w in range(2):
                        unit(i * 2 + w, w, i)

        loaded = [loaded, s.sems(name, "loaded1")[0]]
        acted = sb("acted", [128, 2, HALF])
        hT = [sb(f"hT{i}", [128, FC, NT]) for i in range(2)]
        if biases:
            bg = sb("bg", [128, units, FC])
            bu = sb("bu", [128, units, FC])
            bd = sb("bd", [units, D])
            bg_now = sb("bg_now", [128, 2, FC])
            b_ready = s.sems(name, "b_ready")[0]
            gT = sb("gT", [units, B, TOK])
        block = ctx.enter_context(nc.Block())

        @block.sync
        def _(sp):
            if biases:
                sp.dma_start(bg[:, :, :], biases[0]).then_inc(extra, 16)
                sp.dma_start(bu[:, :, :], biases[1]).then_inc(extra, 16)
                sp.dma_start(bd[:, :], biases[2]).then_inc(extra, 16)
            def unit(u, w, i):
                sp.wait_ge(y_done, (u + 1) * B)
                sp.dma_start(wg[w][:, :, :], w_gate[bass.ds(u, 1)].rearrange("o (k p) f -> p (o k) f", p=128))\
                  .then_inc(loaded[w], 16)
                sp.dma_start(wu[w][:, :, :], w_up[bass.ds(u, 1)].rearrange("o (k p) f -> p (o k) f", p=128))\
                  .then_inc(loaded[w], 16)
                sp.dma_start(wd[w][:, 0:whole, :],
                             w_down[bass.ds(u, 1), 0:whole * 128].rearrange("o (c p) f -> p (o c) f", p=128))\
                  .then_inc(loaded[w], 16)
                if whole < FC:
                    sp.dma_start(wd[w][0:width - whole * 128, whole, :],
                                 w_down[bass.ds(u, 1), whole * 128:width].rearrange("o p f -> (o p) f"))\
                      .then_inc(loaded[w], 16)

            if not ternary:
                over_units(sp, unit)

        @block.tensor
        def _(pe):
            pe.sem_inc(y_done, 2 * B)
            if biases:
                for b in range(B):
                    mm = pe.transpose(s.bank[b][0:units, 0:TOK], s.gates[:, :, b], s.ident[0:TOK, 0:TOK])
                mm.then_inc(gT_done, 1)
                pe.wait_ge(extra, 48)
                pe.wait_ge(gT_copied, 1)
                for b in range(B):
                    mm = pe.matmul(s.bank[b][0:TOK, :], gT[:, b, :], bd[:, :], start=True, stop=True)
                mm.then_inc(b2_done, 1)
                pe.wait_ge(xn_added, B + B)
            def unit(u, w, i=None):
                if not ternary:
                    pe.wait_ge(loaded[w], (i + 1) * 16 * DMAS)
                for q in range(HMULS):
                    half, (f0, fn) = q // FC, chunks[q % FC]
                    pe.wait_ge(h_done, u * HMULS + q + 1)
                    for weight, out, done in ((wg, s.bank[2 * (q % 2)], g_done), (wu, s.bank[2 * (q % 2) + 1], u_done)):
                        for k in range(KD):
                            mm = pe.matmul(out[0:fn, 0:HALF], weight[w][:, k, f0:f0 + fn],
                                           s.xnT[:, k, half * HALF:(half + 1) * HALF],
                                           start=(k == 0), stop=(k == KD - 1))
                        mm.then_inc(done, 1)
                for b in range(B):
                    pe.wait_ge(h_done, 2 + u * HMULS + FC * (1 + b // (B // 2)))
                    pe.wait_ge(y_added, u * B + b + 1)
                    for c, (f0, fn) in enumerate(chunks):
                        mm = pe.matmul(s.bank[4 + b % 4][0:TOK, :], hT[w % 2][0:fn, c, b * TOK:(b + 1) * TOK],
                                       wd[w][0:fn, c, :], start=(c == 0), stop=(c == FC - 1))
                    mm.then_inc(y_done, 1)

            over_units(pe, unit)

        @block.scalar
        def _(act):
            if biases:
                act.wait_ge(gT_done, 1)
                for b in range(B):
                    op = act.activation(gT[:, b, :], s.bank[b][0:units, 0:TOK], ACT.Copy)
                op.then_inc(gT_copied, 1)
            if biases:
                act.wait_ge(extra, 48)

            def unit(u, w, i=None):
                if biases:
                    act.copy(bg_now[:, w, :], bg[:, bass.ds(u, 1), :].rearrange("p o c -> p (o c)")).then_inc(b_ready, 1)
                    act.wait_ge(b_ready, u + 1)
                for q in range(HMULS):
                    f0, fn = chunks[q % FC]
                    piece = u * HMULS + q + 1
                    act.wait_ge(g_done, piece)
                    act.wait_ge(h_done, piece)
                    scale = ternary[0][0:fn, 0:1] if ternary else 1.0
                    kind = dict(bias=bg_now[0:fn, w, q % FC:q % FC + 1]) if biases else {}
                    act.activation(acted[0:fn, q % 2, :], s.bank[2 * (q % 2)][0:fn, 0:HALF], func,
                                   scale=scale, **kind).then_inc(act_done, 1)

            over_units(act, unit)

        @block.vector
        def _(dve):
            if biases:
                for b in range(B):
                    dve.scalar_tensor_tensor(out=s.x[:, b, :], in0=s.xn[:, b, :],
                                             scalar=s.tanh_g[0:TOK, 4 + layer:5 + layer], in1=s.x[:, b, :],
                                             op0=ALU.mult, op1=ALU.add).then_inc(xn_added, 1)
                dve.wait_ge(b2_done, 1)
                for b in range(B):
                    dve.wait_ge(xn_added, B + b)
                    dve.tensor_tensor(s.x[:, b, :], s.x[:, b, :], s.bank[b][0:TOK, :], ALU.add).then_inc(xn_added, 1)
                dve.wait_ge(xn_added, 2 * B)
            dve.sem_inc(h_done, 2)
            dve.sem_inc(y_added, 4)
            def unit(u, w, i=None):
                for q in range(HMULS):
                    half, c, (f0, fn) = q // FC, q % FC, chunks[q % FC]
                    dve.wait_ge(u_done, u * HMULS + q + 1)
                    dve.wait_ge(act_done, u * HMULS + q + 1)
                    out = hT[w % 2][0:fn, c, half * HALF:(half + 1) * HALF]
                    up = s.bank[2 * (q % 2) + 1][0:fn, 0:HALF]
                    if biases:
                        dve.scalar_tensor_tensor(out=out, in0=up, scalar=bu[0:fn, bass.ds(u, 1), c],
                                                 in1=acted[0:fn, q % 2, :], op0=ALU.add, op1=ALU.mult).then_inc(h_done, 1)
                    elif ternary:
                        dve.scalar_tensor_tensor(out=out, in0=up, scalar=ternary[1][0:fn, 0:1],
                                                 in1=acted[0:fn, q % 2, :], op0=ALU.mult, op1=ALU.mult).then_inc(h_done, 1)
                    else:
                        dve.tensor_tensor(out, up, acted[0:fn, q % 2, :], ALU.mult).then_inc(h_done, 1)
                for b in range(B):
                    dve.wait_ge(y_done, 2 * B + u * B + b + 1)
                    dve.wait_ge(y_added, u * B + b + 1)
                    dve.scalar_tensor_tensor(out=s.x[:, b, :], in0=s.bank[4 + b % 4][0:TOK, :],
                                             scalar=s.gates[:, bass.ds(u, 1), b], in1=s.x[:, b, :],
                                             op0=ALU.mult, op1=ALU.add).then_inc(y_added, 1)

            over_units(dve, unit)

def latent_project_stage(nc, s, d, a):
    with ExitStack() as ctx:
        def sb(n, shape, dt=F32):
            return ctx.enter_context(nc.sbuf_tensor(f"l0p_{n}", shape, dt))

        (loaded, kv_done, kv_copied, rot_done, rot_mul, rot_added, tr_done, tr_copied, q_done, ids_f) = s.sems("l0p", "loaded", "kv_done", "kv_copied", "rot_done", "rot_mul", "rot_added", "tr_done",
            "tr_copied", "q_done", "ids_f")
        masked = a.masked
        w_kvc = sb("w_kvc", [128, KD, KVC])
        w_kr = sb("w_kr", [KVC, 2, 128])
        w_dq = sb("w_dq", [128, KD, QC])
        part = sb("part", [128, 2, 2, T])
        ids_i = sb("ids_i", [TOK, B], I32)
        ids = sb("ids", [TOK, B])
        low = sb("low", [TOK, 2, T])
        block = ctx.enter_context(nc.Block())

        @block.sync
        def _(sp):
            sp.dma_start(w_kvc[:, :, :], d["l0_w_kvc"].rearrange("(k p) n -> p k n", p=128)).then_inc(loaded, 16)
            sp.dma_start(w_kr[:, :, :], d["l0_w_kr"]).then_inc(loaded, 16)
            sp.dma_start(w_dq[:, :, :], d["l0_w_dq"].rearrange("(k p) n -> p k n", p=128)).then_inc(loaded, 16)
            sp.dma_start(a.cos[:, :], d["cos"]).then_inc(loaded, 16)
            sp.dma_start(a.sin[:, :], d["sin"]).then_inc(loaded, 16)
            sp.dma_start(ids_i[:, :], d["ids"]).then_inc(loaded, 16)

        @block.tensor
        def _(pe):
            pe.wait_ge(loaded, 96)
            for b in range(B + 1):
                if b < B:
                    if b >= 2:
                        pe.wait_ge(kv_copied, b - 1)
                    for k in range(KD):
                        mm = pe.matmul(s.bank[b % 2][:, 0:T], w_kvc[:, k, :], s.ctxT[:, k, b * T:(b + 1) * T],
                                       start=(k == 0), stop=(k == KD - 1))
                    mm.then_inc(kv_done, 1)
                if b >= 1:
                    c = b - 1
                    pe.wait_ge(kv_copied, c + 1)
                    if c >= 2:
                        pe.wait_ge(rot_mul, 2 * (c - 1))
                        pe.wait_ge(tr_copied, c - 1)
                    for v in range(2):
                        mm = pe.matmul(s.bank[2 + 2 * (c % 2) + v][:, 0:T], w_kr[:, v, :],
                                       a.kvcT[:, c * T:(c + 1) * T], start=True, stop=True)
                    mm.then_inc(rot_done, 1)
                    for t in range(KT):
                        mm = pe.transpose(s.bank[6 + c % 2][0:TT, t * KVC:(t + 1) * KVC],
                                          a.kvcT[:, c * T + t * TT:c * T + (t + 1) * TT], s.ident[:, :])
                    mm.then_inc(tr_done, 1)
            for q in range(4):
                m, half = q // 2, q % 2
                rows = 128 if m == 0 else QC1
                if q < 2:
                    pe.wait_ge(kv_copied, B)
                else:
                    pe.wait_ge(rot_mul, 2 * B)
                for k in range(KD):
                    mm = pe.matmul(s.bank[q][0:rows, 0:HALF], w_dq[:, k, m * 128:m * 128 + rows],
                                   s.xnT[:, k, half * HALF:(half + 1) * HALF], start=(k == 0), stop=(k == KD - 1))
                mm.then_inc(q_done, 1)

        @block.scalar
        def _(act):
            for b in range(B + 1):
                if b < B:
                    act.wait_ge(kv_done, b + 1)
                    act.activation(a.kvcT[:, b * T:(b + 1) * T], s.bank[b % 2][:, 0:T], ACT.Copy).then_inc(kv_copied, 1)
                if b >= 1:
                    c = b - 1
                    act.wait_ge(tr_done, c + 1)
                    act.activation(a.kvc[:, c * KT:(c + 1) * KT, :],
                                   s.bank[6 + c % 2][0:TT, 0:KT * KVC].rearrange("p (t n) -> p t n", t=KT),
                                   ACT.Copy).then_inc(tr_copied, 1)
            for q in range(4):
                act.wait_ge(q_done, q + 1)
                dst = (a.qcT0, a.qcT1)[q // 2]
                rows = dst.shape[0]
                act.activation(dst[:, (q % 2) * HALF:(q % 2 + 1) * HALF], s.bank[q][0:rows, 0:HALF], ACT.Copy)

        @block.vector
        def _(dve):
            for b in range(B):
                dve.wait_ge(rot_done, b + 1)
                if b >= 2:
                    dve.wait_ge(rot_added, b - 1)
                for v, table in enumerate((a.cos, a.sin)):
                    dve.tensor_tensor(part[:, b % 2, v, :], s.bank[2 + 2 * (b % 2) + v][:, 0:T], table[:, :],
                                      ALU.mult).then_inc(rot_mul, 1)
                dve.wait_ge(rot_mul, 2 * (b + 1))
                dve.tensor_tensor(a.krT[:, b * T:(b + 1) * T], part[:, b % 2, 0, :], part[:, b % 2, 1, :],
                                  ALU.add).then_inc(rot_added, 1)
            dve.tensor_copy(ids[:, :], ids_i[:, :]).then_inc(ids_f, 1)
            dve.wait_ge(ids_f, 1)
            for b in range(B):
                dve.tensor_scalar(low[:, 0, :], s.key_ids[:, :], ids[:, b:b + 1], -float(LOOKBACK),
                                  ALU.subtract, ALU.is_ge).then_inc(masked, 1)
                dve.tensor_scalar(low[:, 1, :], s.key_ids[:, :], ids[:, b:b + 1], 0.0,
                                  ALU.subtract, ALU.is_le).then_inc(masked, 1)
                dve.wait_ge(masked, 4 * b + 2)
                dve.scalar_tensor_tensor(out=a.mask[:, b, :], in0=low[:, 0, :], scalar=-2.0, in1=low[:, 1, :],
                                         op0=ALU.add, op1=ALU.add).then_inc(masked, 1)
                dve.wait_ge(masked, 4 * b + 3)
                dve.tensor_scalar(a.mask[:, b, :], a.mask[:, b, :], -NEG / SCALE0, None, ALU.mult).then_inc(masked, 1)


def latent_attention_stage(nc, s, d, a):
    N = B * GH
    BUFS = 4
    with ExitStack() as ctx:
        def sb(n, shape, dt=F32):
            return ctx.enter_context(nc.sbuf_tensor(f"l0a_{n}", shape, dt))

        (loaded, w_done, w_copied, qr_done, qr_mul, qr_added, s_done, s_masked, shift, e_done, inv_done, p_done,
         pt_done, pt_copied, z_done, z_copied, y_done, y_added) = s.sems("l0a", "loaded", "w_done", "w_copied", "qr_done", "qr_mul", "qr_added", "s_done", "s_masked",
            "shift", "e_done", "inv_done", "p_done", "pt_done", "pt_copied", "z_done", "z_copied", "y_done", "y_added")
        w_uq = sb("w_uq", [HD, GH, QC])
        w_uk = sb("w_uk", [HD, GH, KVC])
        w_uv = sb("w_uv", [HD, GH, KVC])
        w_o = sb("w_o", [HD, GH, D])
        w_qr0 = sb("w_qr0", [128, 2, GH * R])
        w_qr1 = sb("w_qr1", [QC1, 2, GH * R])
        qk0 = sb("qk0", [128, GH, KVC])
        qk1 = sb("qk1", [QC1, GH, KVC])
        vo = sb("vo", [KVC, GH, D])
        qT = s.xnT
        qrT = sb("qrT", [128, GH // 2, NT])
        shared = sb("shared", [128, 2 * KT * GH * TOK])
        part = shared[:, 0:4 * HALF].rearrange("p (i v n) -> p i v n", i=2, v=2)
        pT = shared[0:TT, :].rearrange("p (i t h n) -> p i t h n", i=2, t=KT, h=GH)
        p = sb("p", [TOK, BUFS, T])
        top = sb("top", [TOK, BUFS])
        spare = sb("spare", [TOK, 1])
        low = sb("low", [TOK, BUFS])
        total = sb("total", [TOK, BUFS])
        inv = sb("inv", [TOK, BUFS])
        zT = sb("zT", [KVC, 2, GH, TOK])
        block = ctx.enter_context(nc.Block())
        W_COPIES = 2 + GH + 2 * GH
        QR = 2 * 2

        @block.sync
        def _(sp):
            with sp.Fori(0, NG) as g:
                sp.wait_ge(qr_done, g * QR + 1)
                one = bass.ds(g, 1)
                sp.dma_start(w_uq[:, :, :], d["l0_w_uqT"][one].rearrange("o h p n -> p (o h) n")).then_inc(loaded, 16)
                sp.dma_start(w_uk[:, :, :], d["l0_w_ukT"][one].rearrange("o h p n -> p (o h) n")).then_inc(loaded, 16)
                sp.dma_start(w_uv[:, :, :], d["l0_w_uvT"][one].rearrange("o h p n -> p (o h) n")).then_inc(loaded, 16)
                sp.dma_start(w_o[:, :, :], d["l0_w_o"][one].rearrange("o h p n -> p (o h) n")).then_inc(loaded, 16)
                sp.dma_start(w_qr0[:, :, :], d["l0_w_qr"][one, :, 0:128].rearrange("o v p n -> p (o v) n")).then_inc(loaded, 16)
                sp.dma_start(w_qr1[:, :, :], d["l0_w_qr"][one, :, 128:QC].rearrange("o v p n -> p (o v) n")).then_inc(loaded, 16)

        @block.tensor
        def _(pe):
            pe.sem_inc(qr_done, 1)

            def scores(g, n):
                b, j = n // GH, n % GH
                if n >= 3:
                    pe.wait_ge(s_masked, 1 + g * N + n - 2)
                out = s.bank[n % 3][0:TOK, 0:T]
                r = 64 * (j % 2)
                pe.matmul(out, qT[:, j, b * TOK:(b + 1) * TOK], a.kvcT[:, b * T:(b + 1) * T], start=True, stop=False)
                pe.matmul(out, qrT[r:r + R, j // 2, b * TOK:(b + 1) * TOK], a.krT[r:r + R, b * T:(b + 1) * T],
                          start=False, stop=True).then_inc(s_done, 1)

            def turn(g, n):
                pe.wait_ge(p_done, g * N + n + 1)
                if n >= 2:
                    pe.wait_ge(pt_copied, 1 + g * N + n - 1)
                for t in range(KT):
                    mm = pe.transpose(s.bank[3 + n % 2][0:TT, t * TOK:(t + 1) * TOK],
                                      p[:, n % BUFS, t * TT:(t + 1) * TT], s.ident[0:TOK, 0:TOK])
                mm.then_inc(pt_done, 1)

            def mix(g, b):
                pe.wait_ge(pt_copied, 1 + g * N + (b + 1) * GH)
                if b:
                    pe.wait_ge(z_copied, 1 + g * B + b)
                for t in range(KT):
                    mm = pe.matmul(s.bank[5][:, 0:GH * TOK], a.kvc[:, b * KT + t, :],
                                   pT[:, b % 2, t, :, :].rearrange("p h n -> p (h n)"),
                                   start=(t == 0), stop=(t == KT - 1))
                mm.then_inc(z_done, 1)

            def project(g, b):
                pe.wait_ge(z_copied, 1 + g * B + b + 1)
                if b >= 2:
                    pe.wait_ge(y_added, 1 + g * B + b - 1)
                for j in range(GH):
                    mm = pe.matmul(s.bank[6 + b % 2][0:TOK, :], zT[:, b % 2, j, :], vo[:, j, :],
                                   start=(j == 0), stop=(j == GH - 1))
                mm.then_inc(y_done, 1)

            with pe.Fori(0, NG) as g:
                pe.wait_ge(loaded, (g + 1) * 96)
                pe.wait_ge(y_added, 1 + g * B)
                for j in range(GH):
                    pe.matmul(s.bank[0][:, j * KVC:(j + 1) * KVC], w_uq[:, j, 0:128], w_uk[:, j, :],
                              start=True, stop=True)
                    mm = pe.matmul(s.bank[1][0:QC1, j * KVC:(j + 1) * KVC], w_uq[:, j, 128:QC], w_uk[:, j, :],
                                   start=True, stop=True)
                mm.then_inc(w_done, 1)
                for j in range(GH):
                    pe.matmul(s.bank[2 + j][:, :], w_uv[:, j, :], w_o[:, j, :], start=True, stop=True).then_inc(w_done, 1)
                for i in range(QR):
                    jj, half = i // 2, i % 2
                    pair = (6, 7) if i % 2 == 0 else (0, 1)
                    if i == 1:
                        pe.wait_ge(w_copied, g * W_COPIES + 2)
                    if i >= 2:
                        pe.wait_ge(qr_mul, g * 2 * QR + 2 * (i - 1))
                    for v in range(2):
                        out = s.bank[pair[v]][:, 0:HALF]
                        cols = slice(jj * 128, jj * 128 + 128)
                        toks = slice(half * HALF, (half + 1) * HALF)
                        pe.matmul(out, w_qr0[:, v, cols], a.qcT0[:, toks], start=True, stop=False)
                        mm = pe.matmul(out, w_qr1[:, v, cols], a.qcT1[:, toks], start=False, stop=True)
                    mm.then_inc(qr_done, 1)
                for i in range(2 * GH):
                    j, half = i // 2, i % 2
                    pe.wait_ge(w_copied, g * W_COPIES + 2 + i % 4 + 1 + (4 if i >= 4 else 0))
                    out = s.bank[2 + i % 4][:, 0:HALF]
                    toks = slice(half * HALF, (half + 1) * HALF)
                    pe.matmul(out, qk0[:, j, :], a.qcT0[:, toks], start=True, stop=False)
                    pe.matmul(out, qk1[:, j, :], a.qcT1[:, toks], start=False, stop=True).then_inc(w_done, 1)
                pe.wait_ge(w_copied, (g + 1) * W_COPIES)
                pe.wait_ge(qr_added, (g + 1) * QR)
                for n in range(N + 5):
                    if n < N:
                        scores(g, n)
                    if 2 <= n < N + 2:
                        turn(g, n - 2)
                    if n >= 3 + GH - 1 and (n - 3) % GH == GH - 1 and (n - 3) // GH < B:
                        mix(g, (n - 3) // GH)
                    if n >= 4 + GH - 1 and (n - 4) % GH == GH - 1 and (n - 4) // GH < B:
                        project(g, (n - 4) // GH)

        @block.scalar
        def _(act):
            act.sem_inc(pt_copied, 1)
            with act.Fori(0, NG) as g:
                act.wait_ge(w_done, g * (1 + 3 * GH) + 1)
                act.activation(qk0[:, :, :], s.bank[0][:, 0:GH * KVC].rearrange("p (h n) -> p h n", h=GH),
                               ACT.Copy).then_inc(w_copied, 1)
                act.activation(qk1[:, :, :], s.bank[1][0:QC1, 0:GH * KVC].rearrange("p (h n) -> p h n", h=GH),
                               ACT.Copy).then_inc(w_copied, 1)
                for j in range(GH):
                    act.wait_ge(w_done, g * (1 + 3 * GH) + 2 + j)
                    act.activation(vo[:, j, :], s.bank[2 + j][:, :], ACT.Copy).then_inc(w_copied, 1)
                for i in range(2 * GH):
                    act.wait_ge(w_done, g * (1 + 3 * GH) + 2 + GH + i)
                    act.activation(qT[:, i // 2, (i % 2) * HALF:(i % 2 + 1) * HALF], s.bank[2 + i % 4][:, 0:HALF],
                                   ACT.Copy).then_inc(w_copied, 1)
                for n in range(N + 3):
                    if n < N:
                        act.wait_ge(shift, g * N + n + 1)
                        act.activation(p[:, n % BUFS, :], p[:, n % BUFS, :], ACT.Exp,
                                       bias=low[:, n % BUFS:n % BUFS + 1], scale=SCALE0,
                                       accum_out=total[:, n % BUFS:n % BUFS + 1]).then_inc(e_done, 1)
                    if 1 <= n < N + 1:
                        m = n - 1
                        act.wait_ge(inv_done, g * N + m + 1)
                        act.activation(p[:, m % BUFS, :], p[:, m % BUFS, :], ACT.Copy,
                                       scale=inv[:, m % BUFS:m % BUFS + 1]).then_inc(p_done, 1)
                    if n >= 2 and n - 2 < N:
                        m = n - 2
                        b, j = m // GH, m % GH
                        act.wait_ge(pt_done, g * N + m + 1)
                        if b >= 2 and j == 0:
                            act.wait_ge(z_done, g * B + b - 1)
                        act.activation(pT[:, b % 2, :, j, :],
                                       s.bank[3 + m % 2][0:TT, 0:KT * TOK].rearrange("p (t n) -> p t n", t=KT),
                                       ACT.Copy).then_inc(pt_copied, 1)

        @block.vector
        def _(dve):
            dve.sem_inc(s_masked, 1)
            dve.sem_inc(z_copied, 1)
            dve.sem_inc(y_added, 1)
            with dve.Fori(0, NG) as g:
                for i in range(QR):
                    jj, half = i // 2, i % 2
                    pair = (6, 7) if i % 2 == 0 else (0, 1)
                    dve.wait_ge(qr_done, 1 + g * QR + i + 1)
                    for v, table in enumerate((a.cos, a.sin)):
                        dve.tensor_tensor(part[:, i % 2, v, :].rearrange("p (b t) -> p b t", t=TOK),
                                          s.bank[pair[v]][:, 0:HALF].rearrange("p (b t) -> p b t", t=TOK),
                                          table[:, 0:TOK].unsqueeze(1).to_broadcast([128, B // 2, TOK]),
                                          ALU.mult).then_inc(qr_mul, 1)
                    dve.wait_ge(qr_mul, g * 2 * QR + 2 * (i + 1))
                    dve.tensor_tensor(qrT[:, jj, half * HALF:(half + 1) * HALF], part[:, i % 2, 0, :],
                                      part[:, i % 2, 1, :], ALU.add).then_inc(qr_added, 1)
                for n in range(N + 6):
                    if n < N:
                        b = n // GH
                        dve.wait_ge(a.masked, 4 * B)
                        dve.wait_ge(s_done, g * N + n + 1)
                        if n == 0:
                            dve.memset(spare[:, :], 0.0)
                        if n >= BUFS:
                            dve.wait_ge(pt_done, g * N + n - BUFS + 1)
                        dve.tensor_tensor_reduce(out=p[:, n % BUFS, :], in0=s.bank[n % 3][0:TOK, 0:T],
                                                 in1=a.mask[:, b, :], scale=1.0, scalar=-3.0e38, op0=ALU.add,
                                                 op1=ALU.max, accum_out=top[:, n % BUFS:n % BUFS + 1]).then_inc(s_masked, 1)
                        dve.wait_ge(s_masked, 1 + g * N + n + 1)
                        dve.tensor_scalar(low[:, n % BUFS:n % BUFS + 1], top[:, n % BUFS:n % BUFS + 1], -SCALE0, None,
                                          ALU.mult).then_inc(shift, 1)
                    if 1 <= n < N + 1:
                        m = (n - 1) % BUFS
                        dve.wait_ge(e_done, g * N + n)
                        dve.reciprocal(inv[:, m:m + 1], total[:, m:m + 1]).then_inc(inv_done, 1)
                    if n >= 3 + GH - 1 and (n - 3) % GH == GH - 1 and (n - 3) // GH < B:
                        b = (n - 3) // GH
                        dve.wait_ge(z_done, g * B + b + 1)
                        if b >= 2:
                            dve.wait_ge(y_done, g * B + b - 1)
                        dve.tensor_copy(zT[:, b % 2, :, :], s.bank[5][:, 0:GH * TOK].rearrange("p (h n) -> p h n", h=GH))\
                           .then_inc(z_copied, 1)
                    if n >= 5 + GH - 1 and (n - 5) % GH == GH - 1 and (n - 5) // GH < B:
                        b = (n - 5) // GH
                        dve.wait_ge(y_done, g * B + b + 1)
                        dve.wait_ge(y_added, 1 + g * B + b)
                        dve.scalar_tensor_tensor(out=s.x[:, b, :], in0=s.bank[6 + b % 2][0:TOK, :],
                                                 scalar=s.tanh_g[0:TOK, 0:1], in1=s.x[:, b, :],
                                                 op0=ALU.mult, op1=ALU.add).then_inc(y_added, 1)


def heads_attention_stage(nc, s, d):
    N = B * GH
    BUFS = 4
    VB = 128
    with ExitStack() as ctx:
        def sb(n, shape, dt=F32):
            return ctx.enter_context(nc.sbuf_tensor(f"l1a_{n}", shape, dt))

        (const, loaded, k_done, k_copied, q_done, q_copied, v_done, v_copied, s_done, max_done, shift, e_done,
         inv_done, pt_done, pt_copied, z_done, z_scaled, zt_done, zt_copied, y_done, y_added) = s.sems("l1a", "const", "loaded", "k_done", "k_copied", "q_done", "q_copied", "v_done", "v_copied",
            "s_done", "max_done", "shift", "e_done", "inv_done", "pt_done", "pt_copied", "z_done", "z_scaled",
            "zt_done", "zt_copied", "y_done", "y_added")
        w_q = sb("w_q", [128, KD, VB])
        w_k = sb("w_k", [128, KD, VB])
        w_v = sb("w_v", [128, KD, VB])
        w_o = sb("w_o", [128, D])
        b_q = sb("b_q", [128, NG])
        b_k = sb("b_k", [128, NG])
        b_now = sb("b_now", [128, 2])
        b_ready = s.sems("l1a", "b_ready")[0]
        b_v = sb("b_v", [TT, D])
        b_o = sb("b_o", [TOK, D])
        kT = sb("kT", [128, B * T])
        v = sb("v", [TT, B * KT, VB])
        qT = sb("qT", [128, NT])
        p = sb("p", [TOK, BUFS, T])
        top = sb("top", [TOK, BUFS])
        low = sb("low", [TOK, BUFS])
        total = sb("total", [TOK, 2, GH])
        inv = sb("inv", [TOK, 2, GH])
        pT = sb("pT", [TT, 2, KT, GH, TOK])
        z = sb("z", [TOK, 2, VB])
        zT = sb("zT", [VB, 2, TOK])
        block = ctx.enter_context(nc.Block())
        VT = B * KT // 4

        @block.sync
        def _(sp):
            sp.dma_start(b_q[:, :], d["l1_b_q"]).then_inc(const, 16)
            sp.dma_start(b_k[:, :], d["l1_b_k"]).then_inc(const, 16)
            sp.dma_start(b_v[:, :], d["l1_b_v"].partition_broadcast(TT)).then_inc(const, 16)
            sp.dma_start(b_o[:, :], d["l1_b_o"].partition_broadcast(TOK)).then_inc(const, 16)
            with sp.Fori(0, NG) as g:
                sp.wait_ge(y_done, g * B + 1)
                one = bass.ds(g, 1)
                for dst, src in ((w_q, "l1_w_qT"), (w_k, "l1_w_kT"), (w_v, "l1_w_vT")):
                    sp.dma_start(dst[:, :, :], d[src][one].rearrange("o p k n -> p (o k) n")).then_inc(loaded, 16)
                sp.dma_start(w_o[:, :], d["l1_w_oT"][one].rearrange("o p n -> p (o n)")).then_inc(loaded, 16)

        @block.tensor
        def _(pe):
            pe.sem_inc(y_done, 1)

            def scores(g, n):
                b, r = n // GH, HD1 * (n % GH)
                if n >= 3:
                    pe.wait_ge(e_done, g * N + n - 2)
                pe.matmul(s.bank[n % 3][0:TOK, 0:T], qT[r:r + HD1, b * TOK:(b + 1) * TOK],
                          kT[r:r + HD1, b * T:(b + 1) * T], start=True, stop=True).then_inc(s_done, 1)

            def turn(g, n):
                pe.wait_ge(e_done, g * N + n + 1)
                if n >= 2:
                    pe.wait_ge(pt_copied, 1 + g * N + n - 1)
                for t in range(KT):
                    mm = pe.transpose(s.bank[3 + n % 2][0:TT, t * TOK:(t + 1) * TOK],
                                      p[:, n % BUFS, t * TT:(t + 1) * TT], s.ident[0:TOK, 0:TOK])
                mm.then_inc(pt_done, 1)

            def mix(g, b):
                pe.wait_ge(pt_copied, 1 + g * N + (b + 1) * GH)
                if b:
                    pe.wait_ge(zt_copied, 1 + g * B + b)
                for j in range(GH):
                    for t in range(KT):
                        mm = pe.matmul(s.bank[5][0:TOK, j * HD1:(j + 1) * HD1], pT[:, b % 2, t, j, :],
                                       v[:, b * KT + t, j * HD1:(j + 1) * HD1], start=(t == 0), stop=(t == KT - 1))
                mm.then_inc(z_done, 1)

            def turn_mix(g, b):
                pe.wait_ge(z_scaled, 1 + g * B + b + 1)
                pe.transpose(s.bank[5][:, 256:256 + TOK], z[:, b % 2, :], s.ident[0:TOK, 0:TOK]).then_inc(zt_done, 1)

            def project(g, b):
                pe.wait_ge(zt_copied, 1 + g * B + b + 1)
                if b >= 2:
                    pe.wait_ge(y_added, 1 + g * B + b - 1)
                pe.matmul(s.bank[6 + b % 2][0:TOK, :], zT[:, b % 2, :], w_o[:, :], start=True, stop=True)\
                  .then_inc(y_done, 1)

            with pe.Fori(0, NG) as g:
                pe.wait_ge(loaded, (g + 1) * 64)
                pe.wait_ge(y_added, 1 + g * B)
                for h in range(2):
                    for k in range(KD):
                        mm = pe.matmul(s.bank[h][:, 0:HALF], w_q[:, k, :], s.xnT[:, k, h * HALF:(h + 1) * HALF],
                                       start=(k == 0), stop=(k == KD - 1))
                    mm.then_inc(q_done, 1)
                for b in range(B):
                    if b >= 2:
                        pe.wait_ge(k_copied, g * B + b - 1)
                    for k in range(KD):
                        mm = pe.matmul(s.bank[2 + b % 2][:, 0:T], w_k[:, k, :], s.ctxT[:, k, b * T:(b + 1) * T],
                                       start=(k == 0), stop=(k == KD - 1))
                    mm.then_inc(k_done, 1)
                for c in range(VT):
                    if c >= 2:
                        pe.wait_ge(v_copied, g * VT + c - 1)
                    for i in range(4):
                        r0 = (c * 4 + i) * TT
                        for k in range(KD):
                            mm = pe.matmul(s.bank[4 + c % 2][0:TT, i * VB:(i + 1) * VB], s.ctxT[:, k, r0:r0 + TT],
                                           w_v[:, k, :], start=(k == 0), stop=(k == KD - 1))
                    mm.then_inc(v_done, 1)
                pe.wait_ge(q_copied, 2 * (g + 1))
                pe.wait_ge(k_copied, B * (g + 1))
                pe.wait_ge(v_copied, VT * (g + 1))
                for n in range(N + 6):
                    if n < N:
                        scores(g, n)
                    if 2 <= n < N + 2:
                        turn(g, n - 2)
                    for lag, step in ((3, mix), (4, turn_mix), (5, project)):
                        if n >= lag + GH - 1 and (n - lag) % GH == GH - 1 and (n - lag) // GH < B:
                            step(g, (n - lag) // GH)

        @block.scalar
        def _(act):
            act.wait_ge(const, 64)
            act.sem_inc(pt_copied, 1)
            act.sem_inc(zt_copied, 1)
            with act.Fori(0, NG) as g:
                act.copy(b_now[:, 0:1], b_q[:, bass.ds(g, 1)]).then_inc(b_ready, 1)
                act.copy(b_now[:, 1:2], b_k[:, bass.ds(g, 1)]).then_inc(b_ready, 1)
                act.wait_ge(b_ready, 2 * (g + 1))
                for h in range(2):
                    act.wait_ge(q_done, 2 * g + h + 1)
                    act.activation(qT[:, h * HALF:(h + 1) * HALF], s.bank[h][:, 0:HALF], ACT.Identity,
                                   bias=b_now[:, 0:1]).then_inc(q_copied, 1)
                for b in range(B):
                    act.wait_ge(k_done, g * B + b + 1)
                    act.activation(kT[:, b * T:(b + 1) * T], s.bank[2 + b % 2][:, 0:T], ACT.Identity,
                                   bias=b_now[:, 1:2]).then_inc(k_copied, 1)
                for n in range(N + 5):
                    if n < N:
                        b, j = n // GH, n % GH
                        act.wait_ge(shift, g * N + n + 1)
                        if n >= BUFS:
                            act.wait_ge(pt_done, g * N + n - BUFS + 1)
                        if j == 0 and b >= 2:
                            act.wait_ge(inv_done, g * B + b - 1)
                        act.activation(p[:, n % BUFS, :], s.bank[n % 3][0:TOK, 0:T], ACT.Exp,
                                       bias=low[:, n % BUFS:n % BUFS + 1], scale=SCALE1,
                                       accum_out=total[:, b % 2, j:j + 1]).then_inc(e_done, 1)
                    if n >= 2 and n - 2 < N:
                        m = n - 2
                        b, j = m // GH, m % GH
                        act.wait_ge(pt_done, g * N + m + 1)
                        if b >= 2 and j == 0:
                            act.wait_ge(z_done, g * B + b - 1)
                        act.activation(pT[:, b % 2, :, j, :],
                                       s.bank[3 + m % 2][0:TT, 0:KT * TOK].rearrange("p (t n) -> p t n", t=KT),
                                       ACT.Copy).then_inc(pt_copied, 1)
                    if n >= 4 + GH - 1 and (n - 4) % GH == GH - 1 and (n - 4) // GH < B:
                        b = (n - 4) // GH
                        act.wait_ge(zt_done, g * B + b + 1)
                        if b >= 2:
                            act.wait_ge(y_done, 1 + g * B + b - 1)
                        act.activation(zT[:, b % 2, :], s.bank[5][:, 256:256 + TOK], ACT.Copy).then_inc(zt_copied, 1)

        @block.vector
        def _(dve):
            dve.wait_ge(const, 64)
            dve.sem_inc(z_scaled, 1)
            dve.sem_inc(y_added, 1)
            for b in range(B):
                op = dve.scalar_tensor_tensor(out=s.x[:, b, :], in0=b_o[:, :], scalar=s.tanh_g[0:TOK, 1:2],
                                              in1=s.x[:, b, :], op0=ALU.mult, op1=ALU.add)
            op.then_inc(const, 1)
            dve.wait_ge(const, 65)
            with dve.Fori(0, NG) as g:
                for c in range(VT):
                    dve.wait_ge(v_done, g * VT + c + 1)
                    dve.tensor_tensor(v[:, c * 4:(c + 1) * 4, :],
                                      s.bank[4 + c % 2][0:TT, :].rearrange("p (i n) -> p i n", i=4),
                                      b_v[:, bass.ds(g * VB, VB)].unsqueeze(1).to_broadcast([TT, 4, VB]),
                                      ALU.add).then_inc(v_copied, 1)
                for n in range(N + 7):
                    if n < N:
                        dve.wait_ge(s_done, g * N + n + 1)
                        if n >= BUFS:
                            dve.wait_ge(e_done, g * N + n - BUFS + 1)
                        dve.tensor_reduce(top[:, n % BUFS:n % BUFS + 1], s.bank[n % 3][0:TOK, 0:T], AX_X, ALU.max)\
                           .then_inc(max_done, 1)
                        dve.wait_ge(max_done, g * N + n + 1)
                        dve.tensor_scalar(low[:, n % BUFS:n % BUFS + 1], top[:, n % BUFS:n % BUFS + 1], -SCALE1, None,
                                          ALU.mult).then_inc(shift, 1)
                    if n >= 3 + GH - 1 and (n - 3) % GH == GH - 1 and (n - 3) // GH < B:
                        b = (n - 3) // GH
                        dve.wait_ge(e_done, g * N + (b + 1) * GH)
                        dve.reciprocal(inv[:, b % 2, :], total[:, b % 2, :]).then_inc(inv_done, 1)
                        dve.wait_ge(inv_done, g * B + b + 1)
                        dve.wait_ge(z_done, g * B + b + 1)
                        if b >= 2:
                            dve.wait_ge(zt_done, g * B + b - 1)
                        dve.tensor_tensor(z[:, b % 2, :].rearrange("p (h n) -> p h n", h=GH),
                                          s.bank[5][0:TOK, 0:VB].rearrange("p (h n) -> p h n", h=GH),
                                          inv[:, b % 2, :].unsqueeze(2).to_broadcast([TOK, GH, HD1]),
                                          ALU.mult).then_inc(z_scaled, 1)
                    if n >= 6 + GH - 1 and (n - 6) % GH == GH - 1 and (n - 6) // GH < B:
                        b = (n - 6) // GH
                        dve.wait_ge(y_done, 1 + g * B + b + 1)
                        dve.wait_ge(y_added, 1 + g * B + b)
                        dve.scalar_tensor_tensor(out=s.x[:, b, :], in0=s.bank[6 + b % 2][0:TOK, :],
                                                 scalar=s.tanh_g[0:TOK, 1:2], in1=s.x[:, b, :],
                                                 op0=ALU.mult, op1=ALU.add).then_inc(y_added, 1)


def recurrence_stage(nc, s, d):
    with ExitStack() as ctx:
        def sb(n, shape, dt=F32):
            return ctx.enter_context(nc.sbuf_tensor(f"l2a_{n}", shape, dt))

        (loaded, step, decay_e, sums_done, state_done, state_copied, spread, y_done, y_added, stats_done, mv_done,
         sd_done, rstd_done, normed, scaled, shifted) = s.sems("l2a", "loaded", "step", "decay_e", "sums_done", "state_done", "state_copied", "spread", "y_done",
            "y_added", "stats_done", "mv_done", "sd_done", "rstd_done", "normed", "scaled", "shifted")
        decay = sb("decay", [128, 1])
        decay_exp = sb("decay_exp", [128, 1])
        keep = sb("keep", [128, 1])
        keeps = sb("keeps", [128, T])
        ones = sb("ones", [128, T])
        coef = sb("coef", [128, T])
        coef_sum = sb("coef_sum", [128, 1])
        weighted = sb("weighted", [128, 2, T])
        sums = sb("sums", [128, KD, B])
        w_in = sb("w_in", [128, KD, D])
        w_out = sb("w_out", [128, KD, D])
        b_in = sb("b_in", [128, KD])
        b_in_sum = sb("b_in_sum", [128, KD])
        b_out = sb("b_out", [TOK, D])
        gamma = sb("gamma", [TOK, D])
        beta = sb("beta", [TOK, D])
        state = sb("state", [128, KD, B])
        wide = sb("wide", [128, B, KD, TOK])
        block = ctx.enter_context(nc.Block())

        @block.sync
        def _(sp):
            sp.dma_start(decay[:, :], d["l2_decay"].partition_broadcast(128)).then_inc(loaded, 16)
            sp.dma_start(w_in[:, :, :], d["l2_w_inT"].rearrange("(k p) n -> p k n", p=128)).then_inc(loaded, 16)
            sp.dma_start(w_out[:, :, :], d["l2_w_outT"].rearrange("(k p) n -> p k n", p=128)).then_inc(loaded, 16)
            sp.dma_start(b_in[:, :], d["l2_b_in"]).then_inc(loaded, 16)
            sp.dma_start(b_out[:, :], d["l2_b_out"].partition_broadcast(TOK)).then_inc(loaded, 16)
            sp.dma_start(gamma[:, :], d["l2_gamma"].partition_broadcast(TOK)).then_inc(loaded, 16)
            sp.dma_start(beta[:, :], d["l2_beta"].partition_broadcast(TOK)).then_inc(loaded, 16)

        LOADED = 7 * 16

        @block.scalar
        def _(act):
            act.wait_ge(loaded, LOADED)
            act.activation(decay_exp[:, :], decay[:, :], ACT.Exp, scale=-1.0).then_inc(decay_e, 1)
            act.wait_ge(mv_done, B)
            act.activation(s.sd[:, :], s.mv[:, :, 1], ACT.Sqrt, bias=s.eps[0:TOK, :]).then_inc(sd_done, 1)

        @block.tensor
        def _(pe):
            pe.wait_ge(loaded, LOADED)
            pe.wait_ge(sums_done, KD * B)
            for m in range(KD):
                for k in range(KD):
                    mm = pe.matmul(s.bank[0][:, m * B:(m + 1) * B], w_in[:, k, m * 128:(m + 1) * 128], sums[:, k, :],
                                   start=(k == 0), stop=(k == KD - 1))
            mm.then_inc(state_done, 1)
            for b in range(B):
                pe.wait_ge(spread, b + 1)
                if b >= 4:
                    pe.wait_ge(y_added, 2 * (b - 3))
                for k in range(KD):
                    mm = pe.matmul(s.bank[1 + b % 4][0:TOK, :], wide[:, b, k, :], w_out[:, k, :],
                                   start=(k == 0), stop=(k == KD - 1))
                mm.then_inc(y_done, 1)

        @block.vector
        def _(dve):
            chain = [0]

            def then(instruction):
                chain[0] += 1
                instruction.then_inc(step, 1)
                dve.wait_ge(step, chain[0])

            dve.wait_ge(loaded, LOADED)
            then(dve.memset(ones[:, :], 1.0))
            dve.wait_ge(decay_e, 1)
            then(dve.tensor_scalar(keep[:, :], decay_exp[:, :], 1.0, None, ALU.add))
            then(dve.reciprocal(keep[:, :], keep[:, :]))
            then(dve.tensor_scalar(keeps[:, :], ones[:, :], keep[:, :], None, ALU.mult))
            then(dve.tensor_tensor_scan(coef[:, ::-1], keeps[:, :], ones[:, :], 0.0, ALU.mult, ALU.add))
            then(dve.tensor_reduce(coef_sum[:, :], coef[:, :], AX_X, ALU.add))
            then(dve.tensor_scalar(b_in_sum[:, :], b_in[:, :], coef_sum[:, :], None, ALU.mult))
            for i in range(KD * B):
                k, b = i // B, i % B
                if i >= 2:
                    dve.wait_ge(sums_done, i - 1)
                dve.tensor_tensor_reduce(out=weighted[:, i % 2, :], in0=s.ctxT[:, k, b * T:(b + 1) * T],
                                         in1=coef[:, :], scale=1.0, scalar=0.0, op0=ALU.mult, op1=ALU.add,
                                         accum_out=sums[:, k, b:b + 1]).then_inc(sums_done, 1)
            dve.wait_ge(state_done, 1)
            for m in range(KD):
                dve.tensor_scalar(state[:, m, :], s.bank[0][:, m * B:(m + 1) * B], b_in_sum[:, m:m + 1], 1.0 / T,
                                  ALU.add, ALU.mult).then_inc(state_copied, 1)
            dve.wait_ge(state_copied, KD)
            for b in range(B):
                dve.tensor_copy(wide[:, b, :, :], state[:, :, b:b + 1].to_broadcast([128, KD, TOK])).then_inc(spread, 1)
            for b in range(B):
                dve.wait_ge(y_done, b + 1)
                dve.tensor_tensor(s.xn[:, b, :], s.xn[:, b, :], s.bank[1 + b % 4][0:TOK, :], ALU.add).then_inc(y_added, 1)
                dve.wait_ge(y_added, 2 * b + 1)
                dve.tensor_tensor(s.xn[:, b, :], s.xn[:, b, :], b_out[:, :], ALU.add).then_inc(y_added, 1)
                dve.wait_ge(y_added, 2 * b + 2)
                dve.bn_stats(s.stats[:, b, :], s.xn[:, b, :]).then_inc(stats_done, 1)
            for b in range(B):
                dve.wait_ge(stats_done, b + 1)
                dve.bn_aggr(s.mv[:, b, :], s.stats[:, b, :]).then_inc(mv_done, 1)
            dve.wait_ge(sd_done, 1)
            dve.reciprocal(s.rstd[:, :], s.sd[:, :]).then_inc(rstd_done, 1)
            dve.wait_ge(rstd_done, 1)
            for b in range(B):
                dve.tensor_scalar(s.xn[:, b, :], s.xn[:, b, :], s.mv[:, b, 0:1], s.rstd[:, b:b + 1],
                                  ALU.subtract, ALU.mult).then_inc(normed, 1)
            for b in range(B):
                dve.wait_ge(normed, b + 1)
                dve.tensor_tensor(s.xn[:, b, :], s.xn[:, b, :], gamma[:, :], ALU.mult).then_inc(scaled, 1)
            for b in range(B):
                dve.wait_ge(scaled, b + 1)
                dve.tensor_tensor(s.xn[:, b, :], s.xn[:, b, :], beta[:, :], ALU.add).then_inc(shifted, 1)
            for b in range(B):
                dve.wait_ge(shifted, b + 1)
                dve.scalar_tensor_tensor(out=s.x[:, b, :], in0=s.xn[:, b, :], scalar=s.tanh_g[0:TOK, 2:3],
                                         in1=s.x[:, b, :], op0=ALU.mult, op1=ALU.add)


def cache_attention_stage(nc, s, d):
    with ExitStack() as ctx:
        def sb(n, shape, dt=F32):
            return ctx.enter_context(nc.sbuf_tensor(f"l3a_{n}", shape, dt))

        (loaded, v_loaded0, v_loaded1, qk_done, qk_copied, vn_done, vn_copied, s_done, max_done, shift, e_done,
         inv_done, pt_done, pt_copied, z_done, z_scaled, zt_done, zt_copied, y_done, y_added) = s.sems("l3a", "loaded", "v_loaded0", "v_loaded1", "qk_done", "qk_copied", "vn_done", "vn_copied",
            "s_done", "max_done", "shift", "e_done", "inv_done", "pt_done", "pt_copied", "z_done", "z_scaled",
            "zt_done", "zt_copied", "y_done", "y_added")
        ALL = T + TOK
        w = [sb(f"w{i}", [128, KD, D]) for i in range(4)]
        w_q, w_k, w_v, w_o = w
        qkT = [sb("qT", [128, KD, NT]), sb("kT", [128, KD, NT])]
        vn = sb("vn", [TOK, B, D])
        vc = sb("vc", [TT, 2, KT, D])
        p = sb("p", [TOK, 2, ALL])
        top = sb("top", [TOK, 2])
        low = sb("low", [TOK, 2])
        total = sb("total", [TOK, 2])
        inv = sb("inv", [TOK, 2])
        pT = sb("pT", [TT, 2, KT + 1, TOK])
        z = sb("z", [TOK, 2, D])
        zT = sb("zT", [128, 2, KD, TOK])
        v_loaded = (v_loaded0, v_loaded1)
        QK = 2 * KD * 2
        block = ctx.enter_context(nc.Block())

        @block.sync
        def _(sp):
            for dst, src in zip(w, ("l3_w_qT", "l3_w_kT", "l3_w_vT", "l3_w_oT")):
                sp.dma_start(dst[:, :, :], d[src].rearrange("(k p) n -> p k n", p=128)).then_inc(loaded, 16)
            for b in range(B):
                if b >= 2:
                    sp.wait_ge(z_done, b - 1)
                sp.dma_start(vc[:, b % 2, :, :], d["ctx"][b].rearrange("(t p) n -> p t n", p=TT)).then_inc(v_loaded[b % 2], 16)

        @block.tensor
        def _(pe):
            pe.wait_ge(loaded, 64)
            for i in range(QK):
                m, h = (i // 2) % KD, i % 2
                if i >= 4:
                    pe.wait_ge(qk_copied, i - 3)
                for k in range(KD):
                    mm = pe.matmul(s.bank[i % 4][:, 0:HALF], w[i // (2 * KD)][:, k, m * 128:(m + 1) * 128],
                                   s.xnT[:, k, h * HALF:(h + 1) * HALF], start=(k == 0), stop=(k == KD - 1))
                mm.then_inc(qk_done, 1)
            for b in range(B):
                if b >= 4:
                    pe.wait_ge(vn_copied, b - 3)
                for k in range(KD):
                    mm = pe.matmul(s.bank[4 + b % 4][0:TOK, :], s.xnT[:, k, b * TOK:(b + 1) * TOK], w_v[:, k, :],
                                   start=(k == 0), stop=(k == KD - 1))
                mm.then_inc(vn_done, 1)

            def scores(b):
                if b >= 2:
                    pe.wait_ge(e_done, b - 1)
                toks = slice(b * TOK, (b + 1) * TOK)
                for k in range(KD):
                    pe.matmul(s.bank[b % 2][0:TOK, 0:T], qkT[0][:, k, toks], s.ctxT[:, k, b * T:(b + 1) * T],
                              start=(k == 0), stop=(k == KD - 1))
                for k in range(KD):
                    mm = pe.matmul(s.bank[b % 2][0:TOK, T:ALL], qkT[0][:, k, toks], qkT[1][:, k, toks],
                                   start=(k == 0), stop=(k == KD - 1))
                mm.then_inc(s_done, 1)

            def turn(b):
                pe.wait_ge(e_done, b + 1)
                if b >= 2:
                    pe.wait_ge(pt_copied, 2 * (b - 1))
                for t in range(KT + 1):
                    rows = TT if t < KT else TOK
                    mm = pe.transpose(s.bank[2 + b % 2][0:rows, t * TOK:(t + 1) * TOK],
                                      p[:, b % 2, t * TT:t * TT + rows], s.ident[0:TOK, 0:TOK])
                mm.then_inc(pt_done, 1)

            def mix(b):
                pe.wait_ge(pt_copied, 2 * (b + 1))
                pe.wait_ge(v_loaded[b % 2], 16 * (b // 2 + 1))
                if b >= 2:
                    pe.wait_ge(z_scaled, b - 1)
                for t in range(KT):
                    pe.matmul(s.bank[4 + b % 2][0:TOK, :], pT[:, b % 2, t, :], vc[:, b % 2, t, :],
                              start=(t == 0), stop=False)
                pe.matmul(s.bank[4 + b % 2][0:TOK, :], pT[0:TOK, b % 2, KT, :], vn[:, b, :],
                          start=False, stop=True).then_inc(z_done, 1)

            def turn_mix(b):
                pe.wait_ge(z_scaled, b + 1)
                if b:
                    pe.wait_ge(zt_copied, b)
                for k in range(KD):
                    mm = pe.transpose(s.bank[6][:, k * TOK:(k + 1) * TOK], z[:, b % 2, k * 128:(k + 1) * 128],
                                      s.ident[0:TOK, 0:TOK])
                mm.then_inc(zt_done, 1)

            def project(b):
                pe.wait_ge(zt_copied, b + 1)
                if b:
                    pe.wait_ge(y_added, b)
                for k in range(KD):
                    mm = pe.matmul(s.bank[7][0:TOK, :], zT[:, b % 2, k, :], w_o[:, k, :],
                                   start=(k == 0), stop=(k == KD - 1))
                mm.then_inc(y_done, 1)

            pe.wait_ge(qk_copied, QK)
            pe.wait_ge(vn_copied, B)
            for n in range(B + 4):
                for lag, step in enumerate((scores, turn, mix, turn_mix, project)):
                    if 0 <= n - lag < B:
                        step(n - lag)

        @block.scalar
        def _(act):
            for i in range(QK):
                act.wait_ge(qk_done, i + 1)
                m, h = (i // 2) % KD, i % 2
                act.activation(qkT[i // (2 * KD)][:, m, h * HALF:(h + 1) * HALF], s.bank[i % 4][:, 0:HALF],
                               ACT.Copy).then_inc(qk_copied, 1)
            for n in range(B + 3):
                if n < B:
                    act.wait_ge(shift, n + 1)
                    if n >= 2:
                        act.wait_ge(pt_done, n - 1)
                        act.wait_ge(inv_done, n - 1)
                    act.activation(p[:, n % 2, :], s.bank[n % 2][0:TOK, 0:ALL], ACT.Exp, bias=low[:, n % 2:n % 2 + 1],
                                   scale=SCALE3, accum_out=total[:, n % 2:n % 2 + 1]).then_inc(e_done, 1)
                if 0 <= n - 1 < B:
                    b = n - 1
                    act.wait_ge(pt_done, b + 1)
                    if b >= 2:
                        act.wait_ge(z_done, b - 1)
                    act.activation(pT[:, b % 2, 0:KT, :],
                                   s.bank[2 + b % 2][0:TT, 0:KT * TOK].rearrange("p (t n) -> p t n", t=KT),
                                   ACT.Copy).then_inc(pt_copied, 1)
                    act.activation(pT[0:TOK, b % 2, KT, :], s.bank[2 + b % 2][0:TOK, KT * TOK:(KT + 1) * TOK],
                                   ACT.Copy).then_inc(pt_copied, 1)
                if 0 <= n - 3 < B:
                    b = n - 3
                    act.wait_ge(zt_done, b + 1)
                    if b >= 2:
                        act.wait_ge(y_done, b - 1)
                    act.activation(zT[:, b % 2, :, :], s.bank[6][:, 0:KD * TOK].rearrange("p (k n) -> p k n", k=KD),
                                   ACT.Copy).then_inc(zt_copied, 1)

        @block.vector
        def _(dve):
            for b in range(B):
                dve.wait_ge(vn_done, b + 1)
                dve.tensor_copy(vn[:, b, :], s.bank[4 + b % 4][0:TOK, :]).then_inc(vn_copied, 1)
            for n in range(B + 5):
                if n < B:
                    m = slice(n % 2, n % 2 + 1)
                    dve.wait_ge(s_done, n + 1)
                    if n >= 2:
                        dve.wait_ge(e_done, n - 1)
                    dve.tensor_reduce(top[:, m], s.bank[n % 2][0:TOK, 0:ALL], AX_X, ALU.max).then_inc(max_done, 1)
                    dve.wait_ge(max_done, n + 1)
                    dve.tensor_scalar(low[:, m], top[:, m], -SCALE3, None, ALU.mult).then_inc(shift, 1)
                if 0 <= n - 2 < B:
                    b = n - 2
                    dve.wait_ge(e_done, b + 1)
                    dve.reciprocal(inv[:, b % 2:b % 2 + 1], total[:, b % 2:b % 2 + 1]).then_inc(inv_done, 1)
                    dve.wait_ge(inv_done, b + 1)
                    dve.wait_ge(z_done, b + 1)
                    if b >= 2:
                        dve.wait_ge(zt_done, b - 1)
                    dve.tensor_scalar(z[:, b % 2, :], s.bank[4 + b % 2][0:TOK, :], inv[:, b % 2:b % 2 + 1], None,
                                      ALU.mult).then_inc(z_scaled, 1)
                if 0 <= n - 4 < B:
                    b = n - 4
                    dve.wait_ge(y_done, b + 1)
                    dve.scalar_tensor_tensor(out=s.x[:, b, :], in0=s.bank[7][0:TOK, :], scalar=s.tanh_g[0:TOK, 3:4],
                                             in1=s.x[:, b, :], op0=ALU.mult, op1=ALU.add).then_inc(y_added, 1)


def ternary_stage(nc, s, d, t):
    units, width = 4, 352
    whole, rest = width // 128, width % 128
    matrices = (t.wg, t.wu, t.wd)
    count = float(L3_HIDDEN * D)
    with ExitStack() as ctx:
        def sb(n, shape, dt=F32):
            return ctx.enter_context(nc.sbuf_tensor(f"l3t_{n}", shape, dt))

        zeroed, loaded, sized, summed, scaled, sum_done, low_done, turned = s.sems("l3t", "zeroed", "loaded", "sized", "summed", "scaled", "sum_done", "low_done", "turned")
        size = sb("size", [128, 2, (whole + 1) * D])
        part = sb("part", [128, 3, units])
        total = sb("total", [128, 3])
        below = sb("below", [128, 2, (whole + 1) * D])
        block = ctx.enter_context(nc.Block())

        @block.gpsimd
        def _(pool):
            for u in range(units):
                op = pool.memset(t.wd[u][rest:128, whole, :], 0.0)
            op.then_inc(zeroed, 1)

        @block.sync
        def _(sp):
            for u in range(units):
                sp.dma_start(t.wg[u][:, :, :], d["l3_w_1T"][u].rearrange("(k p) f -> p k f", p=128)).then_inc(loaded, 16)
            for u in range(units):
                sp.dma_start(t.wu[u][:, :, :], d["l3_w_3T"][u].rearrange("(k p) f -> p k f", p=128)).then_inc(loaded, 16)
            for u in range(units):
                sp.dma_start(t.wd[u][:, 0:whole, :],
                             d["l3_w_2T"][u, 0:whole * 128].rearrange("(c p) f -> p c f", p=128)).then_inc(loaded, 16)
                sp.dma_start(t.wd[u][0:rest, whole, :], d["l3_w_2T"][u, whole * 128:width]).then_inc(loaded, 16)

        @block.scalar
        def _(act):
            act.wait_ge(loaded, 16 * units * 4)
            act.wait_ge(zeroed, 1)
            for i in range(3 * units):
                m, u = i // units, i % units
                w = matrices[m][u]
                n = w.shape[1] * w.shape[2]
                if i >= 2:
                    act.wait_ge(sized, i - 1)
                act.activation(size[:, i % 2, 0:n], w[:, :, :].rearrange("p a b -> p (a b)"), ACT.Abs,
                               accum_out=part[:, m, u:u + 1]).then_inc(sized, 1)

        @block.tensor
        def _(pe):
            pe.wait_ge(summed, 1)
            pe.matmul(s.bank[0][:, 0:3], s.ones[:, :], total[:, :], start=True, stop=True).then_inc(sum_done, 1)

        @block.vector
        def _(dve):
            dve.wait_ge(sized, 3 * units)
            dve.tensor_reduce(total[:, :], part[:, :, :], AX_X, ALU.add).then_inc(summed, 1)
            dve.wait_ge(sum_done, 1)
            dve.tensor_scalar(t.scale[:, :], s.bank[0][:, 0:3], 1.0 / count, None, ALU.mult).then_inc(scaled, 1)
            dve.wait_ge(scaled, 1)
            for i, sign in enumerate((0.5, -0.5)):
                dve.tensor_scalar(t.half[:, 3 * i:3 * i + 3], t.scale[:, :], sign, None, ALU.mult).then_inc(scaled, 1)
            dve.wait_ge(scaled, 3)
            dve.tensor_scalar(s.gates[:, 0:units, :], s.ones[0:TOK, 0:units * B].rearrange("p (u b) -> p u b", u=units),
                              t.scale[0:TOK, 2:3], s.tanh_g[0:TOK, 7:8], ALU.mult, ALU.mult)
            for i in range(3 * units):
                m, u = i // units, i % units
                w = matrices[m][u][:, :, :].rearrange("p a b -> p (a b)")
                n = w.shape[1]
                if i >= 2:
                    dve.wait_ge(turned, i - 1)
                dve.tensor_scalar(below[:, i % 2, 0:n], w, t.half[:, 3 + m:4 + m], None, ALU.is_lt).then_inc(low_done, 1)
                dve.wait_ge(low_done, i + 1)
                dve.scalar_tensor_tensor(out=w, in0=w, scalar=t.half[:, m:m + 1], in1=below[:, i % 2, 0:n],
                                         op0=ALU.is_gt, op1=ALU.subtract).then_inc(turned, 1)


def store_stage(nc, s, out):
    with ExitStack() as ctx:
        (stored,) = s.sems("store", "stored")
        block = ctx.enter_context(nc.Block())

        @block.sync
        def _(sp):
            sp.dma_start(out.rearrange("b p d -> p b d"), s.x[:, :, :]).then_inc(stored, 16)
            sp.wait_ge(stored, 16)


class Latent:

    def __init__(self, nc, ctx, s):
        def sb(name, shape):
            return ctx.enter_context(nc.sbuf_tensor(f"l0_{name}", shape, F32))

        self.kvcT = sb("kvcT", [KVC, B * T])
        self.kvc = sb("kvc", [TT, B * KT, KVC])
        self.krT = sb("krT", [128, B * T])
        self.qcT0 = sb("qcT0", [128, NT])
        self.qcT1 = sb("qcT1", [QC1, NT])
        self.mask = s.xn[:, :, :].rearrange("p b d -> p (b d)")[:, 0:B * T].rearrange("p (b t) -> p b t", b=B)
        self.masked = s.sems("l0", "masked")[0]
        self.cos = sb("cos", [128, T])
        self.sin = sb("sin", [128, T])


class Ternary:

    def __init__(self, nc, ctx):
        def sb(name, shape):
            return ctx.enter_context(nc.sbuf_tensor(f"l3_{name}", shape, F32))

        self.wg = [sb(f"wg{u}", [128, KD, 352]) for u in range(4)]
        self.wu = [sb(f"wu{u}", [128, KD, 352]) for u in range(4)]
        self.wd = [sb(f"wd{u}", [128, 3, D]) for u in range(4)]
        self.scale = sb("scale", [128, 3])
        self.half = sb("half", [128, 6])


def build(nc, d, out, parts=range(8)):
    with ExitStack() as ctx:
        s = Chip(nc, ctx)
        setup_stage(nc, s, d)
        if 0 in parts:
            layernorm_stage(nc, s, "ln0")
            with ExitStack() as own:
                a = Latent(nc, own, s)
                latent_project_stage(nc, s, d, a)
                latent_attention_stage(nc, s, d, a)
        if 1 in parts:
            layernorm_stage(nc, s, "ln1")
            router_stage(nc, s, "r0", d["l0_router"], 2, 0, softmax=False, eps=0.0)
            gated_units_stage(nc, s, "f0", E + 2, 256, ACT.Gelu, d["l0_wg"], d["l0_wu"], d["l0_wd"], 0,
                              biases=(d["l0_bg"], d["l0_bu"], d["l0_bd"]))
        if 2 in parts:
            s.clear_semaphores()
            layernorm_stage(nc, s, "ln2")
            heads_attention_stage(nc, s, d)
        if 3 in parts:
            layernorm_stage(nc, s, "ln3")
            router_stage(nc, s, "r1", d["l1_router"], 4, 1, softmax=True, eps=1e-20, capacity=CAP)
            gated_units_stage(nc, s, "f1", E + 2, 352, ACT.Silu, d["l1_wg"], d["l1_wu"], d["l1_wd"], 1)
        if 4 in parts:
            s.clear_semaphores()
            layernorm_stage(nc, s, "ln4")
            recurrence_stage(nc, s, d)
        if 5 in parts:
            layernorm_stage(nc, s, "ln5")
            router_stage(nc, s, "r2", d["l2_router"], 6, 2, softmax=True, eps=1e-20)
            gated_units_stage(nc, s, "f2", E + 2, 352, ACT.Silu, d["l2_wg"], d["l2_wu"], d["l2_wd"], 2)
        if 6 in parts:
            s.clear_semaphores()
            layernorm_stage(nc, s, "ln6")
            cache_attention_stage(nc, s, d)
        if 7 in parts:
            layernorm_stage(nc, s, "ln7")
            with ExitStack() as own:
                t = Ternary(nc, own)
                ternary_stage(nc, s, d, t)
                gated_units_stage(nc, s, "f3", 4, 352, ACT.Silu, None, None, None, 3,
                                  ternary=(t.scale[:, 0:1], t.scale[:, 1:2], (t.wg, t.wu, t.wd)))
        store_stage(nc, s, out)


def halves_swapped(w, width):
    n = w.shape[-1] // width
    return np.ascontiguousarray(w.reshape(w.shape[0], n, 2, width // 2)[:, :, ::-1].reshape(w.shape))


def lay_out(i):
    f = {k: np.asarray(v) for k, v in i.items()}
    c = np.ascontiguousarray
    d = {"x": f["x"], "g_xattn": f["g_xattn"], "g_ffn": f["g_ffn"], "ids": c(f["itok_BxS_0_1023"].T)}
    d["ctx"] = f["ctx_2048"]
    d["ctxT"] = c(f["ctx_2048"].reshape(B * T, KD, 128).transpose(2, 1, 0))
    half = R // 2
    freq = (np.float32(1.0) / np.power(np.float32(10000.0), np.arange(half, dtype=np.float32) / np.float32(half)))
    ang = (np.arange(T, dtype=np.float32)[:, None] * freq.astype(np.float32)).astype(np.float32)
    d["cos"] = c(np.tile(np.cos(ang).T, (4, 1)).astype(np.float32))
    sin = np.sin(ang).T.astype(np.float32)
    d["sin"] = c(np.concatenate([-sin, sin, -sin, sin], axis=0))
    d["l0_w_kvc"] = f["L0_xattn_W_kvc"]
    kr = f["L0_xattn_W_kr"]
    d["l0_w_kr"] = c(np.stack([np.tile(kr, (1, 2)), np.tile(halves_swapped(kr, R), (1, 2))], axis=1))
    d["l0_w_dq"] = f["L0_xattn_W_dq"]
    d["l0_w_uqT"] = c(f["L0_xattn_W_uq"].T.reshape(NG, GH, HD, QC))
    d["l0_w_ukT"] = c(f["L0_xattn_W_uk"].T.reshape(NG, GH, HD, KVC))
    d["l0_w_uvT"] = c(f["L0_xattn_W_uv"].T.reshape(NG, GH, HD, KVC))
    d["l0_w_o"] = c(f["L0_xattn_W_o"].reshape(NG, GH, HD, D))
    qr = f["L0_xattn_W_qr"]
    both = np.stack([qr, halves_swapped(qr, R)])
    d["l0_w_qr"] = c(both.reshape(2, QC, NG, GH * R).transpose(2, 0, 1, 3))
    d["l0_router"] = f["L0_ffn_wa"]
    for name, routed, shared in (("wg", "rg", "sg"), ("wu", "rw1", "sw1"), ("wd", "rw2", "sw2")):
        d["l0_" + name] = c(np.concatenate([f["L0_ffn_" + routed], f["L0_ffn_" + shared]]))
    for name, routed, shared in (("bg", "rgb", "sgb"), ("bu", "rb1", "sb1")):
        d["l0_" + name] = c(np.concatenate([f["L0_ffn_" + routed], f["L0_ffn_" + shared]])
                            .reshape(E + 2, 2, 128).transpose(2, 0, 1))
    d["l0_bd"] = c(np.concatenate([f["L0_ffn_rb2"], f["L0_ffn_sb2"]]))
    for n in "qkv":
        w = f["L1_xattn_W" + n].T
        d[f"l1_w_{n}T"] = c(w.reshape(KD, 128, NG, 128).transpose(2, 1, 0, 3))
        d[f"l1_b_{n}"] = f["L1_xattn_b" + n] if n == "v" else c(f["L1_xattn_b" + n].reshape(NG, 128).T)
    d["l1_w_oT"] = c(f["L1_xattn_Wo"].T.reshape(NG, 128, D))
    d["l1_b_o"] = f["L1_xattn_bo"]
    d["l1_router"] = c(f["L1_ffn_gate_w"].T)
    for name, routed, shared in (("wg", "w_gate", "sw_gate"), ("wu", "w_up", "sw_up")):
        d["l1_" + name] = c(np.concatenate([f["L1_ffn_" + routed],
                                            f["L1_ffn_" + shared].reshape(D, 2, 352).transpose(1, 0, 2)]))
    d["l1_wd"] = c(np.concatenate([f["L1_ffn_w_down"], f["L1_ffn_sw_down"].reshape(2, 352, D)]))
    d["l2_router"] = c(f["L2_ffn_gate_w"].T)
    w13 = f["L2_ffn_w13"].reshape(E, 2, 352, D).transpose(1, 0, 3, 2)
    s13 = f["L2_ffn_sw13"].reshape(2, 2, 352, D).transpose(0, 1, 3, 2)
    d["l2_wg"], d["l2_wu"] = c(np.concatenate([w13[0], s13[0]])), c(np.concatenate([w13[1], s13[1]]))
    d["l2_wd"] = c(np.concatenate([f["L2_ffn_w2"].transpose(0, 2, 1), f["L2_ffn_sw2"].T.reshape(2, 352, D)]))
    d["l2_decay"] = f["L2_xattn_decay"].reshape(1)
    d["l2_w_inT"], d["l2_w_outT"] = c(f["L2_xattn_W_in"].T), c(f["L2_xattn_W_out"].T)
    d["l2_b_in"] = c(f["L2_xattn_b_in"].reshape(KD, 128).T)
    for n in ("b_out", "gamma", "beta"):
        d["l2_" + n] = f["L2_xattn_" + n]
    for n in "qkvo":
        d[f"l3_w_{n}T"] = c(f["L3_xattn_w" + n].T)
    pad = 4 * 352 - L3_HIDDEN
    for n in "13":
        w = np.pad(f["L3_ffn_w" + n].T, ((0, 0), (0, pad)))
        d[f"l3_w_{n}T"] = c(w.reshape(D, 4, 352).transpose(1, 0, 2))
    d["l3_w_2T"] = c(np.pad(f["L3_ffn_w2"].T, ((0, pad), (0, 0))).reshape(4, 352, D))
    return d


def kernel(**inputs):
    from concourse import bacc
    from concourse.bass_utils import run_bass_kernel_spmd

    nc = bacc.Bacc("TRN2", target_bir_lowering=False, num_devices=1)
    arrays = {f"in_{k}": v for k, v in lay_out(inputs).items()}
    dram = {k[3:]: nc.dram_tensor(k, v.shape, mybir.dt.from_np(v.dtype), kind="ExternalInput").ap()
            for k, v in arrays.items()}
    out = nc.dram_tensor("out_x", (B, TOK, D), F32, kind="ExternalOutput").ap()
    build(nc, dram, out)
    return run_bass_kernel_spmd(nc, [arrays], core_ids=[0]).results[0]["out_x"]
```

```python
from contextlib import ExitStack

import numpy as np

import concourse.bass as bass
from concourse import mybir

F32 = mybir.dt.float32
I32 = mybir.dt.int32
U32 = mybir.dt.uint32
ALU = mybir.AluOpType
ACT = mybir.ActivationFunctionType
AX_X = mybir.AxisListType.X

B, TOK, D = 8, 112, 512
NT = B * TOK
HALF = NT // 2
KD = D // 128
T = 375
KT, TT = 3, 125
NEG = -1e30
LN_EPS = 1e-5

H, HD, KVC, QC, R = 16, 128, 128, 192, 64
QC1 = QC - 128
LOOKBACK = 8
SCALE0 = 1.0 / float(np.sqrt(np.float32(HD + R)))
GH = 4
NG = H // GH
HD1 = D // H
SCALE1 = 1.0 / float(np.sqrt(np.float32(HD1)))
SCALE3 = 1.0 / float(np.sqrt(D))
E = 16
CAP = 256
BLK = 128


def most_blocks(top_k):
    return (E + (NT * top_k - top_k) // BLK + 1) // 2 * 2


MAX_BLOCKS = most_blocks(6)
L3_HIDDEN = int(2 * D * 4 / 3)


class Chip:

    def __init__(self, nc, ctx):
        self.nc = nc
        self.used = []

        def sb(name, shape, dt=F32):
            return ctx.enter_context(nc.sbuf_tensor(name, shape, dt))

        self.x = sb("x", [TOK, B, D])
        self.xn = sb("xn", [TOK, B, D])
        self.xnT = sb("xnT", [128, KD, NT])
        self.ctxT = sb("ctxT", [128, KD, B * T])
        self.ident = sb("ident", [128, 128])
        self.ones = sb("ones", [128, 128])
        self.before = sb("before", [TOK, TOK])
        self.tanh_g = sb("tanh_g", [128, 8])
        self.raw_g = sb("raw_g", [128, 8])
        self.eps = sb("eps", [128, 1])
        self.expert_ids = sb("expert_ids", [TOK, E])
        self.gates = sb("gates", [TOK, E + 2, B])
        self.gate_w = sb("gate_w", [128, KD, E])
        self.slots = sb("slots", [TOK, 6, B], U32)
        self.slots_in = sb("slots_in", [TOK, 6, B], U32)
        self.weights = sb("weights", [TOK, B, 8])
        self.token_ids = sb("token_ids", [TOK, B])
        self.slot_tokens = sb("slot_tokens", [BLK, MAX_BLOCKS], U32)
        self.table = sb("table", [1, 3 * MAX_BLOCKS + E + 1], I32)
        self.block_ids = sb("block_ids", [TOK, MAX_BLOCKS])
        self.thresholds = sb("thresholds", [TOK, 7])
        self.turns = sb("turns", [TOK, E])
        self.twos = sb("twos", [TOK, MAX_BLOCKS // 2])
        self.xn_rows = nc.dram_tensor("xn_rows", (NT, D), F32, kind="Internal").ap()
        self.slot_rows = nc.dram_tensor("slot_rows", (MAX_BLOCKS * BLK, D), F32, kind="Internal").ap()
        self.slot_list = nc.dram_tensor("slot_list", (MAX_BLOCKS * BLK, 1), F32, kind="Internal").ap()
        self.zeros = sb("zeros", [128, D])
        self.ctx_loaded = nc.alloc_semaphore("ctx_loaded")
        self.cleared = nc.alloc_semaphore("cleared")
        self.bank = [ctx.enter_context(nc.psum_tensor(f"bank{i}", [128, 512], F32)) for i in range(8)]
        self.iota_i = sb("iota_i", [TOK, T], I32)
        self.key_ids = sb("key_ids", [TOK, T])
        self.ids_i = sb("ids_i", [TOK, B], I32)
        self.stats = sb("stats", [TOK, B, 6])
        self.mv = sb("mv", [TOK, B, 2])
        self.sd = sb("sd", [TOK, B])
        self.rstd = sb("rstd", [TOK, B])

    def sems(self, stage, *names):
        own = [self.nc.alloc_semaphore(f"{stage}_{n}") for n in names]
        self.used += own
        return own

    def clear_semaphores(self):
        self.nc.clear_and_free_semaphores(self.used)
        self.used = []
        self.nc.all_engine_barrier()


def setup_stage(nc, s, d):
    with ExitStack() as ctx:
        loaded, made, masked = s.sems("setup", "loaded", "made", "masked")
        block = ctx.enter_context(nc.Block())

        @block.sync
        def _(sp):
            sp.dma_start(s.x[:, :, :], d["x"].rearrange("b p d -> p b d")).then_inc(loaded, 16)
            sp.dma_start(s.raw_g[:, 0:4], d["g_xattn"].partition_broadcast(128)).then_inc(loaded, 16)
            sp.dma_start(s.raw_g[:, 4:8], d["g_ffn"].partition_broadcast(128)).then_inc(loaded, 16)
            for k in range(KD):
                sp.dma_start(s.ctxT[:, k, :], d["ctxT"][:, k, :]).then_inc(s.ctx_loaded, 16)
            sp.wait_ge(loaded, 16 * 3)

        @block.scalar
        def _(act):
            act.wait_ge(loaded, 16 * 3)
            act.activation(s.tanh_g[:, :], s.raw_g[:, :], ACT.Tanh)

        @block.gpsimd
        def _(pool):
            pool.memset(s.ident[:, :], 0.0).then_inc(made, 1)
            pool.memset(s.before[:, :], 1.0).then_inc(made, 1)
            pool.memset(s.ones[:, :], 1.0)
            pool.memset(s.eps[:, :], LN_EPS)
            pool.iota(s.iota_i[:, :], pattern=[[1, T]], base=0, channel_multiplier=0).then_inc(made, 1)
            pool.wait_ge(made, 3)
            pool.affine_select(out=s.ident[:, :], in_=s.ident[:, :], compare_op=ALU.not_equal, fill=1.0,
                               base=0, pattern=[[-1, 128]], channel_multiplier=1)
            pool.affine_select(out=s.before[:, :], in_=s.before[:, :], compare_op=ALU.is_gt, fill=0.0,
                               base=0, pattern=[[1, TOK]], channel_multiplier=-1)
            pool.tensor_copy(s.key_ids[:, :], s.iota_i[:, :]).then_inc(masked, 1)
            pool.iota(s.ids_i[:, :], pattern=[[TOK, B]], base=0, channel_multiplier=1).then_inc(masked, 1)
            pool.memset(s.turns[:, :], -1.0).then_inc(masked, 1)
            pool.memset(s.zeros[:, :], 0.0).then_inc(masked, 1)
            pool.wait_ge(masked, 4)
            pool.tensor_copy(s.expert_ids[:, :], s.key_ids[:, 0:E])
            pool.tensor_copy(s.token_ids[:, :], s.ids_i[:, :])
            pool.tensor_copy(s.block_ids[:, :], s.key_ids[:, 0:MAX_BLOCKS])
            pool.tensor_scalar(s.thresholds[:, :], s.key_ids[:, 0:7], float(BLK), None, ALU.mult).then_inc(masked, 1)
            pool.tensor_scalar(s.twos[:, :], s.key_ids[:, 0:MAX_BLOCKS // 2], 2.0, None, ALU.mult)
            pool.memset(s.turns[:, :].rearrange("p (e two) -> p e two", two=2)[:, :, 1], 1.0)
            pool.wait_ge(masked, 5)
            pool.memset(s.turns[:, 0:1], 0.0)
            pool.memset(s.thresholds[:, 0:1], -1.0)


def clear_scratch(sp, s):
    with sp.Fori(0, MAX_BLOCKS) as n:
        sp.dma_start(s.slot_rows[bass.ds(n * BLK, BLK), :], s.zeros[:, :]).then_inc(s.cleared, 16)
    sp.dma_start(s.slot_list.rearrange("(n p) o -> n (p o)", p=BLK), s.zeros[0:MAX_BLOCKS, 0:BLK]).then_inc(s.cleared, 16)


def layernorm_stage(nc, s, name):
    with ExitStack() as ctx:
        stats_done, mv_done, sd_done, rstd_done, norm_done, tr_done = s.sems(name, "stats_done", "mv_done", "sd_done", "rstd_done", "norm_done", "tr_done")
        block = ctx.enter_context(nc.Block())

        @block.vector
        def _(dve):
            for b in range(B):
                dve.bn_stats(s.stats[:, b, :], s.x[:, b, :]).then_inc(stats_done, 1)
            for b in range(B):
                dve.wait_ge(stats_done, b + 1)
                dve.bn_aggr(s.mv[:, b, :], s.stats[:, b, :]).then_inc(mv_done, 1)
            dve.wait_ge(sd_done, 1)
            dve.reciprocal(s.rstd[:, :], s.sd[:, :]).then_inc(rstd_done, 1)
            dve.wait_ge(rstd_done, 1)
            for b in range(B):
                dve.tensor_scalar(s.xn[:, b, :], s.x[:, b, :], s.mv[:, b, 0:1], s.rstd[:, b:b + 1],
                                  ALU.subtract, ALU.mult).then_inc(norm_done, 1)

        @block.scalar
        def _(act):
            act.wait_ge(mv_done, B)
            act.activation(s.sd[:, :], s.mv[:, :, 1], ACT.Sqrt, bias=s.eps[0:TOK, :]).then_inc(sd_done, 1)
            for b in range(B):
                act.wait_ge(tr_done, b + 1)
                act.activation(s.xnT[:, :, b * TOK:(b + 1) * TOK],
                               s.bank[b][:, 0:KD * TOK].rearrange("p (k t) -> p k t", k=KD), ACT.Copy)

        @block.tensor
        def _(pe):
            for b in range(B):
                pe.wait_ge(norm_done, b + 1)
                for k in range(KD):
                    mm = pe.transpose(s.bank[b][:, k * TOK:(k + 1) * TOK],
                                      s.xn[:, b, k * 128:(k + 1) * 128], s.ident[0:TOK, 0:TOK])
                mm.then_inc(tr_done, 1)


def router_stage(nc, s, name, gate_dram, top_k, layer, softmax, eps, shared, capacity=None):
    NB = most_blocks(top_k)
    with ExitStack() as ctx:
        def sb(n, shape, dt=F32):
            return ctx.enter_context(nc.sbuf_tensor(f"{name}_{n}", shape, dt))

        (loaded, logits_done, act_done, step, hot_done, rank_done, rows_stored) = s.sems(
            name, "loaded", "logits_done", "act_done", "step", "hot_done", "rank_done", "rows_stored")
        lmax = sb("lmax", [TOK, B])
        shifted = sb("shifted", [TOK, B, E])
        expd = sb("expd", [TOK, B, E])
        denom = sb("denom", [TOK, B, E])
        esum = sb("esum", [TOK, B])
        einv = sb("einv", [TOK, B])
        scores = sb("scores", [TOK, B, E])
        top = s.weights
        top_i = sb("top_i", [TOK, B, 8], U32)
        top_f = sb("top_f", [TOK, B, 8])
        wsum = sb("wsum", [TOK, B])
        winv = sb("winv", [TOK, B])
        hot = sb("hot", [TOK, top_k, B, E])
        part = sb("part", [TOK, B, E])
        mix = sb("mix", [TOK, B, E])
        chosen = sb("chosen", [TOK, B, E])
        kept = sb("kept", [TOK, B, E])
        place = sb("place", [TOK, B, E])
        place_in = sb("place_in", [TOK, B, E])
        slot_f = sb("slot_f", [TOK, B])
        kept_k = sb("kept_k", [TOK, B])
        counts = sb("counts", [TOK, E])
        over_t = sb("over_t", [TOK, E, 7])
        blocks = sb("blocks", [TOK, E])
        upto = sb("upto", [TOK, E])
        first = sb("first", [TOK, E])
        first_slot = sb("first_slot", [TOK, E])
        at = sb("at", [1, NB, E])
        at_turn = sb("at_turn", [1, NB, E])
        expert = sb("expert", [1, NB])
        parity = sb("parity", [1, NB])
        field = sb("field", [1, NB])
        pairs = sb("pairs", [1, NB // 2])
        pair_count = sb("pair_count", [1, 1])
        logits = s.bank[0][0:TOK, 0:B * E].rearrange("p (b e) -> p b e", b=B)
        rank = s.bank[1][0:TOK, 0:B * E].rearrange("p (b e) -> p b e", b=B)
        counted = s.bank[2][0:TOK, 0:E]
        block = ctx.enter_context(nc.Block())

        @block.sync
        def _(sp):
            sp.dma_start(s.gate_w[:, :, :], gate_dram.rearrange("(k p) e -> p k e", p=128)).then_inc(loaded, 16)
            sp.dma_start(s.xn_rows.rearrange("(b p) d -> p b d", p=TOK), s.xn[:, :, :]).then_inc(rows_stored, 16)
            load_shared(sp, shared, 0)
            sp.wait_ge(rows_stored, 16)
            sp.wait_ge(s.cleared, 16 * (MAX_BLOCKS + 1))

        @block.tensor
        def _(pe):
            pe.wait_ge(loaded, 16)
            for b in range(B):
                for k in range(KD):
                    mm = pe.matmul(logits[:, b, :], s.xnT[:, k, b * TOK:(b + 1) * TOK], s.gate_w[:, k, :],
                                   start=(k == 0), stop=(k == KD - 1))
            mm.then_inc(logits_done, 1)
            pe.wait_ge(hot_done, 1)
            for c in range(B):
                pe.matmul(counted, s.ones[0:TOK, 0:TOK], chosen[:, c, :], start=(c == 0), stop=(c == B - 1))
            for b in range(B):
                for c in range(b + 1):
                    mm = pe.matmul(rank[:, b, :], s.before[:, :] if c == b else s.ones[0:TOK, 0:TOK],
                                   chosen[:, c, :], start=(c == 0), stop=(c == b))
            mm.then_inc(rank_done, 1)

        @block.scalar
        def _(act):
            if softmax:
                act.wait_ge(step, 2)
                act.activation(expd[:, :, :], shifted[:, :, :], ACT.Exp).then_inc(act_done, 1)
            else:
                act.wait_ge(logits_done, 1)
                act.activation(expd[:, :, :], logits, ACT.Exp, scale=-1.0).then_inc(act_done, 1)

        @block.vector
        def _(dve):
            chain = [0]

            def then(instruction):
                chain[0] += 1
                instruction.then_inc(step, 1)
                dve.wait_ge(step, chain[0])

            def over(ap):
                return ap.unsqueeze(2).to_broadcast([TOK, B, E])

            def each_tile(ap):
                return ap.unsqueeze(1).to_broadcast([TOK, B, E])

            dve.wait_ge(logits_done, 1)
            if softmax:
                then(dve.tensor_reduce(lmax[:, :], logits, AX_X, ALU.max))
                then(dve.tensor_tensor(shifted[:, :, :], logits, over(lmax[:, :]), ALU.subtract))
                dve.wait_ge(act_done, 1)
                then(dve.tensor_reduce(esum[:, :], expd[:, :, :], AX_X, ALU.add))
                then(dve.reciprocal(einv[:, :], esum[:, :]))
                then(dve.tensor_tensor(scores[:, :, :], expd[:, :, :], over(einv[:, :]), ALU.mult))
            else:
                dve.wait_ge(act_done, 1)
                then(dve.tensor_scalar(denom[:, :, :], expd[:, :, :], 1.0, None, ALU.add))
                then(dve.reciprocal(scores[:, :, :], denom[:, :, :]))
            for b in range(B):
                op = dve.max(top[:, b, :], scores[:, b, :])
            then(op)
            for b in range(B):
                op = dve.max_index(top_i[:, b, :], top[:, b, :], scores[:, b, :])
            then(op)
            then(dve.tensor_copy(top_f[:, :, :], top_i[:, :, :]))
            for k in range(top_k):
                op = dve.tensor_tensor(hot[:, k, :, :], each_tile(s.expert_ids[:, :]), over(top_f[:, :, k]), ALU.is_equal)
            then(op)
            then(dve.tensor_tensor(chosen[:, :, :], hot[:, 0, :, :], hot[:, 1, :, :], ALU.add))
            for k in range(2, top_k):
                then(dve.tensor_tensor(chosen[:, :, :], chosen[:, :, :], hot[:, k, :, :], ALU.add))
            dve.sem_inc(hot_done, 1)
            then(dve.tensor_reduce(wsum[:, :], top[:, :, 0:top_k], AX_X, ALU.add))
            if eps:
                then(dve.tensor_scalar(wsum[:, :], wsum[:, :], eps, None, ALU.add))
            then(dve.reciprocal(winv[:, :], wsum[:, :]))
            then(dve.tensor_scalar(winv[:, :], winv[:, :], s.tanh_g[0:TOK, 4 + layer:5 + layer], None, ALU.mult))
            then(dve.tensor_tensor(top[:, :, 0:top_k], top[:, :, 0:top_k],
                                   winv[:, :].unsqueeze(2).to_broadcast([TOK, B, top_k]), ALU.mult))
            dve.wait_ge(rank_done, 1)
            if capacity:
                then(dve.tensor_scalar(kept[:, :, :], rank, float(capacity), None, ALU.is_lt))
                then(dve.tensor_scalar(counts[:, :], counted, float(capacity), None, ALU.min))
                then(dve.tensor_scalar(place[:, :, :], rank, float(capacity - 1), None, ALU.min))
            else:
                then(dve.tensor_copy(counts[:, :], counted))
                then(dve.tensor_copy(place[:, :, :], rank))
            then(dve.tensor_tensor(over_t[:, :, :], counts[:, :].unsqueeze(2).to_broadcast([TOK, E, 7]),
                                   s.thresholds[:, :].unsqueeze(1).to_broadcast([TOK, E, 7]), ALU.is_gt))
            then(dve.tensor_reduce(blocks[:, :], over_t[:, :, :], AX_X, ALU.add))
            then(dve.tensor_tensor_scan(upto[:, :], s.ones[0:TOK, 0:E], blocks[:, :], 0.0, ALU.mult, ALU.add))
            then(dve.tensor_tensor(first[:, :], upto[:, :], blocks[:, :], ALU.subtract))
            then(dve.tensor_scalar(first_slot[:, :], first[:, :], float(BLK), None, ALU.mult))
            then(dve.tensor_tensor(place[:, :, :], place[:, :, :], each_tile(first_slot[:, :]), ALU.add))
            for k in range(top_k):
                then(dve.tensor_tensor(part[:, :, :], hot[:, k, :, :], place[:, :, :], ALU.mult))
                then(dve.tensor_reduce(slot_f[:, :], part[:, :, :], AX_X, ALU.add))
                then(dve.tensor_copy(s.slots[:, k, :], slot_f[:, :]))
                if capacity:
                    then(dve.tensor_tensor(part[:, :, :], hot[:, k, :, :], kept[:, :, :], ALU.mult))
                    then(dve.tensor_reduce(kept_k[:, :], part[:, :, :], AX_X, ALU.add))
                    then(dve.tensor_tensor(top[:, :, k], top[:, :, k], kept_k[:, :], ALU.mult))
                    then(dve.tensor_scalar(kept_k[:, :], kept_k[:, :], -1.0, -float(NB * BLK), ALU.add, ALU.mult))
                    then(dve.tensor_tensor(slot_f[:, :], slot_f[:, :], kept_k[:, :], ALU.add))
                    then(dve.tensor_copy(s.slots_in[:, k, :], slot_f[:, :]))
            ids = s.block_ids[0:1, 0:NB].unsqueeze(2).to_broadcast([1, NB, E])
            then(dve.tensor_tensor(at[:, :, :], ids, first[0:1, :].unsqueeze(1).to_broadcast([1, NB, E]), ALU.is_ge))
            then(dve.tensor_reduce(expert[:, :], at[:, :, :], AX_X, ALU.add))
            then(dve.tensor_tensor(at_turn[:, :, :], at[:, :, :],
                                   s.turns[0:1, :].unsqueeze(1).to_broadcast([1, NB, E]), ALU.mult))
            then(dve.tensor_reduce(parity[:, :], at_turn[:, :, :], AX_X, ALU.add))
            then(dve.tensor_copy(s.table[0:1, 0:NB], parity[:, :]))
            then(dve.tensor_tensor(field[:, :], expert[:, :], parity[:, :], ALU.subtract))
            then(dve.tensor_scalar(field[:, :], field[:, :], 1.0, load_inc(layer) / 2, ALU.add, ALU.mult))
            then(dve.tensor_scalar(s.table[0:1, MAX_BLOCKS:MAX_BLOCKS + NB], field[:, :], 1.0, None, ALU.add))
            then(dve.tensor_tensor(field[:, :], expert[:, :], parity[:, :], ALU.add))
            then(dve.tensor_scalar(field[:, :], field[:, :], -1.0, load_inc(layer) / 2, ALU.add, ALU.mult))
            then(dve.tensor_scalar(s.table[0:1, 2 * MAX_BLOCKS:2 * MAX_BLOCKS + NB], field[:, :], 1.0, None, ALU.add))
            then(dve.memset(s.table[0:1, 3 * MAX_BLOCKS:3 * MAX_BLOCKS + 2], 0))
            then(dve.tensor_copy(s.table[0:1, 3 * MAX_BLOCKS + 2:3 * MAX_BLOCKS + E], first[0:1, 1:E - 1]))
            then(dve.tensor_tensor(pairs[:, :], upto[0:1, E - 1:E].to_broadcast([1, NB // 2]), s.twos[0:1, 0:NB // 2], ALU.is_gt))
            then(dve.tensor_reduce(pair_count[:, :], pairs[:, :], AX_X, ALU.add))
            then(dve.tensor_scalar(s.table[0:1, 3 * MAX_BLOCKS + E:], pair_count[:, :], -1.0, None, ALU.add))
            if layer == 0:
                then(dve.tensor_tensor(mix[:, :, :], hot[:, 0, :, :], over(top[:, :, 0]), ALU.mult))
                for k in range(1, top_k):
                    then(dve.tensor_tensor(part[:, :, :], hot[:, k, :, :], over(top[:, :, k]), ALU.mult))
                    then(dve.tensor_tensor(mix[:, :, :], mix[:, :, :], part[:, :, :], ALU.add))
                dve.tensor_copy(s.gates[:, 0:E, :].rearrange("p e b -> p b e"), mix[:, :, :])
            dve.tensor_scalar(s.gates[:, E:E + 2, :], s.ones[0:TOK, 0:2 * B].rearrange("p (u b) -> p u b", u=2),
                              s.tanh_g[0:TOK, 4 + layer:5 + layer], None, ALU.mult)


def load_inc(layer):
    return 16 * (5 if layer == 0 else 4)


class Shared:

    def __init__(self, nc, ctx, s, name, w_gate, w_up, w_down, width, func, biases=None):
        self.name, self.dram, self.width, self.func, self.biases = name, (w_gate, w_up, w_down), width, func, biases
        FC = len(chunks_of(width))
        self.w = [[ctx.enter_context(nc.sbuf_tensor(f"{name}_shared_{n}{i}", shape, F32))
                   for n, shape in (("g", [128, KD, width]), ("u", [128, KD, width]), ("d", [128, FC, D]))] for i in range(2)]
        self.loaded = s.sems(name, "shared0", "shared1")


def chunks_of(width):
    return [(c * 128, min(128, width - c * 128)) for c in range((width + 127) // 128)]


def load_unit(eng, dram, u, width, wg, wu, wd, done):
    w_gate, w_up, w_down = dram
    first = width // 128 * 128 if width % 128 else 128
    one = bass.ds(u, 1)
    eng.dma_start(wg[:, :, :], w_gate[one].rearrange("o (k p) f -> p (o k) f", p=128)).then_inc(done, 16)
    eng.dma_start(wu[:, :, :], w_up[one].rearrange("o (k p) f -> p (o k) f", p=128)).then_inc(done, 16)
    eng.dma_start(wd[:, 0:first // 128, :],
                  w_down[one, 0:first].rearrange("o (c p) f -> p (o c) f", p=128)).then_inc(done, 16)
    eng.dma_start(wd[0:width - first, first // 128, :],
                  w_down[one, first:width].rearrange("o p f -> (o p) f")).then_inc(done, 16)


def load_shared(eng, shared, i):
    load_unit(eng, shared.dram, E + i, shared.width, *shared.w[i], shared.loaded[i])


def shared_unit_stage(nc, s, shared, i, layer, dispatch=None, combine=None):
    width, func, biases = shared.width, shared.func, shared.biases
    chunks = chunks_of(width)
    FC = len(chunks)
    PIECES = 2 * FC
    DEPTH = 4
    name = f"{shared.name}s{i}"
    with ExitStack() as ctx:
        def sb(n, shape, dt=F32):
            return ctx.enter_context(nc.sbuf_tensor(f"{name}_{n}", shape, dt))

        (g_done, u_done, act_done, h_done, y_done, y_added, prepared, extra, gT_done, gT_copied, b2_done, scattered,
         listed, turned, combined) = s.sems(
            name, "g_done", "u_done", "act_done", "h_done", "y_done", "y_added", "prepared", "extra", "gT_done",
            "gT_copied", "b2_done", "scattered", "listed", "turned", "combined")
        if combine:
            gathered = s.sems(name, *[f"gathered{j}" for j in range(DEPTH)])
        wg, wu, wd = shared.w[i]
        acted = sb("acted", [128, 2, HALF])
        hT = sb("hT", [128, FC, NT])
        if biases:
            bg, bu = sb("bg", [128, FC]), sb("bu", [128, FC])
        output_bias = biases and dispatch
        if output_bias:
            bd, gT = sb("bd", [E + 2, D]), sb("gT", [E + 2, B, TOK])
        if dispatch:
            slot_list = sb("slot_list", [MAX_BLOCKS, BLK])
        if combine:
            rows = sb("rows", [TOK, DEPTH, D])
        block = ctx.enter_context(nc.Block())

        @block.sync
        def _(sp):
            if biases:
                sp.dma_start(bg[:, :], biases[0][:, E + i, :]).then_inc(extra, 16)
                sp.dma_start(bu[:, :], biases[1][:, E + i, :]).then_inc(extra, 16)
            if output_bias:
                sp.dma_start(bd[:, :], biases[2]).then_inc(extra, 16)
            if i == 0:
                load_shared(sp, shared, 1)
            if dispatch:
                sp.wait_ge(scattered, 16 * dispatch * B)
                sp.dma_start(slot_list[:, :], s.slot_list.rearrange("(n p) o -> n (p o)", p=BLK)).then_inc(listed, 16)

        @block.gpsimd
        def _(pool):
            if dispatch:
                bound = {}
                slots = s.slots
                if layer == 1:
                    slots, bound = s.slots_in, dict(bounds_check=most_blocks(dispatch) * BLK - 1, oob_is_err=False)
                for k in range(dispatch):
                    for b in range(B):
                        pool.indirect_dma_start(s.slot_list, bass.IndirectOffsetOnAxis(ap=slots[:, k, b:b + 1], axis=0),
                                                s.token_ids[:, b:b + 1], None, **bound).then_inc(scattered, 16)
            if combine:
                for j in range(combine * B):
                    k, b = j // B, j % B
                    if j >= DEPTH:
                        pool.wait_ge(combined, j - DEPTH + 1)
                    pool.indirect_dma_start(rows[:, j % DEPTH, :], None, s.slot_rows,
                                            bass.IndirectOffsetOnAxis(ap=s.slots[:, k, b:b + 1], axis=0))\
                        .then_inc(gathered[j % DEPTH], 16)

        @block.tensor
        def _(pe):
            if output_bias:
                for b in range(B):
                    mm = pe.transpose(s.bank[b][0:E + 2, 0:TOK], s.gates[:, :, b], s.ident[0:TOK, 0:TOK])
                mm.then_inc(gT_done, 1)
                pe.wait_ge(extra, 48)
                pe.wait_ge(gT_copied, 1)
                for b in range(B):
                    mm = pe.matmul(s.bank[b][0:TOK, :], gT[:, b, :], bd[:, :], start=True, stop=True)
                mm.then_inc(b2_done, 1)
                pe.wait_ge(prepared, 2 * B)
            pe.wait_ge(shared.loaded[i], 16 * 4)
            for q in range(PIECES):
                half, (f0, fn) = q // FC, chunks[q % FC]
                if q >= 2:
                    pe.wait_ge(h_done, q - 1)
                for weight, out, done in ((wg, s.bank[2 * (q % 2)], g_done), (wu, s.bank[2 * (q % 2) + 1], u_done)):
                    for k in range(KD):
                        mm = pe.matmul(out[0:fn, 0:HALF], weight[:, k, f0:f0 + fn],
                                       s.xnT[:, k, half * HALF:(half + 1) * HALF], start=(k == 0), stop=(k == KD - 1))
                    mm.then_inc(done, 1)
            for b in range(B):
                pe.wait_ge(h_done, FC * (1 + b // (B // 2)))
                if b >= 4:
                    pe.wait_ge(y_added, b - 3)
                for c, (f0, fn) in enumerate(chunks):
                    mm = pe.matmul(s.bank[4 + b % 4][0:TOK, :], hT[0:fn, c, b * TOK:(b + 1) * TOK], wd[0:fn, c, :],
                                   start=(c == 0), stop=(c == FC - 1))
                mm.then_inc(y_done, 1)
            if dispatch:
                pe.wait_ge(listed, 16)
                pe.transpose(s.bank[0][:, 0:MAX_BLOCKS], slot_list[:, :], s.ident[0:MAX_BLOCKS, 0:MAX_BLOCKS])\
                  .then_inc(turned, 1)

        @block.scalar
        def _(act):
            if output_bias:
                act.wait_ge(gT_done, 1)
                for b in range(B):
                    op = act.activation(gT[:, b, :], s.bank[b][0:E + 2, 0:TOK], ACT.Copy)
                op.then_inc(gT_copied, 1)
            if biases:
                act.wait_ge(extra, 48 if output_bias else 32)
            for q in range(PIECES):
                f0, fn = chunks[q % FC]
                act.wait_ge(g_done, q + 1)
                if q >= 2:
                    act.wait_ge(h_done, q - 1)
                kind = dict(bias=bg[0:fn, q % FC:q % FC + 1]) if biases else {}
                act.activation(acted[0:fn, q % 2, :], s.bank[2 * (q % 2)][0:fn, 0:HALF], func, **kind).then_inc(act_done, 1)

        @block.vector
        def _(dve):
            added = [0]

            def combine_some(upto):
                while combine and added[0] < min(upto, combine * B):
                    j = added[0]
                    k, b = j // B, j % B
                    dve.wait_ge(gathered[j % DEPTH], 16 * (j // DEPTH + 1))
                    if j >= B:
                        dve.wait_ge(combined, j - B + 1)
                    dve.scalar_tensor_tensor(out=s.x[:, b, :], in0=rows[:, j % DEPTH, :],
                                             scalar=s.weights[:, b, k:k + 1], in1=s.x[:, b, :],
                                             op0=ALU.mult, op1=ALU.add).then_inc(combined, 1)
                    added[0] += 1

            if output_bias:
                for b in range(B):
                    dve.scalar_tensor_tensor(out=s.x[:, b, :], in0=s.xn[:, b, :],
                                             scalar=s.tanh_g[0:TOK, 4 + layer:5 + layer], in1=s.x[:, b, :],
                                             op0=ALU.mult, op1=ALU.add).then_inc(prepared, 1)
                dve.wait_ge(b2_done, 1)
                for b in range(B):
                    dve.wait_ge(prepared, B + b)
                    dve.tensor_tensor(s.x[:, b, :], s.x[:, b, :], s.bank[b][0:TOK, :], ALU.add).then_inc(prepared, 1)
                dve.wait_ge(prepared, 2 * B)
            if biases:
                dve.wait_ge(extra, 48 if output_bias else 32)
            for q in range(PIECES):
                half, c, (f0, fn) = q // FC, q % FC, chunks[q % FC]
                dve.wait_ge(u_done, q + 1)
                dve.wait_ge(act_done, q + 1)
                out = hT[0:fn, c, half * HALF:(half + 1) * HALF]
                up = s.bank[2 * (q % 2) + 1][0:fn, 0:HALF]
                if biases:
                    dve.scalar_tensor_tensor(out=out, in0=up, scalar=bu[0:fn, c:c + 1], in1=acted[0:fn, q % 2, :],
                                             op0=ALU.add, op1=ALU.mult).then_inc(h_done, 1)
                else:
                    dve.tensor_tensor(out, up, acted[0:fn, q % 2, :], ALU.mult).then_inc(h_done, 1)
                combine_some(8 * (q + 1))
            combine_some(combine * B if combine else 0)
            if combine:
                dve.wait_ge(combined, combine * B)
            for b in range(B):
                dve.wait_ge(y_done, b + 1)
                dve.scalar_tensor_tensor(out=s.x[:, b, :], in0=s.bank[4 + b % 4][0:TOK, :],
                                         scalar=s.gates[:, E + i, b:b + 1], in1=s.x[:, b, :],
                                         op0=ALU.mult, op1=ALU.add).then_inc(y_added, 1)
            if dispatch:
                dve.wait_ge(turned, 1)
                dve.tensor_copy(s.slot_tokens[:, :], s.bank[0][:, 0:MAX_BLOCKS])


def routed_blocks_stage(nc, s, name, layer, top_k, dram, width, func, biases=None):
    chunks = chunks_of(width)
    FC = len(chunks)
    with ExitStack() as ctx:
        def sb(n, shape, dt=F32):
            return ctx.enter_context(nc.sbuf_tensor(f"{name}_{n}", shape, dt))

        (w_loaded0, w_loaded1, ids_copied, xg_loaded0, xg_loaded1, tx_done, xT_copied, g_done, u_done, act_done,
         h_done, th_done, hT_copied, y_done, y_copied, stored0, stored1) = s.sems(
            name, "w_loaded0", "w_loaded1", "ids_copied", "xg_loaded0", "xg_loaded1", "tx_done", "xT_copied", "g_done",
            "u_done", "act_done", "h_done", "th_done", "hT_copied", "y_done", "y_copied", "stored0", "stored1")
        w_loaded, xg_loaded, stored = (w_loaded0, w_loaded1), (xg_loaded0, xg_loaded1), (stored0, stored1)
        wg = sb("wg", [128, 2, KD, width])
        wu = sb("wu", [128, 2, KD, width])
        wd = sb("wd", [128, 2, FC, D])
        ids = sb("ids", [BLK, 2], U32)
        spare = sb("spare", [BLK, 1])
        spare_act = sb("spare_act", [BLK, 1])
        xg = sb("xg", [BLK, 2, D])
        xT = sb("xT", [128, 2, KD, BLK])
        acted = sb("acted", [BLK, 2, width])
        h = sb("h", [BLK, 2, width])
        hT = sb("hT", [128, 2, FC, BLK])
        y = sb("y", [BLK, 2, D])
        if biases is not None:
            bias_rows = sb("bias_rows", [1, 2, 2, width])
        bank_g, bank_u, bank_x, bank_h, bank_y = s.bank[0:2], s.bank[2:4], s.bank[4], s.bank[5], s.bank[6:8]
        block = ctx.enter_context(nc.Block())
        PAIRS = 3 * MAX_BLOCKS + E
        most_pairs = most_blocks(top_k) // 2

        def pairs_less_one(eng):
            return eng.value_load(s.table[0:1, PAIRS:PAIRS + 1], min_val=1, max_val=most_pairs - 1)

        def over_blocks(eng, first, step, last):
            pairs = pairs_less_one(eng)
            first()
            with eng.Fori(0, pairs) as i:
                step(i * 2 + 1, 1, i)
                step(i * 2 + 2, 0, i + 1)
            last(pairs * 2 + 1, 1, pairs)
            return pairs

        @block.sync
        def _(sp):
            sp.sem_inc(w_loaded[0], 1)
            sp.sem_inc(w_loaded[1], 1)
            with sp.Fori(0, E // 2) as i:
                for v in range(2):
                    free_at = sp.value_load(s.table[0:1, bass.ds(i * 2 + (3 * MAX_BLOCKS + v), 1)], min_val=0,
                                            max_val=MAX_BLOCKS)
                    sp.wait_ge(y_done, free_at + 2)
                    load_unit(sp, dram, i * 2 + v, width, wg[:, v, :, :], wu[:, v, :, :], wd[:, v, :, :], w_loaded[v])
                    if biases is not None:
                        sp.dma_start(bias_rows[0:1, v, :, :], biases[bass.ds(i * 2 + v, 1)]).then_inc(w_loaded[v], 16)

        @block.gpsimd
        def _(pool):
            pairs = pairs_less_one(pool)
            pool.memset(spare[:, :], 0.0)
            with pool.Fori(0, pairs + 1) as i:
                for v in range(2):
                    n = i * 2 + v
                    pool.wait_ge(tx_done, n + 1)
                    pool.tensor_copy(ids[:, v:v + 1], s.slot_tokens[:, bass.ds(n, 1)]).then_inc(ids_copied, 1)
                    pool.wait_ge(ids_copied, n + 1)
                    pool.tensor_tensor(spare[:, :], spare[:, :], spare[:, :], ALU.add)
                    pool.indirect_dma_start(xg[:, v, :], None, s.xn_rows,
                                            bass.IndirectOffsetOnAxis(ap=ids[:, v:v + 1], axis=0)).then_inc(xg_loaded[v], 16)

        @block.tensor
        def _(pe):
            pe.sem_inc(tx_done, 2)
            pe.sem_inc(u_done, 2)
            pe.sem_inc(th_done, 2)
            pe.sem_inc(y_done, 2)

            def turn_x(n, v, m):
                pe.wait_ge(xg_loaded[v], m * 16 + 16)
                pe.wait_ge(xT_copied, n + 1)
                for k in range(KD):
                    mm = pe.transpose(bank_x[:, k * BLK:(k + 1) * BLK], xg[:, v, k * 128:(k + 1) * 128], s.ident[:, :])
                mm.then_inc(tx_done, 1)

            def gate_up(n, v, m):
                at = pe.value_load(s.table[0:1, bass.ds(n, 1)], min_val=0, max_val=1)
                need = [pe.value_load(s.table[0:1, bass.ds(n + (w + 1) * MAX_BLOCKS, 1)], min_val=1,
                                      max_val=1 + load_inc(layer) * E // 2) for w in range(2)]
                for w in range(2):
                    pe.wait_ge(w_loaded[w], need[w])
                pe.wait_ge(xT_copied, n + 2)
                pe.wait_ge(h_done, n + 1)
                for j, (w, bank, done) in enumerate(((wg, bank_g[v], g_done), (wu, bank_u[v], u_done))):
                    if biases is not None:
                        pe.matmul(bank[:, 0:width], s.ones[0:1, :], bias_rows[0:1, bass.ds(at, 1), j, :]
                                  .rearrange("p o f -> p (o f)"), start=True, stop=False)
                    for k in range(KD):
                        mm = pe.matmul(bank[:, 0:width], xT[:, v, k, :],
                                       w[:, bass.ds(at, 1), k, :].rearrange("p o f -> p (o f)"),
                                       start=(k == 0 and biases is None), stop=(k == KD - 1))
                    mm.then_inc(done, 1)

            def turn_h(n, v, m):
                pe.wait_ge(h_done, n + 3)
                pe.wait_ge(hT_copied, n + 1)
                for c, (f0, fn) in enumerate(chunks):
                    mm = pe.transpose(bank_h[0:fn, c * BLK:(c + 1) * BLK], h[:, v, f0:f0 + fn], s.ident[:, :])
                mm.then_inc(th_done, 1)

            def down(n, v, m):
                at = pe.value_load(s.table[0:1, bass.ds(n, 1)], min_val=0, max_val=1)
                pe.wait_ge(hT_copied, n + 2)
                pe.wait_ge(y_copied, n + 1)
                for c, (f0, fn) in enumerate(chunks):
                    mm = pe.matmul(bank_y[v][:, :], hT[0:fn, v, c, :],
                                   wd[0:fn, bass.ds(at, 1), c, :].rearrange("p o f -> p (o f)"),
                                   start=(c == 0), stop=(c == FC - 1))
                mm.then_inc(y_done, 1)

            def first():
                turn_x(0, 0, 0)
                gate_up(0, 0, 0)
                turn_x(1, 1, 0)
                turn_h(0, 0, 0)

            def step(n, v, m):
                gate_up(n, v, m)
                down(n - 1, 1 - v, m)
                turn_x(n + 1, 1 - v, m + v)
                turn_h(n, v, m)

            def last(n, v, m):
                gate_up(n, v, m)
                down(n - 1, 1 - v, m)
                turn_h(n, v, m)
                down(n, v, m)

            over_blocks(pe, first, step, last)

        @block.scalar
        def _(act):
            act.sem_inc(xT_copied, 1)
            act.sem_inc(stored[0], 1)
            act.sem_inc(stored[1], 1)

            def copy_xT(n, v, m):
                act.wait_ge(tx_done, n + 3)
                act.wait_ge(u_done, n + 1)
                act.activation(xT[:, v, :, :], bank_x[:, :].rearrange("p (k n) -> p k n", k=KD), ACT.Copy)\
                   .then_inc(xT_copied, 1)

            def hidden(n, v, m):
                act.wait_ge(g_done, n + 1)
                act.wait_ge(h_done, n + 1)
                act.activation(acted[:, v, :], bank_g[v][:, 0:width], func).then_inc(act_done, 1)

            def store(n, v, m):
                act.wait_ge(y_copied, n + 3)
                act.dma_start(s.slot_rows[bass.ds(n * BLK, BLK), :], y[:, v, :]).then_inc(stored[v], 16)

            def first():
                copy_xT(0, 0, 0)
                hidden(0, 0, 0)
                copy_xT(1, 1, 0)

            def step(n, v, m):
                hidden(n, v, m)
                store(n - 1, 1 - v, m)
                copy_xT(n + 1, 1 - v, m + v)

            def last(n, v, m):
                hidden(n, v, m)
                store(n - 1, 1 - v, m)
                store(n, v, m)

            pairs = over_blocks(act, first, step, last)
            for v in range(2):
                act.wait_ge(stored[v], pairs * 16 + 17)
            act.copy(spare_act[:, :], s.ones[:, 0:1])

        @block.vector
        def _(dve):
            dve.sem_inc(h_done, 2)
            dve.sem_inc(hT_copied, 1)
            dve.sem_inc(y_copied, 2)

            def product(n, v, m):
                dve.wait_ge(u_done, n + 3)
                dve.wait_ge(act_done, n + 1)
                dve.wait_ge(th_done, n + 1)
                dve.tensor_tensor(h[:, v, :], bank_u[v][:, 0:width], acted[:, v, :], ALU.mult).then_inc(h_done, 1)

            def copy_y(n, v, m):
                dve.wait_ge(y_done, n + 3)
                dve.wait_ge(stored[v], m * 16 + 1)
                dve.tensor_copy(y[:, v, :], bank_y[v][:, :]).then_inc(y_copied, 1)

            def copy_hT(n, v, m):
                dve.wait_ge(th_done, n + 3)
                dve.wait_ge(y_done, n + 1)
                whole, rest = width // 128, width % 128
                op = dve.tensor_copy(hT[:, v, 0:whole, :], bank_h[:, 0:whole * BLK].rearrange("p (c n) -> p c n", c=whole))
                if rest:
                    op = dve.tensor_copy(hT[0:rest, v, whole, :], bank_h[0:rest, whole * BLK:(whole + 1) * BLK])
                op.then_inc(hT_copied, 1)

            def first():
                product(0, 0, 0)
                copy_hT(0, 0, 0)

            def step(n, v, m):
                product(n, v, m)
                copy_y(n - 1, 1 - v, m + v - 1)
                copy_hT(n, v, m)

            def last(n, v, m):
                product(n, v, m)
                copy_y(n - 1, 1 - v, m + v - 1)
                copy_hT(n, v, m)
                copy_y(n, v, m)

            over_blocks(dve, first, step, last)


def routed_ffn(nc, s, d, layer, top_k, width, func, softmax, eps, capacity=None):
    dram = tuple(d[f"l{layer}_{n}"] for n in ("wg", "wu", "wd"))
    biases = tuple(d[f"l{layer}_{n}"] for n in ("bg", "bu", "bd")) if layer == 0 else None
    bias_rows = d["l0_bias_rows"] if layer == 0 else None
    with ExitStack() as own:
        shared = Shared(nc, own, s, f"f{layer}", *dram, width, func, biases)
        router_stage(nc, s, f"r{layer}", d[f"l{layer}_router"], top_k, layer, softmax, eps, shared, capacity)
        shared_unit_stage(nc, s, shared, 0, layer, dispatch=top_k)
        routed_blocks_stage(nc, s, f"f{layer}b", layer, top_k, dram, width, func, bias_rows)
        shared_unit_stage(nc, s, shared, 1, layer, combine=top_k)


def ternary_units_stage(nc, s, t):
    units, width = 4, 352
    chunks = chunks_of(width)
    FC = len(chunks)
    PIECES = 2 * FC
    with ExitStack() as ctx:
        def sb(n, shape, dt=F32):
            return ctx.enter_context(nc.sbuf_tensor(f"f3_{n}", shape, dt))

        g_done, u_done, act_done, h_done, y_done, y_added = s.sems(
            "f3", "g_done", "u_done", "act_done", "h_done", "y_done", "y_added")
        acted = sb("acted", [128, 2, HALF])
        hT = [sb(f"hT{i}", [128, FC, NT]) for i in range(2)]
        block = ctx.enter_context(nc.Block())

        @block.tensor
        def _(pe):
            for u in range(units):
                for q in range(PIECES):
                    half, (f0, fn) = q // FC, chunks[q % FC]
                    n = u * PIECES + q
                    if n >= 2:
                        pe.wait_ge(h_done, n - 1)
                    for weight, out, done in ((t.wg[u], s.bank[2 * (q % 2)], g_done),
                                              (t.wu[u], s.bank[2 * (q % 2) + 1], u_done)):
                        for k in range(KD):
                            mm = pe.matmul(out[0:fn, 0:HALF], weight[:, k, f0:f0 + fn],
                                           s.xnT[:, k, half * HALF:(half + 1) * HALF], start=(k == 0), stop=(k == KD - 1))
                        mm.then_inc(done, 1)
                for b in range(B):
                    pe.wait_ge(h_done, u * PIECES + FC * (1 + b // (B // 2)))
                    if u * B + b >= 4:
                        pe.wait_ge(y_added, u * B + b - 3)
                    for c, (f0, fn) in enumerate(chunks):
                        mm = pe.matmul(s.bank[4 + b % 4][0:TOK, :], hT[u % 2][0:fn, c, b * TOK:(b + 1) * TOK],
                                       t.wd[u][0:fn, c, :], start=(c == 0), stop=(c == FC - 1))
                    mm.then_inc(y_done, 1)

        @block.scalar
        def _(act):
            for n in range(units * PIECES):
                q = n % PIECES
                f0, fn = chunks[q % FC]
                act.wait_ge(g_done, n + 1)
                if n >= 2:
                    act.wait_ge(h_done, n - 1)
                act.activation(acted[0:fn, q % 2, :], s.bank[2 * (q % 2)][0:fn, 0:HALF], ACT.Silu,
                               scale=t.scale[0:fn, 0:1]).then_inc(act_done, 1)

        @block.vector
        def _(dve):
            for u in range(units):
                for q in range(PIECES):
                    half, c, (f0, fn) = q // FC, q % FC, chunks[q % FC]
                    dve.wait_ge(u_done, u * PIECES + q + 1)
                    dve.wait_ge(act_done, u * PIECES + q + 1)
                    if u >= 2:
                        dve.wait_ge(y_done, (u - 1) * B)
                    dve.scalar_tensor_tensor(out=hT[u % 2][0:fn, c, half * HALF:(half + 1) * HALF],
                                             in0=s.bank[2 * (q % 2) + 1][0:fn, 0:HALF], scalar=t.scale[0:fn, 1:2],
                                             in1=acted[0:fn, q % 2, :], op0=ALU.mult, op1=ALU.mult).then_inc(h_done, 1)
                for b in range(B):
                    dve.wait_ge(y_done, u * B + b + 1)
                    if u:
                        dve.wait_ge(y_added, (u - 1) * B + b + 1)
                    dve.scalar_tensor_tensor(out=s.x[:, b, :], in0=s.bank[4 + b % 4][0:TOK, :],
                                             scalar=s.gates[:, u, b:b + 1], in1=s.x[:, b, :],
                                             op0=ALU.mult, op1=ALU.add).then_inc(y_added, 1)


def latent_project_stage(nc, s, d, a):
    with ExitStack() as ctx:
        def sb(n, shape, dt=F32):
            return ctx.enter_context(nc.sbuf_tensor(f"l0p_{n}", shape, dt))

        (loaded, kv_done, kv_copied, rot_done, rot_mul, rot_added, tr_done, tr_copied, q_done, ids_f) = s.sems("l0p", "loaded", "kv_done", "kv_copied", "rot_done", "rot_mul", "rot_added", "tr_done",
            "tr_copied", "q_done", "ids_f")
        masked = a.masked
        w_kvc = sb("w_kvc", [128, KD, KVC])
        w_kr = sb("w_kr", [KVC, 2, 128])
        w_dq = sb("w_dq", [128, KD, QC])
        part = sb("part", [128, 2, 2, T])
        ids_i = sb("ids_i", [TOK, B], I32)
        ids = sb("ids", [TOK, B])
        low = sb("low", [TOK, 2, T])
        block = ctx.enter_context(nc.Block())

        @block.sync
        def _(sp):
            sp.dma_start(w_kvc[:, :, :], d["l0_w_kvc"].rearrange("(k p) n -> p k n", p=128)).then_inc(loaded, 16)
            sp.dma_start(w_kr[:, :, :], d["l0_w_kr"]).then_inc(loaded, 16)
            sp.dma_start(w_dq[:, :, :], d["l0_w_dq"].rearrange("(k p) n -> p k n", p=128)).then_inc(loaded, 16)
            sp.dma_start(a.cos[:, :], d["cos"]).then_inc(loaded, 16)
            sp.dma_start(a.sin[:, :], d["sin"]).then_inc(loaded, 16)
            sp.dma_start(ids_i[:, :], d["ids"]).then_inc(loaded, 16)
            clear_scratch(sp, s)

        @block.tensor
        def _(pe):
            pe.wait_ge(loaded, 96)
            pe.wait_ge(s.ctx_loaded, 16 * KD)
            for b in range(B + 1):
                if b < B:
                    if b >= 2:
                        pe.wait_ge(kv_copied, b - 1)
                    for k in range(KD):
                        mm = pe.matmul(s.bank[b % 2][:, 0:T], w_kvc[:, k, :], s.ctxT[:, k, b * T:(b + 1) * T],
                                       start=(k == 0), stop=(k == KD - 1))
                    mm.then_inc(kv_done, 1)
                if b >= 1:
                    c = b - 1
                    pe.wait_ge(kv_copied, c + 1)
                    if c >= 2:
                        pe.wait_ge(rot_mul, 2 * (c - 1))
                        pe.wait_ge(tr_copied, c - 1)
                    for v in range(2):
                        mm = pe.matmul(s.bank[2 + 2 * (c % 2) + v][:, 0:T], w_kr[:, v, :],
                                       a.kvcT[:, c * T:(c + 1) * T], start=True, stop=True)
                    mm.then_inc(rot_done, 1)
                    for t in range(KT):
                        mm = pe.transpose(s.bank[6 + c % 2][0:TT, t * KVC:(t + 1) * KVC],
                                          a.kvcT[:, c * T + t * TT:c * T + (t + 1) * TT], s.ident[:, :])
                    mm.then_inc(tr_done, 1)
            for q in range(4):
                m, half = q // 2, q % 2
                rows = 128 if m == 0 else QC1
                if q < 2:
                    pe.wait_ge(kv_copied, B)
                else:
                    pe.wait_ge(rot_mul, 2 * B)
                for k in range(KD):
                    mm = pe.matmul(s.bank[q][0:rows, 0:HALF], w_dq[:, k, m * 128:m * 128 + rows],
                                   s.xnT[:, k, half * HALF:(half + 1) * HALF], start=(k == 0), stop=(k == KD - 1))
                mm.then_inc(q_done, 1)

        @block.scalar
        def _(act):
            for b in range(B + 1):
                if b < B:
                    act.wait_ge(kv_done, b + 1)
                    act.activation(a.kvcT[:, b * T:(b + 1) * T], s.bank[b % 2][:, 0:T], ACT.Copy).then_inc(kv_copied, 1)
                if b >= 1:
                    c = b - 1
                    act.wait_ge(tr_done, c + 1)
                    act.activation(a.kvc[:, c * KT:(c + 1) * KT, :],
                                   s.bank[6 + c % 2][0:TT, 0:KT * KVC].rearrange("p (t n) -> p t n", t=KT),
                                   ACT.Copy).then_inc(tr_copied, 1)
            for q in range(4):
                act.wait_ge(q_done, q + 1)
                dst = (a.qcT0, a.qcT1)[q // 2]
                rows = dst.shape[0]
                act.activation(dst[:, (q % 2) * HALF:(q % 2 + 1) * HALF], s.bank[q][0:rows, 0:HALF], ACT.Copy)

        @block.vector
        def _(dve):
            for b in range(B):
                dve.wait_ge(rot_done, b + 1)
                if b >= 2:
                    dve.wait_ge(rot_added, b - 1)
                for v, table in enumerate((a.cos, a.sin)):
                    dve.tensor_tensor(part[:, b % 2, v, :], s.bank[2 + 2 * (b % 2) + v][:, 0:T], table[:, :],
                                      ALU.mult).then_inc(rot_mul, 1)
                dve.wait_ge(rot_mul, 2 * (b + 1))
                dve.tensor_tensor(a.krT[:, b * T:(b + 1) * T], part[:, b % 2, 0, :], part[:, b % 2, 1, :],
                                  ALU.add).then_inc(rot_added, 1)
            dve.tensor_copy(ids[:, :], ids_i[:, :]).then_inc(ids_f, 1)
            dve.wait_ge(ids_f, 1)
            for b in range(B):
                dve.tensor_scalar(low[:, 0, :], s.key_ids[:, :], ids[:, b:b + 1], -float(LOOKBACK),
                                  ALU.subtract, ALU.is_ge).then_inc(masked, 1)
                dve.tensor_scalar(low[:, 1, :], s.key_ids[:, :], ids[:, b:b + 1], 0.0,
                                  ALU.subtract, ALU.is_le).then_inc(masked, 1)
                dve.wait_ge(masked, 4 * b + 2)
                dve.scalar_tensor_tensor(out=a.mask[:, b, :], in0=low[:, 0, :], scalar=-2.0, in1=low[:, 1, :],
                                         op0=ALU.add, op1=ALU.add).then_inc(masked, 1)
                dve.wait_ge(masked, 4 * b + 3)
                dve.tensor_scalar(a.mask[:, b, :], a.mask[:, b, :], -NEG / SCALE0, None, ALU.mult).then_inc(masked, 1)


def latent_attention_stage(nc, s, d, a):
    N = B * GH
    BUFS = 4
    with ExitStack() as ctx:
        def sb(n, shape, dt=F32):
            return ctx.enter_context(nc.sbuf_tensor(f"l0a_{n}", shape, dt))

        (loaded, w_done, w_copied, qr_done, qr_mul, qr_added, s_done, s_masked, shift, e_done, inv_done, p_done,
         pt_done, pt_copied, z_done, z_copied, y_done, y_added) = s.sems("l0a", "loaded", "w_done", "w_copied", "qr_done", "qr_mul", "qr_added", "s_done", "s_masked",
            "shift", "e_done", "inv_done", "p_done", "pt_done", "pt_copied", "z_done", "z_copied", "y_done", "y_added")
        w_uq = sb("w_uq", [HD, GH, QC])
        w_uk = sb("w_uk", [HD, GH, KVC])
        w_uv = sb("w_uv", [HD, GH, KVC])
        w_o = sb("w_o", [HD, GH, D])
        w_qr0 = sb("w_qr0", [128, 2, GH * R])
        w_qr1 = sb("w_qr1", [QC1, 2, GH * R])
        qk0 = sb("qk0", [128, GH, KVC])
        qk1 = sb("qk1", [QC1, GH, KVC])
        vo = sb("vo", [KVC, GH, D])
        qT = s.xnT
        qrT = sb("qrT", [128, GH // 2, NT])
        shared = sb("shared", [128, 2 * KT * GH * TOK])
        part = shared[:, 0:4 * HALF].rearrange("p (i v n) -> p i v n", i=2, v=2)
        pT = shared[0:TT, :].rearrange("p (i t h n) -> p i t h n", i=2, t=KT, h=GH)
        p = sb("p", [TOK, BUFS, T])
        top = sb("top", [TOK, BUFS])
        spare = sb("spare", [TOK, 1])
        low = sb("low", [TOK, BUFS])
        total = sb("total", [TOK, BUFS])
        inv = sb("inv", [TOK, BUFS])
        zT = sb("zT", [KVC, 2, GH, TOK])
        block = ctx.enter_context(nc.Block())
        W_COPIES = 2 + GH + 2 * GH
        QR = 2 * 2

        @block.sync
        def _(sp):
            with sp.Fori(0, NG) as g:
                sp.wait_ge(qr_done, g * QR + 1)
                one = bass.ds(g, 1)
                sp.dma_start(w_uq[:, :, :], d["l0_w_uqT"][one].rearrange("o h p n -> p (o h) n")).then_inc(loaded, 16)
                sp.dma_start(w_uk[:, :, :], d["l0_w_ukT"][one].rearrange("o h p n -> p (o h) n")).then_inc(loaded, 16)
                sp.dma_start(w_uv[:, :, :], d["l0_w_uvT"][one].rearrange("o h p n -> p (o h) n")).then_inc(loaded, 16)
                sp.dma_start(w_o[:, :, :], d["l0_w_o"][one].rearrange("o h p n -> p (o h) n")).then_inc(loaded, 16)
                sp.dma_start(w_qr0[:, :, :], d["l0_w_qr"][one, :, 0:128].rearrange("o v p n -> p (o v) n")).then_inc(loaded, 16)
                sp.dma_start(w_qr1[:, :, :], d["l0_w_qr"][one, :, 128:QC].rearrange("o v p n -> p (o v) n")).then_inc(loaded, 16)

        @block.tensor
        def _(pe):
            pe.sem_inc(qr_done, 1)

            def scores(g, n):
                b, j = n // GH, n % GH
                if n >= 3:
                    pe.wait_ge(s_masked, 1 + g * N + n - 2)
                out = s.bank[n % 3][0:TOK, 0:T]
                r = 64 * (j % 2)
                pe.matmul(out, qT[:, j, b * TOK:(b + 1) * TOK], a.kvcT[:, b * T:(b + 1) * T], start=True, stop=False)
                pe.matmul(out, qrT[r:r + R, j // 2, b * TOK:(b + 1) * TOK], a.krT[r:r + R, b * T:(b + 1) * T],
                          start=False, stop=True).then_inc(s_done, 1)

            def turn(g, n):
                pe.wait_ge(p_done, g * N + n + 1)
                if n >= 2:
                    pe.wait_ge(pt_copied, 1 + g * N + n - 1)
                for t in range(KT):
                    mm = pe.transpose(s.bank[3 + n % 2][0:TT, t * TOK:(t + 1) * TOK],
                                      p[:, n % BUFS, t * TT:(t + 1) * TT], s.ident[0:TOK, 0:TOK])
                mm.then_inc(pt_done, 1)

            def mix(g, b):
                pe.wait_ge(pt_copied, 1 + g * N + (b + 1) * GH)
                if b:
                    pe.wait_ge(z_copied, 1 + g * B + b)
                for t in range(KT):
                    mm = pe.matmul(s.bank[5][:, 0:GH * TOK], a.kvc[:, b * KT + t, :],
                                   pT[:, b % 2, t, :, :].rearrange("p h n -> p (h n)"),
                                   start=(t == 0), stop=(t == KT - 1))
                mm.then_inc(z_done, 1)

            def project(g, b):
                pe.wait_ge(z_copied, 1 + g * B + b + 1)
                if b >= 2:
                    pe.wait_ge(y_added, 1 + g * B + b - 1)
                for j in range(GH):
                    mm = pe.matmul(s.bank[6 + b % 2][0:TOK, :], zT[:, b % 2, j, :], vo[:, j, :],
                                   start=(j == 0), stop=(j == GH - 1))
                mm.then_inc(y_done, 1)

            with pe.Fori(0, NG) as g:
                pe.wait_ge(loaded, (g + 1) * 96)
                pe.wait_ge(y_added, 1 + g * B)
                for j in range(GH):
                    pe.matmul(s.bank[0][:, j * KVC:(j + 1) * KVC], w_uq[:, j, 0:128], w_uk[:, j, :],
                              start=True, stop=True)
                    mm = pe.matmul(s.bank[1][0:QC1, j * KVC:(j + 1) * KVC], w_uq[:, j, 128:QC], w_uk[:, j, :],
                                   start=True, stop=True)
                mm.then_inc(w_done, 1)
                for j in range(GH):
                    pe.matmul(s.bank[2 + j][:, :], w_uv[:, j, :], w_o[:, j, :], start=True, stop=True).then_inc(w_done, 1)
                for i in range(QR):
                    jj, half = i // 2, i % 2
                    pair = (6, 7) if i % 2 == 0 else (0, 1)
                    if i == 1:
                        pe.wait_ge(w_copied, g * W_COPIES + 2)
                    if i >= 2:
                        pe.wait_ge(qr_mul, g * 2 * QR + 2 * (i - 1))
                    for v in range(2):
                        out = s.bank[pair[v]][:, 0:HALF]
                        cols = slice(jj * 128, jj * 128 + 128)
                        toks = slice(half * HALF, (half + 1) * HALF)
                        pe.matmul(out, w_qr0[:, v, cols], a.qcT0[:, toks], start=True, stop=False)
                        mm = pe.matmul(out, w_qr1[:, v, cols], a.qcT1[:, toks], start=False, stop=True)
                    mm.then_inc(qr_done, 1)
                for i in range(2 * GH):
                    j, half = i // 2, i % 2
                    pe.wait_ge(w_copied, g * W_COPIES + 2 + i % 4 + 1 + (4 if i >= 4 else 0))
                    out = s.bank[2 + i % 4][:, 0:HALF]
                    toks = slice(half * HALF, (half + 1) * HALF)
                    pe.matmul(out, qk0[:, j, :], a.qcT0[:, toks], start=True, stop=False)
                    pe.matmul(out, qk1[:, j, :], a.qcT1[:, toks], start=False, stop=True).then_inc(w_done, 1)
                pe.wait_ge(w_copied, (g + 1) * W_COPIES)
                pe.wait_ge(qr_added, (g + 1) * QR)
                for n in range(N + 5):
                    if n < N:
                        scores(g, n)
                    if 2 <= n < N + 2:
                        turn(g, n - 2)
                    if n >= 3 + GH - 1 and (n - 3) % GH == GH - 1 and (n - 3) // GH < B:
                        mix(g, (n - 3) // GH)
                    if n >= 4 + GH - 1 and (n - 4) % GH == GH - 1 and (n - 4) // GH < B:
                        project(g, (n - 4) // GH)

        @block.scalar
        def _(act):
            act.sem_inc(pt_copied, 1)
            with act.Fori(0, NG) as g:
                act.wait_ge(w_done, g * (1 + 3 * GH) + 1)
                act.activation(qk0[:, :, :], s.bank[0][:, 0:GH * KVC].rearrange("p (h n) -> p h n", h=GH),
                               ACT.Copy).then_inc(w_copied, 1)
                act.activation(qk1[:, :, :], s.bank[1][0:QC1, 0:GH * KVC].rearrange("p (h n) -> p h n", h=GH),
                               ACT.Copy).then_inc(w_copied, 1)
                for j in range(GH):
                    act.wait_ge(w_done, g * (1 + 3 * GH) + 2 + j)
                    act.activation(vo[:, j, :], s.bank[2 + j][:, :], ACT.Copy).then_inc(w_copied, 1)
                for i in range(2 * GH):
                    act.wait_ge(w_done, g * (1 + 3 * GH) + 2 + GH + i)
                    act.activation(qT[:, i // 2, (i % 2) * HALF:(i % 2 + 1) * HALF], s.bank[2 + i % 4][:, 0:HALF],
                                   ACT.Copy).then_inc(w_copied, 1)
                for n in range(N + 3):
                    if n < N:
                        act.wait_ge(shift, g * N + n + 1)
                        act.activation(p[:, n % BUFS, :], p[:, n % BUFS, :], ACT.Exp,
                                       bias=low[:, n % BUFS:n % BUFS + 1], scale=SCALE0,
                                       accum_out=total[:, n % BUFS:n % BUFS + 1]).then_inc(e_done, 1)
                    if 1 <= n < N + 1:
                        m = n - 1
                        act.wait_ge(inv_done, g * N + m + 1)
                        act.activation(p[:, m % BUFS, :], p[:, m % BUFS, :], ACT.Copy,
                                       scale=inv[:, m % BUFS:m % BUFS + 1]).then_inc(p_done, 1)
                    if n >= 2 and n - 2 < N:
                        m = n - 2
                        b, j = m // GH, m % GH
                        act.wait_ge(pt_done, g * N + m + 1)
                        if b >= 2 and j == 0:
                            act.wait_ge(z_done, g * B + b - 1)
                        act.activation(pT[:, b % 2, :, j, :],
                                       s.bank[3 + m % 2][0:TT, 0:KT * TOK].rearrange("p (t n) -> p t n", t=KT),
                                       ACT.Copy).then_inc(pt_copied, 1)

        @block.vector
        def _(dve):
            dve.sem_inc(s_masked, 1)
            dve.sem_inc(z_copied, 1)
            dve.sem_inc(y_added, 1)
            with dve.Fori(0, NG) as g:
                for i in range(QR):
                    jj, half = i // 2, i % 2
                    pair = (6, 7) if i % 2 == 0 else (0, 1)
                    dve.wait_ge(qr_done, 1 + g * QR + i + 1)
                    for v, table in enumerate((a.cos, a.sin)):
                        dve.tensor_tensor(part[:, i % 2, v, :].rearrange("p (b t) -> p b t", t=TOK),
                                          s.bank[pair[v]][:, 0:HALF].rearrange("p (b t) -> p b t", t=TOK),
                                          table[:, 0:TOK].unsqueeze(1).to_broadcast([128, B // 2, TOK]),
                                          ALU.mult).then_inc(qr_mul, 1)
                    dve.wait_ge(qr_mul, g * 2 * QR + 2 * (i + 1))
                    dve.tensor_tensor(qrT[:, jj, half * HALF:(half + 1) * HALF], part[:, i % 2, 0, :],
                                      part[:, i % 2, 1, :], ALU.add).then_inc(qr_added, 1)
                for n in range(N + 6):
                    if n < N:
                        b = n // GH
                        dve.wait_ge(a.masked, 4 * B)
                        dve.wait_ge(s_done, g * N + n + 1)
                        if n == 0:
                            dve.memset(spare[:, :], 0.0)
                        if n >= BUFS:
                            dve.wait_ge(pt_done, g * N + n - BUFS + 1)
                        dve.tensor_tensor_reduce(out=p[:, n % BUFS, :], in0=s.bank[n % 3][0:TOK, 0:T],
                                                 in1=a.mask[:, b, :], scale=1.0, scalar=-3.0e38, op0=ALU.add,
                                                 op1=ALU.max, accum_out=top[:, n % BUFS:n % BUFS + 1]).then_inc(s_masked, 1)
                        dve.wait_ge(s_masked, 1 + g * N + n + 1)
                        dve.tensor_scalar(low[:, n % BUFS:n % BUFS + 1], top[:, n % BUFS:n % BUFS + 1], -SCALE0, None,
                                          ALU.mult).then_inc(shift, 1)
                    if 1 <= n < N + 1:
                        m = (n - 1) % BUFS
                        dve.wait_ge(e_done, g * N + n)
                        dve.reciprocal(inv[:, m:m + 1], total[:, m:m + 1]).then_inc(inv_done, 1)
                    if n >= 3 + GH - 1 and (n - 3) % GH == GH - 1 and (n - 3) // GH < B:
                        b = (n - 3) // GH
                        dve.wait_ge(z_done, g * B + b + 1)
                        if b >= 2:
                            dve.wait_ge(y_done, g * B + b - 1)
                        dve.tensor_copy(zT[:, b % 2, :, :], s.bank[5][:, 0:GH * TOK].rearrange("p (h n) -> p h n", h=GH))\
                           .then_inc(z_copied, 1)
                    if n >= 5 + GH - 1 and (n - 5) % GH == GH - 1 and (n - 5) // GH < B:
                        b = (n - 5) // GH
                        dve.wait_ge(y_done, g * B + b + 1)
                        dve.wait_ge(y_added, 1 + g * B + b)
                        dve.scalar_tensor_tensor(out=s.x[:, b, :], in0=s.bank[6 + b % 2][0:TOK, :],
                                                 scalar=s.tanh_g[0:TOK, 0:1], in1=s.x[:, b, :],
                                                 op0=ALU.mult, op1=ALU.add).then_inc(y_added, 1)


def heads_attention_stage(nc, s, d):
    N = B * GH
    BUFS = 4
    VB = 128
    with ExitStack() as ctx:
        def sb(n, shape, dt=F32):
            return ctx.enter_context(nc.sbuf_tensor(f"l1a_{n}", shape, dt))

        (const, loaded, k_done, k_copied, q_done, q_copied, v_done, v_copied, s_done, max_done, shift, e_done,
         inv_done, pt_done, pt_copied, z_done, z_scaled, zt_done, zt_copied, y_done, y_added) = s.sems("l1a", "const", "loaded", "k_done", "k_copied", "q_done", "q_copied", "v_done", "v_copied",
            "s_done", "max_done", "shift", "e_done", "inv_done", "pt_done", "pt_copied", "z_done", "z_scaled",
            "zt_done", "zt_copied", "y_done", "y_added")
        w_q = sb("w_q", [128, KD, VB])
        w_k = sb("w_k", [128, KD, VB])
        w_v = sb("w_v", [128, KD, VB])
        w_o = sb("w_o", [128, D])
        b_q = sb("b_q", [128, NG])
        b_k = sb("b_k", [128, NG])
        b_now = sb("b_now", [128, 2])
        b_ready = s.sems("l1a", "b_ready")[0]
        b_v = sb("b_v", [TT, D])
        b_o = sb("b_o", [TOK, D])
        kT = sb("kT", [128, B * T])
        v = sb("v", [TT, B * KT, VB])
        qT = sb("qT", [128, NT])
        p = sb("p", [TOK, BUFS, T])
        top = sb("top", [TOK, BUFS])
        low = sb("low", [TOK, BUFS])
        total = sb("total", [TOK, 2, GH])
        inv = sb("inv", [TOK, 2, GH])
        pT = sb("pT", [TT, 2, KT, GH, TOK])
        z = sb("z", [TOK, 2, VB])
        zT = sb("zT", [VB, 2, TOK])
        block = ctx.enter_context(nc.Block())
        VT = B * KT // 4

        @block.sync
        def _(sp):
            sp.dma_start(b_q[:, :], d["l1_b_q"]).then_inc(const, 16)
            sp.dma_start(b_k[:, :], d["l1_b_k"]).then_inc(const, 16)
            sp.dma_start(b_v[:, :], d["l1_b_v"].partition_broadcast(TT)).then_inc(const, 16)
            sp.dma_start(b_o[:, :], d["l1_b_o"].partition_broadcast(TOK)).then_inc(const, 16)
            with sp.Fori(0, NG) as g:
                sp.wait_ge(y_done, g * B + 1)
                one = bass.ds(g, 1)
                for dst, src in ((w_q, "l1_w_qT"), (w_k, "l1_w_kT"), (w_v, "l1_w_vT")):
                    sp.dma_start(dst[:, :, :], d[src][one].rearrange("o p k n -> p (o k) n")).then_inc(loaded, 16)
                sp.dma_start(w_o[:, :], d["l1_w_oT"][one].rearrange("o p n -> p (o n)")).then_inc(loaded, 16)

        @block.tensor
        def _(pe):
            pe.sem_inc(y_done, 1)

            def scores(g, n):
                b, r = n // GH, HD1 * (n % GH)
                if n >= 3:
                    pe.wait_ge(e_done, g * N + n - 2)
                pe.matmul(s.bank[n % 3][0:TOK, 0:T], qT[r:r + HD1, b * TOK:(b + 1) * TOK],
                          kT[r:r + HD1, b * T:(b + 1) * T], start=True, stop=True).then_inc(s_done, 1)

            def turn(g, n):
                pe.wait_ge(e_done, g * N + n + 1)
                if n >= 2:
                    pe.wait_ge(pt_copied, 1 + g * N + n - 1)
                for t in range(KT):
                    mm = pe.transpose(s.bank[3 + n % 2][0:TT, t * TOK:(t + 1) * TOK],
                                      p[:, n % BUFS, t * TT:(t + 1) * TT], s.ident[0:TOK, 0:TOK])
                mm.then_inc(pt_done, 1)

            def mix(g, b):
                pe.wait_ge(pt_copied, 1 + g * N + (b + 1) * GH)
                if b:
                    pe.wait_ge(zt_copied, 1 + g * B + b)
                for j in range(GH):
                    for t in range(KT):
                        mm = pe.matmul(s.bank[5][0:TOK, j * HD1:(j + 1) * HD1], pT[:, b % 2, t, j, :],
                                       v[:, b * KT + t, j * HD1:(j + 1) * HD1], start=(t == 0), stop=(t == KT - 1))
                mm.then_inc(z_done, 1)

            def turn_mix(g, b):
                pe.wait_ge(z_scaled, 1 + g * B + b + 1)
                pe.transpose(s.bank[5][:, 256:256 + TOK], z[:, b % 2, :], s.ident[0:TOK, 0:TOK]).then_inc(zt_done, 1)

            def project(g, b):
                pe.wait_ge(zt_copied, 1 + g * B + b + 1)
                if b >= 2:
                    pe.wait_ge(y_added, 1 + g * B + b - 1)
                pe.matmul(s.bank[6 + b % 2][0:TOK, :], zT[:, b % 2, :], w_o[:, :], start=True, stop=True)\
                  .then_inc(y_done, 1)

            with pe.Fori(0, NG) as g:
                pe.wait_ge(loaded, (g + 1) * 64)
                pe.wait_ge(y_added, 1 + g * B)
                for h in range(2):
                    for k in range(KD):
                        mm = pe.matmul(s.bank[h][:, 0:HALF], w_q[:, k, :], s.xnT[:, k, h * HALF:(h + 1) * HALF],
                                       start=(k == 0), stop=(k == KD - 1))
                    mm.then_inc(q_done, 1)
                for b in range(B):
                    if b >= 2:
                        pe.wait_ge(k_copied, g * B + b - 1)
                    for k in range(KD):
                        mm = pe.matmul(s.bank[2 + b % 2][:, 0:T], w_k[:, k, :], s.ctxT[:, k, b * T:(b + 1) * T],
                                       start=(k == 0), stop=(k == KD - 1))
                    mm.then_inc(k_done, 1)
                for c in range(VT):
                    if c >= 2:
                        pe.wait_ge(v_copied, g * VT + c - 1)
                    for i in range(4):
                        r0 = (c * 4 + i) * TT
                        for k in range(KD):
                            mm = pe.matmul(s.bank[4 + c % 2][0:TT, i * VB:(i + 1) * VB], s.ctxT[:, k, r0:r0 + TT],
                                           w_v[:, k, :], start=(k == 0), stop=(k == KD - 1))
                    mm.then_inc(v_done, 1)
                pe.wait_ge(q_copied, 2 * (g + 1))
                pe.wait_ge(k_copied, B * (g + 1))
                pe.wait_ge(v_copied, VT * (g + 1))
                for n in range(N + 6):
                    if n < N:
                        scores(g, n)
                    if 2 <= n < N + 2:
                        turn(g, n - 2)
                    for lag, step in ((3, mix), (4, turn_mix), (5, project)):
                        if n >= lag + GH - 1 and (n - lag) % GH == GH - 1 and (n - lag) // GH < B:
                            step(g, (n - lag) // GH)

        @block.scalar
        def _(act):
            act.wait_ge(const, 64)
            act.sem_inc(pt_copied, 1)
            act.sem_inc(zt_copied, 1)
            with act.Fori(0, NG) as g:
                act.copy(b_now[:, 0:1], b_q[:, bass.ds(g, 1)]).then_inc(b_ready, 1)
                act.copy(b_now[:, 1:2], b_k[:, bass.ds(g, 1)]).then_inc(b_ready, 1)
                act.wait_ge(b_ready, 2 * (g + 1))
                for h in range(2):
                    act.wait_ge(q_done, 2 * g + h + 1)
                    act.activation(qT[:, h * HALF:(h + 1) * HALF], s.bank[h][:, 0:HALF], ACT.Identity,
                                   bias=b_now[:, 0:1]).then_inc(q_copied, 1)
                for b in range(B):
                    act.wait_ge(k_done, g * B + b + 1)
                    act.activation(kT[:, b * T:(b + 1) * T], s.bank[2 + b % 2][:, 0:T], ACT.Identity,
                                   bias=b_now[:, 1:2]).then_inc(k_copied, 1)
                for n in range(N + 5):
                    if n < N:
                        b, j = n // GH, n % GH
                        act.wait_ge(shift, g * N + n + 1)
                        if n >= BUFS:
                            act.wait_ge(pt_done, g * N + n - BUFS + 1)
                        if j == 0 and b >= 2:
                            act.wait_ge(inv_done, g * B + b - 1)
                        act.activation(p[:, n % BUFS, :], s.bank[n % 3][0:TOK, 0:T], ACT.Exp,
                                       bias=low[:, n % BUFS:n % BUFS + 1], scale=SCALE1,
                                       accum_out=total[:, b % 2, j:j + 1]).then_inc(e_done, 1)
                    if n >= 2 and n - 2 < N:
                        m = n - 2
                        b, j = m // GH, m % GH
                        act.wait_ge(pt_done, g * N + m + 1)
                        if b >= 2 and j == 0:
                            act.wait_ge(z_done, g * B + b - 1)
                        act.activation(pT[:, b % 2, :, j, :],
                                       s.bank[3 + m % 2][0:TT, 0:KT * TOK].rearrange("p (t n) -> p t n", t=KT),
                                       ACT.Copy).then_inc(pt_copied, 1)
                    if n >= 4 + GH - 1 and (n - 4) % GH == GH - 1 and (n - 4) // GH < B:
                        b = (n - 4) // GH
                        act.wait_ge(zt_done, g * B + b + 1)
                        if b >= 2:
                            act.wait_ge(y_done, 1 + g * B + b - 1)
                        act.activation(zT[:, b % 2, :], s.bank[5][:, 256:256 + TOK], ACT.Copy).then_inc(zt_copied, 1)

        @block.vector
        def _(dve):
            dve.wait_ge(const, 64)
            dve.sem_inc(z_scaled, 1)
            dve.sem_inc(y_added, 1)
            for b in range(B):
                op = dve.scalar_tensor_tensor(out=s.x[:, b, :], in0=b_o[:, :], scalar=s.tanh_g[0:TOK, 1:2],
                                              in1=s.x[:, b, :], op0=ALU.mult, op1=ALU.add)
            op.then_inc(const, 1)
            dve.wait_ge(const, 65)
            with dve.Fori(0, NG) as g:
                for c in range(VT):
                    dve.wait_ge(v_done, g * VT + c + 1)
                    dve.tensor_tensor(v[:, c * 4:(c + 1) * 4, :],
                                      s.bank[4 + c % 2][0:TT, :].rearrange("p (i n) -> p i n", i=4),
                                      b_v[:, bass.ds(g * VB, VB)].unsqueeze(1).to_broadcast([TT, 4, VB]),
                                      ALU.add).then_inc(v_copied, 1)
                for n in range(N + 7):
                    if n < N:
                        dve.wait_ge(s_done, g * N + n + 1)
                        if n >= BUFS:
                            dve.wait_ge(e_done, g * N + n - BUFS + 1)
                        dve.tensor_reduce(top[:, n % BUFS:n % BUFS + 1], s.bank[n % 3][0:TOK, 0:T], AX_X, ALU.max)\
                           .then_inc(max_done, 1)
                        dve.wait_ge(max_done, g * N + n + 1)
                        dve.tensor_scalar(low[:, n % BUFS:n % BUFS + 1], top[:, n % BUFS:n % BUFS + 1], -SCALE1, None,
                                          ALU.mult).then_inc(shift, 1)
                    if n >= 3 + GH - 1 and (n - 3) % GH == GH - 1 and (n - 3) // GH < B:
                        b = (n - 3) // GH
                        dve.wait_ge(e_done, g * N + (b + 1) * GH)
                        dve.reciprocal(inv[:, b % 2, :], total[:, b % 2, :]).then_inc(inv_done, 1)
                        dve.wait_ge(inv_done, g * B + b + 1)
                        dve.wait_ge(z_done, g * B + b + 1)
                        if b >= 2:
                            dve.wait_ge(zt_done, g * B + b - 1)
                        dve.tensor_tensor(z[:, b % 2, :].rearrange("p (h n) -> p h n", h=GH),
                                          s.bank[5][0:TOK, 0:VB].rearrange("p (h n) -> p h n", h=GH),
                                          inv[:, b % 2, :].unsqueeze(2).to_broadcast([TOK, GH, HD1]),
                                          ALU.mult).then_inc(z_scaled, 1)
                    if n >= 6 + GH - 1 and (n - 6) % GH == GH - 1 and (n - 6) // GH < B:
                        b = (n - 6) // GH
                        dve.wait_ge(y_done, 1 + g * B + b + 1)
                        dve.wait_ge(y_added, 1 + g * B + b)
                        dve.scalar_tensor_tensor(out=s.x[:, b, :], in0=s.bank[6 + b % 2][0:TOK, :],
                                                 scalar=s.tanh_g[0:TOK, 1:2], in1=s.x[:, b, :],
                                                 op0=ALU.mult, op1=ALU.add).then_inc(y_added, 1)


def recurrence_stage(nc, s, d):
    with ExitStack() as ctx:
        def sb(n, shape, dt=F32):
            return ctx.enter_context(nc.sbuf_tensor(f"l2a_{n}", shape, dt))

        (loaded, step, decay_e, sums_done, state_done, state_copied, spread, y_done, y_added, stats_done, mv_done,
         sd_done, rstd_done, normed, scaled, shifted) = s.sems("l2a", "loaded", "step", "decay_e", "sums_done", "state_done", "state_copied", "spread", "y_done",
            "y_added", "stats_done", "mv_done", "sd_done", "rstd_done", "normed", "scaled", "shifted")
        decay = sb("decay", [128, 1])
        decay_exp = sb("decay_exp", [128, 1])
        keep = sb("keep", [128, 1])
        keeps = sb("keeps", [128, T])
        ones = sb("ones", [128, T])
        coef = sb("coef", [128, T])
        coef_sum = sb("coef_sum", [128, 1])
        weighted = sb("weighted", [128, 2, T])
        sums = sb("sums", [128, KD, B])
        w_in = sb("w_in", [128, KD, D])
        w_out = sb("w_out", [128, KD, D])
        b_in = sb("b_in", [128, KD])
        b_in_sum = sb("b_in_sum", [128, KD])
        b_out = sb("b_out", [TOK, D])
        gamma = sb("gamma", [TOK, D])
        beta = sb("beta", [TOK, D])
        state = sb("state", [128, KD, B])
        wide = sb("wide", [128, B, KD, TOK])
        block = ctx.enter_context(nc.Block())

        @block.sync
        def _(sp):
            sp.dma_start(decay[:, :], d["l2_decay"].partition_broadcast(128)).then_inc(loaded, 16)
            sp.dma_start(w_in[:, :, :], d["l2_w_inT"].rearrange("(k p) n -> p k n", p=128)).then_inc(loaded, 16)
            sp.dma_start(w_out[:, :, :], d["l2_w_outT"].rearrange("(k p) n -> p k n", p=128)).then_inc(loaded, 16)
            sp.dma_start(b_in[:, :], d["l2_b_in"]).then_inc(loaded, 16)
            sp.dma_start(b_out[:, :], d["l2_b_out"].partition_broadcast(TOK)).then_inc(loaded, 16)
            sp.dma_start(gamma[:, :], d["l2_gamma"].partition_broadcast(TOK)).then_inc(loaded, 16)
            sp.dma_start(beta[:, :], d["l2_beta"].partition_broadcast(TOK)).then_inc(loaded, 16)

        LOADED = 7 * 16

        @block.scalar
        def _(act):
            act.wait_ge(loaded, LOADED)
            act.activation(decay_exp[:, :], decay[:, :], ACT.Exp, scale=-1.0).then_inc(decay_e, 1)
            act.wait_ge(mv_done, B)
            act.activation(s.sd[:, :], s.mv[:, :, 1], ACT.Sqrt, bias=s.eps[0:TOK, :]).then_inc(sd_done, 1)

        @block.tensor
        def _(pe):
            pe.wait_ge(loaded, LOADED)
            pe.wait_ge(sums_done, KD * B)
            for m in range(KD):
                for k in range(KD):
                    mm = pe.matmul(s.bank[0][:, m * B:(m + 1) * B], w_in[:, k, m * 128:(m + 1) * 128], sums[:, k, :],
                                   start=(k == 0), stop=(k == KD - 1))
            mm.then_inc(state_done, 1)
            for b in range(B):
                pe.wait_ge(spread, b + 1)
                if b >= 4:
                    pe.wait_ge(y_added, 2 * (b - 3))
                for k in range(KD):
                    mm = pe.matmul(s.bank[1 + b % 4][0:TOK, :], wide[:, b, k, :], w_out[:, k, :],
                                   start=(k == 0), stop=(k == KD - 1))
                mm.then_inc(y_done, 1)

        @block.vector
        def _(dve):
            chain = [0]

            def then(instruction):
                chain[0] += 1
                instruction.then_inc(step, 1)
                dve.wait_ge(step, chain[0])

            dve.wait_ge(loaded, LOADED)
            then(dve.memset(ones[:, :], 1.0))
            dve.wait_ge(decay_e, 1)
            then(dve.tensor_scalar(keep[:, :], decay_exp[:, :], 1.0, None, ALU.add))
            then(dve.reciprocal(keep[:, :], keep[:, :]))
            then(dve.tensor_scalar(keeps[:, :], ones[:, :], keep[:, :], None, ALU.mult))
            then(dve.tensor_tensor_scan(coef[:, ::-1], keeps[:, :], ones[:, :], 0.0, ALU.mult, ALU.add))
            then(dve.tensor_reduce(coef_sum[:, :], coef[:, :], AX_X, ALU.add))
            then(dve.tensor_scalar(b_in_sum[:, :], b_in[:, :], coef_sum[:, :], None, ALU.mult))
            for i in range(KD * B):
                k, b = i // B, i % B
                if i >= 2:
                    dve.wait_ge(sums_done, i - 1)
                dve.tensor_tensor_reduce(out=weighted[:, i % 2, :], in0=s.ctxT[:, k, b * T:(b + 1) * T],
                                         in1=coef[:, :], scale=1.0, scalar=0.0, op0=ALU.mult, op1=ALU.add,
                                         accum_out=sums[:, k, b:b + 1]).then_inc(sums_done, 1)
            dve.wait_ge(state_done, 1)
            for m in range(KD):
                dve.tensor_scalar(state[:, m, :], s.bank[0][:, m * B:(m + 1) * B], b_in_sum[:, m:m + 1], 1.0 / T,
                                  ALU.add, ALU.mult).then_inc(state_copied, 1)
            dve.wait_ge(state_copied, KD)
            for b in range(B):
                dve.tensor_copy(wide[:, b, :, :], state[:, :, b:b + 1].to_broadcast([128, KD, TOK])).then_inc(spread, 1)
            for b in range(B):
                dve.wait_ge(y_done, b + 1)
                dve.tensor_tensor(s.xn[:, b, :], s.xn[:, b, :], s.bank[1 + b % 4][0:TOK, :], ALU.add).then_inc(y_added, 1)
                dve.wait_ge(y_added, 2 * b + 1)
                dve.tensor_tensor(s.xn[:, b, :], s.xn[:, b, :], b_out[:, :], ALU.add).then_inc(y_added, 1)
                dve.wait_ge(y_added, 2 * b + 2)
                dve.bn_stats(s.stats[:, b, :], s.xn[:, b, :]).then_inc(stats_done, 1)
            for b in range(B):
                dve.wait_ge(stats_done, b + 1)
                dve.bn_aggr(s.mv[:, b, :], s.stats[:, b, :]).then_inc(mv_done, 1)
            dve.wait_ge(sd_done, 1)
            dve.reciprocal(s.rstd[:, :], s.sd[:, :]).then_inc(rstd_done, 1)
            dve.wait_ge(rstd_done, 1)
            for b in range(B):
                dve.tensor_scalar(s.xn[:, b, :], s.xn[:, b, :], s.mv[:, b, 0:1], s.rstd[:, b:b + 1],
                                  ALU.subtract, ALU.mult).then_inc(normed, 1)
            for b in range(B):
                dve.wait_ge(normed, b + 1)
                dve.tensor_tensor(s.xn[:, b, :], s.xn[:, b, :], gamma[:, :], ALU.mult).then_inc(scaled, 1)
            for b in range(B):
                dve.wait_ge(scaled, b + 1)
                dve.tensor_tensor(s.xn[:, b, :], s.xn[:, b, :], beta[:, :], ALU.add).then_inc(shifted, 1)
            for b in range(B):
                dve.wait_ge(shifted, b + 1)
                dve.scalar_tensor_tensor(out=s.x[:, b, :], in0=s.xn[:, b, :], scalar=s.tanh_g[0:TOK, 2:3],
                                         in1=s.x[:, b, :], op0=ALU.mult, op1=ALU.add)


def cache_attention_stage(nc, s, d):
    with ExitStack() as ctx:
        def sb(n, shape, dt=F32):
            return ctx.enter_context(nc.sbuf_tensor(f"l3a_{n}", shape, dt))

        (loaded, v_loaded0, v_loaded1, qk_done, qk_copied, vn_done, vn_copied, s_done, max_done, shift, e_done,
         inv_done, pt_done, pt_copied, z_done, z_scaled, zt_done, zt_copied, y_done, y_added) = s.sems("l3a", "loaded", "v_loaded0", "v_loaded1", "qk_done", "qk_copied", "vn_done", "vn_copied",
            "s_done", "max_done", "shift", "e_done", "inv_done", "pt_done", "pt_copied", "z_done", "z_scaled",
            "zt_done", "zt_copied", "y_done", "y_added")
        ALL = T + TOK
        w = [sb(f"w{i}", [128, KD, D]) for i in range(4)]
        w_q, w_k, w_v, w_o = w
        qkT = [sb("qT", [128, KD, NT]), sb("kT", [128, KD, NT])]
        vn = sb("vn", [TOK, B, D])
        vc = sb("vc", [TT, 2, KT, D])
        p = sb("p", [TOK, 2, ALL])
        top = sb("top", [TOK, 2])
        low = sb("low", [TOK, 2])
        total = sb("total", [TOK, 2])
        inv = sb("inv", [TOK, 2])
        pT = sb("pT", [TT, 2, KT + 1, TOK])
        z = sb("z", [TOK, 2, D])
        zT = sb("zT", [128, 2, KD, TOK])
        v_loaded = (v_loaded0, v_loaded1)
        QK = 2 * KD * 2
        block = ctx.enter_context(nc.Block())

        @block.sync
        def _(sp):
            for dst, src in zip(w, ("l3_w_qT", "l3_w_kT", "l3_w_vT", "l3_w_oT")):
                sp.dma_start(dst[:, :, :], d[src].rearrange("(k p) n -> p k n", p=128)).then_inc(loaded, 16)
            for b in range(B):
                if b >= 2:
                    sp.wait_ge(z_done, b - 1)
                sp.dma_start(vc[:, b % 2, :, :], d["ctx"][b].rearrange("(t p) n -> p t n", p=TT)).then_inc(v_loaded[b % 2], 16)

        @block.tensor
        def _(pe):
            pe.wait_ge(loaded, 64)
            for i in range(QK):
                m, h = (i // 2) % KD, i % 2
                if i >= 4:
                    pe.wait_ge(qk_copied, i - 3)
                for k in range(KD):
                    mm = pe.matmul(s.bank[i % 4][:, 0:HALF], w[i // (2 * KD)][:, k, m * 128:(m + 1) * 128],
                                   s.xnT[:, k, h * HALF:(h + 1) * HALF], start=(k == 0), stop=(k == KD - 1))
                mm.then_inc(qk_done, 1)
            for b in range(B):
                if b >= 4:
                    pe.wait_ge(vn_copied, b - 3)
                for k in range(KD):
                    mm = pe.matmul(s.bank[4 + b % 4][0:TOK, :], s.xnT[:, k, b * TOK:(b + 1) * TOK], w_v[:, k, :],
                                   start=(k == 0), stop=(k == KD - 1))
                mm.then_inc(vn_done, 1)

            def scores(b):
                if b >= 2:
                    pe.wait_ge(e_done, b - 1)
                toks = slice(b * TOK, (b + 1) * TOK)
                for k in range(KD):
                    pe.matmul(s.bank[b % 2][0:TOK, 0:T], qkT[0][:, k, toks], s.ctxT[:, k, b * T:(b + 1) * T],
                              start=(k == 0), stop=(k == KD - 1))
                for k in range(KD):
                    mm = pe.matmul(s.bank[b % 2][0:TOK, T:ALL], qkT[0][:, k, toks], qkT[1][:, k, toks],
                                   start=(k == 0), stop=(k == KD - 1))
                mm.then_inc(s_done, 1)

            def turn(b):
                pe.wait_ge(e_done, b + 1)
                if b >= 2:
                    pe.wait_ge(pt_copied, 2 * (b - 1))
                for t in range(KT + 1):
                    rows = TT if t < KT else TOK
                    mm = pe.transpose(s.bank[2 + b % 2][0:rows, t * TOK:(t + 1) * TOK],
                                      p[:, b % 2, t * TT:t * TT + rows], s.ident[0:TOK, 0:TOK])
                mm.then_inc(pt_done, 1)

            def mix(b):
                pe.wait_ge(pt_copied, 2 * (b + 1))
                pe.wait_ge(v_loaded[b % 2], 16 * (b // 2 + 1))
                if b >= 2:
                    pe.wait_ge(z_scaled, b - 1)
                for t in range(KT):
                    pe.matmul(s.bank[4 + b % 2][0:TOK, :], pT[:, b % 2, t, :], vc[:, b % 2, t, :],
                              start=(t == 0), stop=False)
                pe.matmul(s.bank[4 + b % 2][0:TOK, :], pT[0:TOK, b % 2, KT, :], vn[:, b, :],
                          start=False, stop=True).then_inc(z_done, 1)

            def turn_mix(b):
                pe.wait_ge(z_scaled, b + 1)
                if b:
                    pe.wait_ge(zt_copied, b)
                for k in range(KD):
                    mm = pe.transpose(s.bank[6][:, k * TOK:(k + 1) * TOK], z[:, b % 2, k * 128:(k + 1) * 128],
                                      s.ident[0:TOK, 0:TOK])
                mm.then_inc(zt_done, 1)

            def project(b):
                pe.wait_ge(zt_copied, b + 1)
                if b:
                    pe.wait_ge(y_added, b)
                for k in range(KD):
                    mm = pe.matmul(s.bank[7][0:TOK, :], zT[:, b % 2, k, :], w_o[:, k, :],
                                   start=(k == 0), stop=(k == KD - 1))
                mm.then_inc(y_done, 1)

            pe.wait_ge(qk_copied, QK)
            pe.wait_ge(vn_copied, B)
            for n in range(B + 4):
                for lag, step in enumerate((scores, turn, mix, turn_mix, project)):
                    if 0 <= n - lag < B:
                        step(n - lag)

        @block.scalar
        def _(act):
            for i in range(QK):
                act.wait_ge(qk_done, i + 1)
                m, h = (i // 2) % KD, i % 2
                act.activation(qkT[i // (2 * KD)][:, m, h * HALF:(h + 1) * HALF], s.bank[i % 4][:, 0:HALF],
                               ACT.Copy).then_inc(qk_copied, 1)
            for n in range(B + 3):
                if n < B:
                    act.wait_ge(shift, n + 1)
                    if n >= 2:
                        act.wait_ge(pt_done, n - 1)
                        act.wait_ge(inv_done, n - 1)
                    act.activation(p[:, n % 2, :], s.bank[n % 2][0:TOK, 0:ALL], ACT.Exp, bias=low[:, n % 2:n % 2 + 1],
                                   scale=SCALE3, accum_out=total[:, n % 2:n % 2 + 1]).then_inc(e_done, 1)
                if 0 <= n - 1 < B:
                    b = n - 1
                    act.wait_ge(pt_done, b + 1)
                    if b >= 2:
                        act.wait_ge(z_done, b - 1)
                    act.activation(pT[:, b % 2, 0:KT, :],
                                   s.bank[2 + b % 2][0:TT, 0:KT * TOK].rearrange("p (t n) -> p t n", t=KT),
                                   ACT.Copy).then_inc(pt_copied, 1)
                    act.activation(pT[0:TOK, b % 2, KT, :], s.bank[2 + b % 2][0:TOK, KT * TOK:(KT + 1) * TOK],
                                   ACT.Copy).then_inc(pt_copied, 1)
                if 0 <= n - 3 < B:
                    b = n - 3
                    act.wait_ge(zt_done, b + 1)
                    if b >= 2:
                        act.wait_ge(y_done, b - 1)
                    act.activation(zT[:, b % 2, :, :], s.bank[6][:, 0:KD * TOK].rearrange("p (k n) -> p k n", k=KD),
                                   ACT.Copy).then_inc(zt_copied, 1)

        @block.vector
        def _(dve):
            for b in range(B):
                dve.wait_ge(vn_done, b + 1)
                dve.tensor_copy(vn[:, b, :], s.bank[4 + b % 4][0:TOK, :]).then_inc(vn_copied, 1)
            for n in range(B + 5):
                if n < B:
                    m = slice(n % 2, n % 2 + 1)
                    dve.wait_ge(s_done, n + 1)
                    if n >= 2:
                        dve.wait_ge(e_done, n - 1)
                    dve.tensor_reduce(top[:, m], s.bank[n % 2][0:TOK, 0:ALL], AX_X, ALU.max).then_inc(max_done, 1)
                    dve.wait_ge(max_done, n + 1)
                    dve.tensor_scalar(low[:, m], top[:, m], -SCALE3, None, ALU.mult).then_inc(shift, 1)
                if 0 <= n - 2 < B:
                    b = n - 2
                    dve.wait_ge(e_done, b + 1)
                    dve.reciprocal(inv[:, b % 2:b % 2 + 1], total[:, b % 2:b % 2 + 1]).then_inc(inv_done, 1)
                    dve.wait_ge(inv_done, b + 1)
                    dve.wait_ge(z_done, b + 1)
                    if b >= 2:
                        dve.wait_ge(zt_done, b - 1)
                    dve.tensor_scalar(z[:, b % 2, :], s.bank[4 + b % 2][0:TOK, :], inv[:, b % 2:b % 2 + 1], None,
                                      ALU.mult).then_inc(z_scaled, 1)
                if 0 <= n - 4 < B:
                    b = n - 4
                    dve.wait_ge(y_done, b + 1)
                    dve.scalar_tensor_tensor(out=s.x[:, b, :], in0=s.bank[7][0:TOK, :], scalar=s.tanh_g[0:TOK, 3:4],
                                             in1=s.x[:, b, :], op0=ALU.mult, op1=ALU.add).then_inc(y_added, 1)


def ternary_stage(nc, s, d, t):
    units, width = 4, 352
    whole, rest = width // 128, width % 128
    matrices = (t.wg, t.wu, t.wd)
    count = float(L3_HIDDEN * D)
    with ExitStack() as ctx:
        def sb(n, shape, dt=F32):
            return ctx.enter_context(nc.sbuf_tensor(f"l3t_{n}", shape, dt))

        zeroed, loaded, sized, summed, scaled, sum_done, low_done, turned = s.sems("l3t", "zeroed", "loaded", "sized", "summed", "scaled", "sum_done", "low_done", "turned")
        size = sb("size", [128, 2, (whole + 1) * D])
        part = sb("part", [128, 3, units])
        total = sb("total", [128, 3])
        below = sb("below", [128, 2, (whole + 1) * D])
        block = ctx.enter_context(nc.Block())

        @block.gpsimd
        def _(pool):
            for u in range(units):
                op = pool.memset(t.wd[u][rest:128, whole, :], 0.0)
            op.then_inc(zeroed, 1)

        @block.sync
        def _(sp):
            for u in range(units):
                sp.dma_start(t.wg[u][:, :, :], d["l3_w_1T"][u].rearrange("(k p) f -> p k f", p=128)).then_inc(loaded, 16)
            for u in range(units):
                sp.dma_start(t.wu[u][:, :, :], d["l3_w_3T"][u].rearrange("(k p) f -> p k f", p=128)).then_inc(loaded, 16)
            for u in range(units):
                sp.dma_start(t.wd[u][:, 0:whole, :],
                             d["l3_w_2T"][u, 0:whole * 128].rearrange("(c p) f -> p c f", p=128)).then_inc(loaded, 16)
                sp.dma_start(t.wd[u][0:rest, whole, :], d["l3_w_2T"][u, whole * 128:width]).then_inc(loaded, 16)

        @block.scalar
        def _(act):
            act.wait_ge(loaded, 16 * units * 4)
            act.wait_ge(zeroed, 1)
            for i in range(3 * units):
                m, u = i // units, i % units
                w = matrices[m][u]
                n = w.shape[1] * w.shape[2]
                if i >= 2:
                    act.wait_ge(sized, i - 1)
                act.activation(size[:, i % 2, 0:n], w[:, :, :].rearrange("p a b -> p (a b)"), ACT.Abs,
                               accum_out=part[:, m, u:u + 1]).then_inc(sized, 1)

        @block.tensor
        def _(pe):
            pe.wait_ge(summed, 1)
            pe.matmul(s.bank[0][:, 0:3], s.ones[:, :], total[:, :], start=True, stop=True).then_inc(sum_done, 1)

        @block.vector
        def _(dve):
            dve.wait_ge(sized, 3 * units)
            dve.tensor_reduce(total[:, :], part[:, :, :], AX_X, ALU.add).then_inc(summed, 1)
            dve.wait_ge(sum_done, 1)
            dve.tensor_scalar(t.scale[:, :], s.bank[0][:, 0:3], 1.0 / count, None, ALU.mult).then_inc(scaled, 1)
            dve.wait_ge(scaled, 1)
            for i, sign in enumerate((0.5, -0.5)):
                dve.tensor_scalar(t.half[:, 3 * i:3 * i + 3], t.scale[:, :], sign, None, ALU.mult).then_inc(scaled, 1)
            dve.wait_ge(scaled, 3)
            dve.tensor_scalar(s.gates[:, 0:units, :], s.ones[0:TOK, 0:units * B].rearrange("p (u b) -> p u b", u=units),
                              t.scale[0:TOK, 2:3], s.tanh_g[0:TOK, 7:8], ALU.mult, ALU.mult)
            for i in range(3 * units):
                m, u = i // units, i % units
                w = matrices[m][u][:, :, :].rearrange("p a b -> p (a b)")
                n = w.shape[1]
                if i >= 2:
                    dve.wait_ge(turned, i - 1)
                dve.tensor_scalar(below[:, i % 2, 0:n], w, t.half[:, 3 + m:4 + m], None, ALU.is_lt).then_inc(low_done, 1)
                dve.wait_ge(low_done, i + 1)
                dve.scalar_tensor_tensor(out=w, in0=w, scalar=t.half[:, m:m + 1], in1=below[:, i % 2, 0:n],
                                         op0=ALU.is_gt, op1=ALU.subtract).then_inc(turned, 1)


def store_stage(nc, s, out):
    with ExitStack() as ctx:
        (stored,) = s.sems("store", "stored")
        block = ctx.enter_context(nc.Block())

        @block.sync
        def _(sp):
            sp.dma_start(out.rearrange("b p d -> p b d"), s.x[:, :, :]).then_inc(stored, 16)
            sp.wait_ge(stored, 16)


class Latent:

    def __init__(self, nc, ctx, s):
        def sb(name, shape):
            return ctx.enter_context(nc.sbuf_tensor(f"l0_{name}", shape, F32))

        self.kvcT = sb("kvcT", [KVC, B * T])
        self.kvc = sb("kvc", [TT, B * KT, KVC])
        self.krT = sb("krT", [128, B * T])
        self.qcT0 = sb("qcT0", [128, NT])
        self.qcT1 = sb("qcT1", [QC1, NT])
        self.mask = s.xn[:, :, :].rearrange("p b d -> p (b d)")[:, 0:B * T].rearrange("p (b t) -> p b t", b=B)
        self.masked = s.sems("l0", "masked")[0]
        self.cos = sb("cos", [128, T])
        self.sin = sb("sin", [128, T])


class Ternary:

    def __init__(self, nc, ctx):
        def sb(name, shape):
            return ctx.enter_context(nc.sbuf_tensor(f"l3_{name}", shape, F32))

        self.wg = [sb(f"wg{u}", [128, KD, 352]) for u in range(4)]
        self.wu = [sb(f"wu{u}", [128, KD, 352]) for u in range(4)]
        self.wd = [sb(f"wd{u}", [128, 3, D]) for u in range(4)]
        self.scale = sb("scale", [128, 3])
        self.half = sb("half", [128, 6])


def build(nc, d, out, parts=range(8)):
    with ExitStack() as ctx:
        s = Chip(nc, ctx)
        setup_stage(nc, s, d)
        if 0 in parts:
            layernorm_stage(nc, s, "ln0")
            with ExitStack() as own:
                a = Latent(nc, own, s)
                latent_project_stage(nc, s, d, a)
                latent_attention_stage(nc, s, d, a)
        if 1 in parts:
            layernorm_stage(nc, s, "ln1")
            routed_ffn(nc, s, d, 0, 2, 256, ACT.Gelu, softmax=False, eps=0.0)
        if 2 in parts:
            s.clear_semaphores()
            layernorm_stage(nc, s, "ln2")
            heads_attention_stage(nc, s, d)
        if 3 in parts:
            layernorm_stage(nc, s, "ln3")
            routed_ffn(nc, s, d, 1, 4, 352, ACT.Silu, softmax=True, eps=1e-20, capacity=CAP)
        if 4 in parts:
            s.clear_semaphores()
            layernorm_stage(nc, s, "ln4")
            recurrence_stage(nc, s, d)
        if 5 in parts:
            layernorm_stage(nc, s, "ln5")
            routed_ffn(nc, s, d, 2, 6, 352, ACT.Silu, softmax=True, eps=1e-20)
        if 6 in parts:
            s.clear_semaphores()
            layernorm_stage(nc, s, "ln6")
            cache_attention_stage(nc, s, d)
        if 7 in parts:
            layernorm_stage(nc, s, "ln7")
            with ExitStack() as own:
                t = Ternary(nc, own)
                ternary_stage(nc, s, d, t)
                ternary_units_stage(nc, s, t)
        store_stage(nc, s, out)


def halves_swapped(w, width):
    n = w.shape[-1] // width
    return np.ascontiguousarray(w.reshape(w.shape[0], n, 2, width // 2)[:, :, ::-1].reshape(w.shape))


def lay_out(i):
    f = {k: np.asarray(v) for k, v in i.items()}
    c = np.ascontiguousarray
    d = {"x": f["x"], "g_xattn": f["g_xattn"], "g_ffn": f["g_ffn"], "ids": c(f["itok_BxS_0_1023"].T)}
    d["ctx"] = f["ctx_2048"]
    d["ctxT"] = c(f["ctx_2048"].reshape(B * T, KD, 128).transpose(2, 1, 0))
    half = R // 2
    freq = (np.float32(1.0) / np.power(np.float32(10000.0), np.arange(half, dtype=np.float32) / np.float32(half)))
    ang = (np.arange(T, dtype=np.float32)[:, None] * freq.astype(np.float32)).astype(np.float32)
    d["cos"] = c(np.tile(np.cos(ang).T, (4, 1)).astype(np.float32))
    sin = np.sin(ang).T.astype(np.float32)
    d["sin"] = c(np.concatenate([-sin, sin, -sin, sin], axis=0))
    d["l0_w_kvc"] = f["L0_xattn_W_kvc"]
    kr = f["L0_xattn_W_kr"]
    d["l0_w_kr"] = c(np.stack([np.tile(kr, (1, 2)), np.tile(halves_swapped(kr, R), (1, 2))], axis=1))
    d["l0_w_dq"] = f["L0_xattn_W_dq"]
    d["l0_w_uqT"] = c(f["L0_xattn_W_uq"].T.reshape(NG, GH, HD, QC))
    d["l0_w_ukT"] = c(f["L0_xattn_W_uk"].T.reshape(NG, GH, HD, KVC))
    d["l0_w_uvT"] = c(f["L0_xattn_W_uv"].T.reshape(NG, GH, HD, KVC))
    d["l0_w_o"] = c(f["L0_xattn_W_o"].reshape(NG, GH, HD, D))
    qr = f["L0_xattn_W_qr"]
    both = np.stack([qr, halves_swapped(qr, R)])
    d["l0_w_qr"] = c(both.reshape(2, QC, NG, GH * R).transpose(2, 0, 1, 3))
    d["l0_router"] = f["L0_ffn_wa"]
    for name, routed, shared in (("wg", "rg", "sg"), ("wu", "rw1", "sw1"), ("wd", "rw2", "sw2")):
        d["l0_" + name] = c(np.concatenate([f["L0_ffn_" + routed], f["L0_ffn_" + shared]]))
    for name, routed, shared in (("bg", "rgb", "sgb"), ("bu", "rb1", "sb1")):
        d["l0_" + name] = c(np.concatenate([f["L0_ffn_" + routed], f["L0_ffn_" + shared]])
                            .reshape(E + 2, 2, 128).transpose(2, 0, 1))
    d["l0_bias_rows"] = c(np.stack([f["L0_ffn_rgb"], f["L0_ffn_rb1"]], axis=1))
    d["l0_bd"] = c(np.concatenate([f["L0_ffn_rb2"], f["L0_ffn_sb2"]]))
    for n in "qkv":
        w = f["L1_xattn_W" + n].T
        d[f"l1_w_{n}T"] = c(w.reshape(KD, 128, NG, 128).transpose(2, 1, 0, 3))
        d[f"l1_b_{n}"] = f["L1_xattn_b" + n] if n == "v" else c(f["L1_xattn_b" + n].reshape(NG, 128).T)
    d["l1_w_oT"] = c(f["L1_xattn_Wo"].T.reshape(NG, 128, D))
    d["l1_b_o"] = f["L1_xattn_bo"]
    d["l1_router"] = c(f["L1_ffn_gate_w"].T)
    for name, routed, shared in (("wg", "w_gate", "sw_gate"), ("wu", "w_up", "sw_up")):
        d["l1_" + name] = c(np.concatenate([f["L1_ffn_" + routed],
                                            f["L1_ffn_" + shared].reshape(D, 2, 352).transpose(1, 0, 2)]))
    d["l1_wd"] = c(np.concatenate([f["L1_ffn_w_down"], f["L1_ffn_sw_down"].reshape(2, 352, D)]))
    d["l2_router"] = c(f["L2_ffn_gate_w"].T)
    w13 = f["L2_ffn_w13"].reshape(E, 2, 352, D).transpose(1, 0, 3, 2)
    s13 = f["L2_ffn_sw13"].reshape(2, 2, 352, D).transpose(0, 1, 3, 2)
    d["l2_wg"], d["l2_wu"] = c(np.concatenate([w13[0], s13[0]])), c(np.concatenate([w13[1], s13[1]]))
    d["l2_wd"] = c(np.concatenate([f["L2_ffn_w2"].transpose(0, 2, 1), f["L2_ffn_sw2"].T.reshape(2, 352, D)]))
    d["l2_decay"] = f["L2_xattn_decay"].reshape(1)
    d["l2_w_inT"], d["l2_w_outT"] = c(f["L2_xattn_W_in"].T), c(f["L2_xattn_W_out"].T)
    d["l2_b_in"] = c(f["L2_xattn_b_in"].reshape(KD, 128).T)
    for n in ("b_out", "gamma", "beta"):
        d["l2_" + n] = f["L2_xattn_" + n]
    for n in "qkvo":
        d[f"l3_w_{n}T"] = c(f["L3_xattn_w" + n].T)
    pad = 4 * 352 - L3_HIDDEN
    for n in "13":
        w = np.pad(f["L3_ffn_w" + n].T, ((0, 0), (0, pad)))
        d[f"l3_w_{n}T"] = c(w.reshape(D, 4, 352).transpose(1, 0, 2))
    d["l3_w_2T"] = c(np.pad(f["L3_ffn_w2"].T, ((0, pad), (0, 0))).reshape(4, 352, D))
    return d


def kernel(**inputs):
    from concourse import bacc
    from concourse.bass_utils import run_bass_kernel_spmd

    nc = bacc.Bacc("TRN2", target_bir_lowering=False, num_devices=1)
    arrays = {f"in_{k}": v for k, v in lay_out(inputs).items()}
    dram = {k[3:]: nc.dram_tensor(k, v.shape, mybir.dt.from_np(v.dtype), kind="ExternalInput").ap()
            for k, v in arrays.items()}
    out = nc.dram_tensor("out_x", (B, TOK, D), F32, kind="ExternalOutput").ap()
    build(nc, dram, out)
    return run_bass_kernel_spmd(nc, [arrays], core_ids=[0]).results[0]["out_x"]
```

```python
from contextlib import ExitStack

import numpy as np

import concourse.bass as bass
from concourse import mybir

F32 = mybir.dt.float32
F32R = mybir.dt.float32r
I32 = mybir.dt.int32
U32 = mybir.dt.uint32
ALU = mybir.AluOpType
ACT = mybir.ActivationFunctionType
AX_X = mybir.AxisListType.X

B, TOK, D = 8, 112, 512
NT = B * TOK
HALF = NT // 2
KD = D // 128
T = 375
KT, TT = 3, 125
NEG = -1e30
LN_EPS = 1e-5

H, HD, KVC, QC, R = 16, 128, 128, 192, 64
QC1 = QC - 128
LOOKBACK = 8
SCALE0 = 1.0 / float(np.sqrt(np.float32(HD + R)))
GH = 4
NG = H // GH
HD1 = D // H
SCALE1 = 1.0 / float(np.sqrt(np.float32(HD1)))
SCALE3 = 1.0 / float(np.sqrt(D))
E = 16
CAP = 256
BLK = 128


def most_blocks(top_k):
    return (E + (NT * top_k - top_k) // BLK + 1) // 2 * 2


MAX_BLOCKS = most_blocks(6)
CLEARS = 2
L3_HIDDEN = int(2 * D * 4 / 3)
L3_CHUNKS = (L3_HIDDEN + 127) // 128
RAWS = 4


class Chip:

    def __init__(self, nc, ctx):
        self.nc = nc
        self.used = []

        def sb(name, shape, dt=F32):
            return ctx.enter_context(nc.sbuf_tensor(name, shape, dt))

        self.x = sb("x", [TOK, B, D])
        self.xn_buffer = sb("xn", [128, B, D])
        self.xn = self.xn_buffer[0:TOK, :, :]
        self.xnT = sb("xnT", [128, KD, NT])
        self.ident = sb("ident", [128, 128])
        self.ones = sb("ones", [128, 128])
        self.before = sb("before", [TOK, TOK])
        self.tanh_g = sb("tanh_g", [128, 8])
        self.raw_g = sb("raw_g", [128, 8])
        self.eps = sb("eps", [128, 1])
        self.expert_ids = sb("expert_ids", [TOK, E])
        self.gate_w = sb("gate_w", [128, KD, E])
        self.slots = sb("slots", [TOK, 6, B], U32)
        self.slots_in = sb("slots_in", [TOK, 6, B], U32)
        self.weights = sb("weights", [TOK, B, 8])
        self.token_ids = sb("token_ids", [TOK, B])
        self.slot_tokens = sb("slot_tokens", [BLK, MAX_BLOCKS], U32)
        self.table = sb("table", [1, 3 * MAX_BLOCKS + E + 1], I32)
        self.block_ids = sb("block_ids", [TOK, MAX_BLOCKS])
        self.thresholds = sb("thresholds", [TOK, 7])
        self.turns = sb("turns", [TOK, E])
        self.twos = sb("twos", [TOK, MAX_BLOCKS // 2])
        self.xn_rows = nc.dram_tensor("xn_rows", (NT, D), F32, kind="Internal").ap()
        self.slot_rows = nc.dram_tensor("slot_rows", (MAX_BLOCKS * BLK, D), F32, kind="Internal").ap()
        self.slot_list = nc.dram_tensor("slot_list", (MAX_BLOCKS * BLK, 1), F32, kind="Internal").ap()
        self.zeros = sb("zeros", [128, D])
        self.ctx_sums = sb("ctx_sums", [128, KD, B])
        self.coef_sum = sb("coef_sum", [128, 1])
        self.ternary = Ternary(nc, ctx)
        self.ctx_loaded = nc.alloc_semaphore("ctx_loaded")
        self.cleared = nc.alloc_semaphore("cleared")
        self.bank = [ctx.enter_context(nc.psum_tensor(f"bank{i}", [128, 512], F32)) for i in range(8)]
        self.iota_i = sb("iota_i", [TOK, T], I32)
        self.key_ids = sb("key_ids", [TOK, T])
        self.ids_i = sb("ids_i", [TOK, B], I32)
        self.stats = sb("stats", [TOK, B, 6])
        self.mv = sb("mv", [TOK, B, 2])
        self.sd = sb("sd", [TOK, B])
        self.rstd = sb("rstd", [TOK, B])
        self.context_life = ExitStack()
        self.ctxT = self.context_life.enter_context(nc.sbuf_tensor("ctxT", [128, KD, B * T], F32))

    def sems(self, stage, *names):
        own = [self.nc.alloc_semaphore(f"{stage}_{n}") for n in names]
        self.used += own
        return own

    def clear_semaphores(self):
        self.nc.clear_and_free_semaphores(self.used)
        self.used = []
        self.nc.all_engine_barrier()


def setup_stage(nc, s, d, beside=None):
    with ExitStack() as ctx:
        loaded, made, masked = s.sems("setup", "loaded", "made", "masked")
        block = ctx.enter_context(nc.Block())

        @block.sync
        def _(sp):
            sp.dma_start(s.x[:, :, :], d["x"].rearrange("b p d -> p b d")).then_inc(loaded, 16)
            sp.dma_start(s.raw_g[:, 0:4], d["g_xattn"].partition_broadcast(128)).then_inc(loaded, 16)
            sp.dma_start(s.raw_g[:, 4:8], d["g_ffn"].partition_broadcast(128)).then_inc(loaded, 16)
            if beside:
                beside(sp)
            for k in range(KD):
                sp.dma_start(s.ctxT[:, k, :], d["ctxT"][:, k, :]).then_inc(s.ctx_loaded, 16)
            sp.wait_ge(loaded, 16 * 3)

        @block.scalar
        def _(act):
            act.wait_ge(loaded, 16 * 3)
            act.activation(s.tanh_g[:, :], s.raw_g[:, :], ACT.Tanh)

        @block.gpsimd
        def _(pool):
            pool.memset(s.ident[:, :], 0.0).then_inc(made, 1)
            pool.memset(s.before[:, :], 1.0).then_inc(made, 1)
            pool.memset(s.ones[:, :], 1.0)
            pool.memset(s.eps[:, :], LN_EPS)
            pool.iota(s.iota_i[:, :], pattern=[[1, T]], base=0, channel_multiplier=0).then_inc(made, 1)
            pool.wait_ge(made, 3)
            pool.affine_select(out=s.ident[:, :], in_=s.ident[:, :], compare_op=ALU.not_equal, fill=1.0,
                               base=0, pattern=[[-1, 128]], channel_multiplier=1)
            pool.affine_select(out=s.before[:, :], in_=s.before[:, :], compare_op=ALU.is_gt, fill=0.0,
                               base=0, pattern=[[1, TOK]], channel_multiplier=-1)
            pool.tensor_copy(s.key_ids[:, :], s.iota_i[:, :]).then_inc(masked, 1)
            pool.iota(s.ids_i[:, :], pattern=[[TOK, B]], base=0, channel_multiplier=1).then_inc(masked, 1)
            pool.memset(s.turns[:, :], -1.0).then_inc(masked, 1)
            pool.memset(s.zeros[:, :], 0.0).then_inc(masked, 1)
            pool.wait_ge(masked, 4)
            pool.tensor_copy(s.expert_ids[:, :], s.key_ids[:, 0:E])
            pool.tensor_copy(s.token_ids[:, :], s.ids_i[:, :])
            pool.tensor_copy(s.block_ids[:, :], s.key_ids[:, 0:MAX_BLOCKS])
            pool.tensor_scalar(s.thresholds[:, :], s.key_ids[:, 0:7], float(BLK), None, ALU.mult).then_inc(masked, 1)
            pool.tensor_scalar(s.twos[:, :], s.key_ids[:, 0:MAX_BLOCKS // 2], 2.0, None, ALU.mult)
            pool.memset(s.turns[:, :].rearrange("p (e two) -> p e two", two=2)[:, :, 1], 1.0)
            pool.wait_ge(masked, 5)
            pool.memset(s.turns[:, 0:1], 0.0)
            pool.memset(s.thresholds[:, 0:1], -1.0)


def clear_scratch(sp, s):
    shape = [BLK, MAX_BLOCKS // CLEARS, D]
    for i in range(CLEARS):
        rows = s.slot_rows[i * shape[0] * shape[1]:(i + 1) * shape[0] * shape[1], :]
        sp.dma_start(rows.rearrange("(n p) d -> p n d", p=BLK), s.zeros[:, :].unsqueeze(1).to_broadcast(shape))\
          .then_inc(s.cleared, 16)
    sp.dma_start(s.slot_list.rearrange("(n p) o -> n (p o)", p=BLK), s.zeros[0:MAX_BLOCKS, 0:BLK]).then_inc(s.cleared, 16)


def logits_of(s):
    return s.bank[4][0:TOK, 0:B * E].rearrange("p (b e) -> p b e", b=B)


def layernorm_stage(nc, s, name, beside=None, gate_loaded=None):
    with ExitStack() as ctx:
        stats_done, mv_done, sd_done, rstd_done, norm_done, tr_done = s.sems(
            name, "stats_done", "mv_done", "sd_done", "rstd_done", "norm_done", "tr_done")
        copied = s.sems(name, "copied")[0]
        block = ctx.enter_context(nc.Block())

        @block.sync
        def _(sp):
            if beside:
                beside(sp)

        @block.vector
        def _(dve):
            for n in range(B + 4):
                if n < B:
                    dve.bn_stats(s.stats[:, n, :], s.x[:, n, :]).then_inc(stats_done, 1)
                if 1 <= n < B + 1:
                    b = n - 1
                    dve.wait_ge(stats_done, b + 1)
                    dve.bn_aggr(s.mv[:, b, :], s.stats[:, b, :]).then_inc(mv_done, 1)
                if 3 <= n < B + 3:
                    b = n - 3
                    dve.wait_ge(sd_done, b + 1)
                    dve.reciprocal(s.rstd[:, b:b + 1], s.sd[:, b:b + 1]).then_inc(rstd_done, 1)
                if n >= 4:
                    b = n - 4
                    dve.wait_ge(rstd_done, b + 1)
                    dve.tensor_scalar(s.xn[:, b, :], s.x[:, b, :], s.mv[:, b, 0:1], s.rstd[:, b:b + 1],
                                      ALU.subtract, ALU.mult).then_inc(norm_done, 1)

        @block.scalar
        def _(act):
            for n in range(B + 3):
                if n < B:
                    act.wait_ge(mv_done, n + 1)
                    act.activation(s.sd[:, n:n + 1], s.mv[:, n, 1:2], ACT.Sqrt, bias=s.eps[0:TOK, :]).then_inc(sd_done, 1)
                if n >= 3:
                    b = n - 3
                    act.wait_ge(tr_done, b + 1)
                    act.activation(s.xnT[:, :, b * TOK:(b + 1) * TOK],
                                   s.bank[b % 4][:, 0:KD * TOK].rearrange("p (k t) -> p k t", k=KD), ACT.Copy)\
                       .then_inc(copied, 1)

        @block.tensor
        def _(pe):
            for n in range(B + 2):
                if n < B:
                    pe.wait_ge(norm_done, n + 1)
                    if n >= 4:
                        pe.wait_ge(copied, n - 3)
                    for k in range(KD):
                        mm = pe.transpose(s.bank[n % 4][:, k * TOK:(k + 1) * TOK],
                                          s.xn[:, n, k * 128:(k + 1) * 128], s.ident[0:TOK, 0:TOK])
                    mm.then_inc(tr_done, 1)
                if n >= 2 and gate_loaded:
                    b = n - 2
                    if b == 0:
                        pe.wait_ge(gate_loaded, 16)
                    pe.wait_ge(copied, b + 1)
                    for k in range(KD):
                        pe.matmul(logits_of(s)[:, b, :], s.xnT[:, k, b * TOK:(b + 1) * TOK], s.gate_w[:, k, :],
                                  start=(k == 0), stop=(k == KD - 1))


def router_stage(nc, s, name, top_k, layer, softmax, eps, shared, ring, capacity=None):
    NB = most_blocks(top_k)
    width, func, biases = shared.width, shared.func, shared.biases
    chunks = chunks_of(width)
    FC = len(chunks)
    PIECES = 2 * FC
    with ExitStack() as ctx:
        def sb(n, shape, dt=F32):
            return ctx.enter_context(nc.sbuf_tensor(f"{name}_{n}", shape, dt))

        (exp_done, step, hot_done, rank_done, rows_stored, ranks_read, slots_ready, scattered,
         listed, turned, g_done, u_done, act_done, h_done, y_done, y_added, extra, own_added, gates_ready, gT_done,
         gT_copied) = s.sems(
            name, "exp_done", "step", "hot_done", "rank_done", "rows_stored", "ranks_read",
            "slots_ready", "scattered", "listed", "turned", "g_done", "u_done", "act_done", "h_done", "y_done",
            "y_added", "extra", "own_added", "gates_ready", "gT_done", "gT_copied")
        wg, wu, wd = shared.w[0]
        acted = sb("acted", [128, 2, HALF])
        hT = sb("hT", [128, FC, NT])
        slot_list = sb("slot_list", [MAX_BLOCKS, BLK])
        if biases:
            bg, bu = sb("bg", [128, FC]), sb("bu", [128, FC])
            bd = sb("bd", [E + 2, D])
            gates = sb("gates", [TOK, E + 2, B])
            gT = sb("gT", [E + 2, B * TOK])
        lmax = sb("lmax", [TOK, B])
        shifted = sb("shifted", [TOK, B, E])
        expd = sb("expd", [TOK, B, E])
        denom = sb("denom", [TOK, B, E])
        esum = sb("esum", [TOK, B])
        einv = sb("einv", [TOK, B])
        scores = sb("scores", [TOK, B, E])
        top = s.weights
        top_i = sb("top_i", [TOK, B, 8], U32)
        top_f = sb("top_f", [TOK, B, 8])
        wsum = sb("wsum", [TOK, B])
        winv = sb("winv", [TOK, B])
        hot = sb("hot", [TOK, top_k, B, E])
        part = sb("part", [TOK, B, E])
        mix = sb("mix", [TOK, B, E]) if biases else None
        chosen = sb("chosen", [TOK, B, E])
        running = sb("running", [TOK, B + 1, E])
        kept = sb("kept", [TOK, B, E])
        place = sb("place", [TOK, B, E])
        slot_f = sb("slot_f", [TOK, B])
        kept_k = sb("kept_k", [TOK, B])
        counts = sb("counts", [TOK, E])
        over_t = sb("over_t", [TOK, E, 7])
        blocks = sb("blocks", [TOK, E])
        upto = sb("upto", [TOK, E])
        first = sb("first", [TOK, E])
        first_slot = sb("first_slot", [TOK, E])
        at = sb("at", [1, NB, E])
        at_turn = sb("at_turn", [1, NB, E])
        expert = sb("expert", [1, NB])
        parity = sb("parity", [1, NB])
        field = sb("field", [1, NB])
        pairs = sb("pairs", [1, NB // 2])
        pair_count = sb("pair_count", [1, 1])
        logits = logits_of(s)
        ranks = s.bank[5][0:TOK, 0:B * E]
        rank = ranks.rearrange("p (b e) -> p b e", b=B)
        counted = s.bank[5][0:TOK, B * E:B * E + E]
        block = ctx.enter_context(nc.Block())

        @block.sync
        def _(sp):
            sp.dma_start(s.xn_rows.rearrange("(b p) d -> p b d", p=TOK), s.xn[:, :, :]).then_inc(rows_stored, 16)
            if biases:
                sp.dma_start(bg[:, :], biases[0][:, E, :]).then_inc(extra, 16)
                sp.dma_start(bu[:, :], biases[1][:, E, :]).then_inc(extra, 16)
                sp.dma_start(bd[:, :], biases[2]).then_inc(extra, 16)
            load_shared(sp, shared, 1)
            ring.load_first(sp)
            sp.wait_ge(rows_stored, 16)
            sp.wait_ge(scattered, 16 * top_k * B)
            sp.dma_start(slot_list[:, :], s.slot_list.rearrange("(n p) o -> n (p o)", p=BLK)).then_inc(listed, 16)

        @block.gpsimd
        def _(pool):
            slots, bound = s.slots, {}
            if capacity:
                slots, bound = s.slots_in, dict(bounds_check=NB * BLK - 1, oob_is_err=False)
            pool.wait_ge(s.cleared, 16 * (CLEARS + 1))
            for k in range(top_k):
                pool.wait_ge(slots_ready, k + 1)
                for b in range(B):
                    pool.indirect_dma_start(s.slot_list, bass.IndirectOffsetOnAxis(ap=slots[:, k, b:b + 1], axis=0),
                                            s.token_ids[:, b:b + 1], None, **bound).then_inc(scattered, 16)

        @block.tensor
        def _(pe):
            def gate_up(q, between=None):
                half, (f0, fn) = q // FC, chunks[q % FC]
                if q >= 2:
                    pe.wait_ge(h_done, q - 1)
                for weight, out, done in ((wg, s.bank[2 * (q % 2)], g_done), (wu, s.bank[2 * (q % 2) + 1], u_done)):
                    if between and weight is wu:
                        between()
                    for k in range(KD):
                        mm = pe.matmul(out[0:fn, 0:HALF], weight[:, k, f0:f0 + fn],
                                       s.xnT[:, k, half * HALF:(half + 1) * HALF], start=(k == 0), stop=(k == KD - 1))
                    mm.then_inc(done, 1)

            def ranks_and_counts():
                pe.wait_ge(hot_done, 1)
                pe.matmul(counted, s.ones[0:TOK, 0:TOK], running[:, B, :], start=True, stop=True)
                pe.matmul(ranks, s.ones[0:TOK, 0:TOK], running[:, 0:B, :].rearrange("p b e -> p (b e)"),
                          start=True, stop=False)
                pe.matmul(ranks, s.before[:, :], chosen[:, :, :].rearrange("p b e -> p (b e)"),
                          start=False, stop=True).then_inc(rank_done, 1)

            pe.wait_ge(shared.loaded[0], 16 * 4)
            gate_up(0)
            gate_up(1, between=ranks_and_counts)
            gate_up(2)
            gate_up(3)
            if biases:
                pe.wait_ge(gates_ready, 1)
                for b in range(B):
                    mm = pe.transpose(s.bank[6 + b // 4][0:E + 2, (b % 4) * TOK:(b % 4 + 1) * TOK], gates[:, :, b],
                                      s.ident[0:TOK, 0:TOK])
                mm.then_inc(gT_done, 1)
            for q in range(4, PIECES):
                gate_up(q)
            pe.wait_ge(ranks_read, 1)
            if biases:
                pe.wait_ge(extra, 48)
                pe.wait_ge(gT_copied, 2)
            for b in range(B):
                out = s.bank[4 + b % 4][0:TOK, :]
                pe.wait_ge(h_done, FC * (1 + b // (B // 2)))
                if b >= 4:
                    pe.wait_ge(y_added, b - 3)
                if biases:
                    pe.matmul(out, gT[:, b * TOK:(b + 1) * TOK], bd[:, :], start=True, stop=False)
                for c, (f0, fn) in enumerate(chunks):
                    mm = pe.matmul(out, hT[0:fn, c, b * TOK:(b + 1) * TOK], wd[0:fn, c, :],
                                   start=(c == 0 and not biases), stop=(c == FC - 1))
                mm.then_inc(y_done, 1)
            pe.wait_ge(listed, 16)
            pe.transpose(s.bank[0][:, 0:MAX_BLOCKS], slot_list[:, :], s.ident[0:MAX_BLOCKS, 0:MAX_BLOCKS])\
              .then_inc(turned, 1)

        @block.scalar
        def _(act):
            if softmax:
                act.wait_ge(step, 3)
                act.activation(expd[:, :, :], shifted[:, :, :], ACT.Exp).then_inc(exp_done, 1)
            else:
                act.activation(expd[:, :, :], logits, ACT.Exp, scale=-1.0).then_inc(exp_done, 1)
            if biases:
                act.wait_ge(extra, 48)
            for q in range(PIECES):
                f0, fn = chunks[q % FC]
                act.wait_ge(g_done, q + 1)
                if q >= 2:
                    act.wait_ge(h_done, q - 1)
                kind = dict(bias=bg[0:fn, q % FC:q % FC + 1]) if biases else {}
                act.activation(acted[0:fn, q % 2, :], s.bank[2 * (q % 2)][0:fn, 0:HALF], func, **kind).then_inc(act_done, 1)
            if biases:
                act.wait_ge(gT_done, 1)
                for i in range(2):
                    act.activation(gT[:, i * HALF:(i + 1) * HALF], s.bank[6 + i][0:E + 2, 0:HALF], ACT.Copy)\
                       .then_inc(gT_copied, 1)

        @block.vector
        def _(dve):
            chain = [0]

            def then(instruction):
                chain[0] += 1
                instruction.then_inc(step, 1)
                dve.wait_ge(step, chain[0])

            def over(ap):
                return ap.unsqueeze(2).to_broadcast([TOK, B, E])

            def each_tile(ap):
                return ap.unsqueeze(1).to_broadcast([TOK, B, E])

            def hidden(q):
                half, c, (f0, fn) = q // FC, q % FC, chunks[q % FC]
                dve.wait_ge(u_done, q + 1)
                dve.wait_ge(act_done, q + 1)
                out = hT[0:fn, c, half * HALF:(half + 1) * HALF]
                up = s.bank[2 * (q % 2) + 1][0:fn, 0:HALF]
                if biases:
                    dve.scalar_tensor_tensor(out=out, in0=up, scalar=bu[0:fn, c:c + 1], in1=acted[0:fn, q % 2, :],
                                             op0=ALU.add, op1=ALU.mult).then_inc(h_done, 1)
                else:
                    dve.tensor_tensor(out, up, acted[0:fn, q % 2, :], ALU.mult).then_inc(h_done, 1)

            then(dve.memset(running[:, 0, :], 0.0))
            if softmax:
                then(dve.tensor_reduce(lmax[:, :], logits, AX_X, ALU.max))
                then(dve.tensor_tensor(shifted[:, :, :], logits, over(lmax[:, :]), ALU.subtract))
                dve.wait_ge(exp_done, 1)
                then(dve.tensor_reduce(esum[:, :], expd[:, :, :], AX_X, ALU.add))
                then(dve.reciprocal(einv[:, :], esum[:, :]))
                then(dve.tensor_tensor(scores[:, :, :], expd[:, :, :], over(einv[:, :]), ALU.mult))
            else:
                dve.wait_ge(exp_done, 1)
                then(dve.tensor_scalar(denom[:, :, :], expd[:, :, :], 1.0, None, ALU.add))
                then(dve.reciprocal(scores[:, :, :], denom[:, :, :]))
            for b in range(B):
                op = dve.max(top[:, b, :], scores[:, b, :])
            then(op)
            for b in range(B):
                op = dve.max_index(top_i[:, b, :], top[:, b, :], scores[:, b, :])
            then(op)
            then(dve.tensor_copy(top_f[:, :, :], top_i[:, :, :]))
            for k in range(top_k):
                op = dve.tensor_tensor(hot[:, k, :, :], each_tile(s.expert_ids[:, :]), over(top_f[:, :, k]), ALU.is_equal)
            then(op)
            then(dve.tensor_tensor(chosen[:, :, :], hot[:, 0, :, :], hot[:, 1, :, :], ALU.add))
            for k in range(2, top_k):
                then(dve.tensor_tensor(chosen[:, :, :], chosen[:, :, :], hot[:, k, :, :], ALU.add))
            for b in range(B):
                then(dve.tensor_tensor(running[:, b + 1, :], running[:, b, :], chosen[:, b, :], ALU.add))
            dve.sem_inc(hot_done, 1)
            then(dve.tensor_reduce(wsum[:, :], top[:, :, 0:top_k], AX_X, ALU.add))
            if eps:
                then(dve.tensor_scalar(wsum[:, :], wsum[:, :], eps, None, ALU.add))
            then(dve.reciprocal(winv[:, :], wsum[:, :]))
            then(dve.tensor_tensor(top[:, :, 0:top_k], top[:, :, 0:top_k],
                                   winv[:, :].unsqueeze(2).to_broadcast([TOK, B, top_k]), ALU.mult))
            if biases:
                dve.wait_ge(extra, 48)
            hidden(0)
            if biases:
                then(dve.tensor_tensor(mix[:, :, :], hot[:, 0, :, :], over(top[:, :, 0]), ALU.mult))
                for k in range(1, top_k):
                    then(dve.tensor_tensor(part[:, :, :], hot[:, k, :, :], over(top[:, :, k]), ALU.mult))
                    then(dve.tensor_tensor(mix[:, :, :], mix[:, :, :], part[:, :, :], ALU.add))
                dve.tensor_copy(gates[:, E:E + 2, :], s.ones[0:TOK, 0:2 * B].rearrange("p (u b) -> p u b", u=2))
                dve.tensor_copy(gates[:, 0:E, :].rearrange("p e b -> p b e"), mix[:, :, :]).then_inc(gates_ready, 1)
            then(dve.tensor_scalar(top[:, :, 0:top_k], top[:, :, 0:top_k], s.tanh_g[0:TOK, 4 + layer:5 + layer], None,
                                   ALU.mult))
            dve.wait_ge(rank_done, 1)
            if capacity:
                then(dve.tensor_scalar(kept[:, :, :], rank, float(capacity), None, ALU.is_lt))
                then(dve.tensor_scalar(counts[:, :], counted, float(capacity), None, ALU.min))
                then(dve.tensor_scalar(place[:, :, :], rank, float(capacity - 1), None, ALU.min))
            else:
                then(dve.tensor_copy(counts[:, :], counted))
                then(dve.tensor_copy(place[:, :, :], rank))
            dve.sem_inc(ranks_read, 1)
            then(dve.tensor_tensor(over_t[:, :, :], counts[:, :].unsqueeze(2).to_broadcast([TOK, E, 7]),
                                   s.thresholds[:, :].unsqueeze(1).to_broadcast([TOK, E, 7]), ALU.is_gt))
            then(dve.tensor_reduce(blocks[:, :], over_t[:, :, :], AX_X, ALU.add))
            then(dve.tensor_tensor_scan(upto[:, :], s.ones[0:TOK, 0:E], blocks[:, :], 0.0, ALU.mult, ALU.add))
            then(dve.tensor_tensor(first[:, :], upto[:, :], blocks[:, :], ALU.subtract))
            then(dve.tensor_scalar(first_slot[:, :], first[:, :], float(BLK), None, ALU.mult))
            then(dve.tensor_tensor(place[:, :, :], place[:, :, :], each_tile(first_slot[:, :]), ALU.add))
            for k in range(top_k):
                then(dve.tensor_tensor(part[:, :, :], hot[:, k, :, :], place[:, :, :], ALU.mult))
                then(dve.tensor_reduce(slot_f[:, :], part[:, :, :], AX_X, ALU.add))
                then(dve.tensor_copy(s.slots[:, k, :], slot_f[:, :]))
                if capacity:
                    then(dve.tensor_tensor(part[:, :, :], hot[:, k, :, :], kept[:, :, :], ALU.mult))
                    then(dve.tensor_reduce(kept_k[:, :], part[:, :, :], AX_X, ALU.add))
                    then(dve.tensor_tensor(top[:, :, k], top[:, :, k], kept_k[:, :], ALU.mult))
                    then(dve.tensor_scalar(kept_k[:, :], kept_k[:, :], -1.0, -float(NB * BLK), ALU.add, ALU.mult))
                    then(dve.tensor_tensor(slot_f[:, :], slot_f[:, :], kept_k[:, :], ALU.add))
                    then(dve.tensor_copy(s.slots_in[:, k, :], slot_f[:, :]))
                dve.sem_inc(slots_ready, 1)
                if k < 2:
                    hidden(k + 1)
            hidden(3)
            ids = s.block_ids[0:1, 0:NB].unsqueeze(2).to_broadcast([1, NB, E])
            then(dve.tensor_tensor(at[:, :, :], ids, first[0:1, :].unsqueeze(1).to_broadcast([1, NB, E]), ALU.is_ge))
            then(dve.tensor_reduce(expert[:, :], at[:, :, :], AX_X, ALU.add))
            then(dve.tensor_tensor(at_turn[:, :, :], at[:, :, :],
                                   s.turns[0:1, :].unsqueeze(1).to_broadcast([1, NB, E]), ALU.mult))
            then(dve.tensor_reduce(parity[:, :], at_turn[:, :, :], AX_X, ALU.add))
            then(dve.tensor_copy(s.table[0:1, 0:NB], parity[:, :]))
            then(dve.tensor_tensor(field[:, :], expert[:, :], parity[:, :], ALU.subtract))
            then(dve.tensor_scalar(field[:, :], field[:, :], 1.0, load_inc(layer) / 2, ALU.add, ALU.mult))
            then(dve.tensor_scalar(s.table[0:1, MAX_BLOCKS:MAX_BLOCKS + NB], field[:, :], 1.0, None, ALU.add))
            then(dve.tensor_tensor(field[:, :], expert[:, :], parity[:, :], ALU.add))
            then(dve.tensor_scalar(field[:, :], field[:, :], -1.0, load_inc(layer) / 2, ALU.add, ALU.mult))
            then(dve.tensor_scalar(s.table[0:1, 2 * MAX_BLOCKS:2 * MAX_BLOCKS + NB], field[:, :], 1.0, None, ALU.add))
            then(dve.memset(s.table[0:1, 3 * MAX_BLOCKS:3 * MAX_BLOCKS + 2], 0))
            then(dve.tensor_copy(s.table[0:1, 3 * MAX_BLOCKS + 2:3 * MAX_BLOCKS + E], first[0:1, 1:E - 1]))
            then(dve.tensor_tensor(pairs[:, :], upto[0:1, E - 1:E].to_broadcast([1, NB // 2]), s.twos[0:1, 0:NB // 2],
                                   ALU.is_gt))
            then(dve.tensor_reduce(pair_count[:, :], pairs[:, :], AX_X, ALU.add))
            then(dve.tensor_scalar(s.table[0:1, 3 * MAX_BLOCKS + E:], pair_count[:, :], -1.0, None, ALU.add))
            if biases:
                for b in range(B):
                    dve.scalar_tensor_tensor(out=s.x[:, b, :], in0=s.xn[:, b, :],
                                             scalar=s.tanh_g[0:TOK, 4 + layer:5 + layer], in1=s.x[:, b, :],
                                             op0=ALU.mult, op1=ALU.add).then_inc(own_added, 1)
                dve.wait_ge(own_added, B)
            for q in range(4, PIECES):
                hidden(q)
            for b in range(B):
                dve.wait_ge(y_done, b + 1)
                dve.scalar_tensor_tensor(out=s.x[:, b, :], in0=s.bank[4 + b % 4][0:TOK, :],
                                         scalar=s.tanh_g[0:TOK, 4 + layer:5 + layer], in1=s.x[:, b, :],
                                         op0=ALU.mult, op1=ALU.add).then_inc(y_added, 1)
            dve.wait_ge(turned, 1)
            dve.tensor_copy(s.slot_tokens[:, :], s.bank[0][:, 0:MAX_BLOCKS])


def load_inc(layer):
    return 16 * (3 if layer == 0 else 2)


class Ring:

    def __init__(self, nc, ctx, s, name, dram, width, biases):
        def sb(n, shape):
            return ctx.enter_context(nc.sbuf_tensor(f"{name}_{n}", shape, F32))

        self.dram, self.width, self.biases = dram, width, biases
        self.wg = sb("wg", [128, 2, KD, width])
        self.wu = sb("wu", [128, 2, KD, width])
        self.wd = sb("wd", [128, 2, len(chunks_of(width)), D])
        self.bias_rows = sb("bias_rows", [1, 2, 2, width]) if biases is not None else None
        self.w_loaded = s.sems(name, "w_loaded0", "w_loaded1")
        self.d_loaded = s.sems(name, "d_loaded0", "d_loaded1")

    def load_gate_up(self, sp, e, v):
        load_gate_up(sp, self.dram, e, self.wg[:, v, :, :], self.wu[:, v, :, :], self.w_loaded[v])
        if self.biases is not None:
            sp.dma_start(self.bias_rows[0:1, v, :, :], self.biases[bass.ds(e, 1)]).then_inc(self.w_loaded[v], 16)

    def load_down(self, sp, e, v):
        load_down(sp, self.dram, e, self.width, self.wd[:, v, :, :], self.d_loaded[v])
        if self.biases is not None:
            sp.sem_inc(self.d_loaded[v], 16)

    def load_first(self, sp):
        for v in range(2):
            sp.sem_inc(self.w_loaded[v], 1)
            sp.sem_inc(self.d_loaded[v], 1)
            self.load_gate_up(sp, v, v)
            self.load_down(sp, v, v)


class Shared:

    def __init__(self, nc, ctx, s, name, w_gate, w_up, w_down, width, func, biases=None):
        self.name, self.dram, self.width, self.func, self.biases = name, (w_gate, w_up, w_down), width, func, biases
        FC = len(chunks_of(width))
        self.w = [[ctx.enter_context(nc.sbuf_tensor(f"{name}_shared_{n}{i}", shape, F32))
                   for n, shape in (("g", [128, KD, width]), ("u", [128, KD, width]), ("d", [128, FC, D]))] for i in range(2)]
        self.loaded = s.sems(name, "shared0", "shared1")
        self.stored = s.sems(name, "stored0", "stored1")


def chunks_of(width):
    return [(c * 128, min(128, width - c * 128)) for c in range((width + 127) // 128)]


def load_unit(eng, dram, u, width, wg, wu, wd, done):
    load_gate_up(eng, dram, u, wg, wu, done)
    load_down(eng, dram, u, width, wd, done)


def load_gate_up(eng, dram, u, wg, wu, done):
    one = bass.ds(u, 1)
    eng.dma_start(wg[:, :, :], dram[0][one].rearrange("o (k p) f -> p (o k) f", p=128)).then_inc(done, 16)
    eng.dma_start(wu[:, :, :], dram[1][one].rearrange("o (k p) f -> p (o k) f", p=128)).then_inc(done, 16)


def load_down(eng, dram, u, width, wd, done):
    first = width // 128 * 128 if width % 128 else width - 128
    one = bass.ds(u, 1)
    eng.dma_start(wd[:, 0:first // 128, :],
                  dram[2][one, 0:first].rearrange("o (c p) f -> p (o c) f", p=128)).then_inc(done, 16)
    eng.dma_start(wd[0:width - first, first // 128, :],
                  dram[2][one, first:width].rearrange("o p f -> (o p) f")).then_inc(done, 16)


def load_shared(eng, shared, i):
    load_unit(eng, shared.dram, E + i, shared.width, *shared.w[i], shared.loaded[i])


def pairs_less_one(eng, s, top_k):
    at = 3 * MAX_BLOCKS + E
    return eng.value_load(s.table[0:1, at:at + 1], min_val=1, max_val=most_blocks(top_k) // 2 - 1)


def combine_stage(nc, s, name, shared, layer, top_k):
    width, func, biases = shared.width, shared.func, shared.biases
    chunks = chunks_of(width)
    FC = len(chunks)
    PIECES = 2 * FC
    DEPTH = 4
    with ExitStack() as ctx:
        def sb(n, shape, dt=F32):
            return ctx.enter_context(nc.sbuf_tensor(f"{name}_{n}", shape, dt))

        g_done, u_done, act_done, h_done, y_done, y_added, extra, combined, outputs_stored = s.sems(
            name, "g_done", "u_done", "act_done", "h_done", "y_done", "y_added", "extra", "combined", "outputs_stored")
        spare = sb("spare", [128, 1])
        gathered = s.sems(name, *[f"gathered{j}" for j in range(DEPTH)])
        wg, wu, wd = shared.w[1]
        acted = sb("acted", [128, 2, HALF])
        hT = sb("hT", [128, FC, NT])
        if biases:
            bg, bu = sb("bg", [128, FC]), sb("bu", [128, FC])
        rows = sb("rows", [TOK, DEPTH, D])
        block = ctx.enter_context(nc.Block())

        @block.sync
        def _(sp):
            if biases:
                sp.dma_start(bg[:, :], biases[0][:, E + 1, :]).then_inc(extra, 16)
                sp.dma_start(bu[:, :], biases[1][:, E + 1, :]).then_inc(extra, 16)

        @block.gpsimd
        def _(pool):
            pool.wait_ge(outputs_stored, 1)
            for j in range(top_k * B):
                k, b = j // B, j % B
                if j >= DEPTH:
                    pool.wait_ge(combined, j - DEPTH + 1)
                pool.indirect_dma_start(rows[:, j % DEPTH, :], None, s.slot_rows,
                                        bass.IndirectOffsetOnAxis(ap=s.slots[:, k, b:b + 1], axis=0))\
                    .then_inc(gathered[j % DEPTH], 16)

        @block.tensor
        def _(pe):
            pe.wait_ge(shared.loaded[1], 16 * 4)
            for q in range(PIECES):
                half, (f0, fn) = q // FC, chunks[q % FC]
                if q >= 2:
                    pe.wait_ge(h_done, q - 1)
                for weight, out, done in ((wg, s.bank[2 * (q % 2)], g_done), (wu, s.bank[2 * (q % 2) + 1], u_done)):
                    for k in range(KD):
                        mm = pe.matmul(out[0:fn, 0:HALF], weight[:, k, f0:f0 + fn],
                                       s.xnT[:, k, half * HALF:(half + 1) * HALF], start=(k == 0), stop=(k == KD - 1))
                    mm.then_inc(done, 1)
            for b in range(B):
                pe.wait_ge(h_done, FC * (1 + b // (B // 2)))
                if b >= 4:
                    pe.wait_ge(y_added, b - 3)
                for c, (f0, fn) in enumerate(chunks):
                    mm = pe.matmul(s.bank[4 + b % 4][0:TOK, :], hT[0:fn, c, b * TOK:(b + 1) * TOK], wd[0:fn, c, :],
                                   start=(c == 0), stop=(c == FC - 1))
                mm.then_inc(y_done, 1)

        @block.scalar
        def _(act):
            pairs = pairs_less_one(act, s, top_k)
            for v in range(2):
                act.wait_ge(shared.stored[v], pairs * 16 + 17)
            act.copy(spare[:, :], s.ones[:, 0:1]).then_inc(outputs_stored, 1)
            if biases:
                act.wait_ge(extra, 32)
            for q in range(PIECES):
                f0, fn = chunks[q % FC]
                act.wait_ge(g_done, q + 1)
                if q >= 2:
                    act.wait_ge(h_done, q - 1)
                kind = dict(bias=bg[0:fn, q % FC:q % FC + 1]) if biases else {}
                act.activation(acted[0:fn, q % 2, :], s.bank[2 * (q % 2)][0:fn, 0:HALF], func, **kind).then_inc(act_done, 1)

        @block.vector
        def _(dve):
            added = [0]

            def combine_some(upto, own=0):
                if own:
                    dve.wait_ge(y_added, own)
                for j in range(added[0], min(upto, top_k * B)):
                    k, b = j // B, j % B
                    dve.wait_ge(gathered[j % DEPTH], 16 * (j // DEPTH + 1))
                    if j >= B:
                        dve.wait_ge(combined, j - B + 1)
                    dve.scalar_tensor_tensor(out=s.x[:, b, :], in0=rows[:, j % DEPTH, :],
                                             scalar=s.weights[:, b, k:k + 1], in1=s.x[:, b, :],
                                             op0=ALU.mult, op1=ALU.add).then_inc(combined, 1)
                    added[0] += 1

            if biases:
                dve.wait_ge(extra, 32)
            for q in range(PIECES):
                half, c, (f0, fn) = q // FC, q % FC, chunks[q % FC]
                dve.wait_ge(u_done, q + 1)
                dve.wait_ge(act_done, q + 1)
                out = hT[0:fn, c, half * HALF:(half + 1) * HALF]
                up = s.bank[2 * (q % 2) + 1][0:fn, 0:HALF]
                if biases:
                    dve.scalar_tensor_tensor(out=out, in0=up, scalar=bu[0:fn, c:c + 1], in1=acted[0:fn, q % 2, :],
                                             op0=ALU.add, op1=ALU.mult).then_inc(h_done, 1)
                else:
                    dve.tensor_tensor(out, up, acted[0:fn, q % 2, :], ALU.mult).then_inc(h_done, 1)
                combine_some(5 * (q + 1))
            rest = top_k * B - added[0]
            for b in range(B):
                dve.wait_ge(y_done, b + 1)
                dve.wait_ge(combined, added[0])
                dve.scalar_tensor_tensor(out=s.x[:, b, :], in0=s.bank[4 + b % 4][0:TOK, :],
                                         scalar=s.tanh_g[0:TOK, 4 + layer:5 + layer], in1=s.x[:, b, :],
                                         op0=ALU.mult, op1=ALU.add).then_inc(y_added, 1)
                combine_some(top_k * B - rest + (b + 1) * rest // B, own=b + 1)


def routed_blocks_stage(nc, s, name, layer, top_k, ring, shared, width, func):
    chunks = chunks_of(width)
    FC = len(chunks)
    with ExitStack() as ctx:
        def sb(n, shape, dt=F32):
            return ctx.enter_context(nc.sbuf_tensor(f"{name}_{n}", shape, dt))

        (ids_copied, xg_loaded0, xg_loaded1, tx_done, xT_copied, g_done, u_done, act_done,
         h_done, th_done, hT_copied, y_done, y_copied) = s.sems(
            name, "ids_copied", "xg_loaded0", "xg_loaded1", "tx_done", "xT_copied", "g_done",
            "u_done", "act_done", "h_done", "th_done", "hT_copied", "y_done", "y_copied")
        w_loaded, d_loaded, xg_loaded, stored = ring.w_loaded, ring.d_loaded, (xg_loaded0, xg_loaded1), shared.stored
        wg, wu, wd, bias_rows = ring.wg, ring.wu, ring.wd, ring.bias_rows
        ids = sb("ids", [BLK, 2], U32)
        spare = sb("spare", [BLK, 1])
        xg = sb("xg", [BLK, 2, D])
        xT = sb("xT", [128, 2, KD, BLK])
        acted = sb("acted", [BLK, 2, width])
        h = sb("h", [BLK, 2, width])
        hT = sb("hT", [128, 2, FC, BLK])
        y = sb("y", [BLK, 2, D])
        bank_g, bank_u, bank_x, bank_h, bank_y = s.bank[0:2], s.bank[2:4], s.bank[4], s.bank[5], s.bank[6:8]
        block = ctx.enter_context(nc.Block())
        def over_blocks(eng, first, step, last):
            pairs = pairs_less_one(eng, s, top_k)
            first()
            with eng.Fori(0, pairs) as i:
                step(i * 2 + 1, 1, i)
                step(i * 2 + 2, 0, i + 1)
            last(pairs * 2 + 1, 1, pairs)

        @block.sync
        def _(sp):
            with sp.Fori(1, E // 2) as i:
                for v in range(2):
                    free_at = sp.value_load(s.table[0:1, bass.ds(i * 2 + (3 * MAX_BLOCKS + v), 1)], min_val=0,
                                            max_val=MAX_BLOCKS)
                    sp.wait_ge(u_done, free_at + 2)
                    ring.load_gate_up(sp, i * 2 + v, v)
                    sp.wait_ge(y_done, free_at + 2)
                    ring.load_down(sp, i * 2 + v, v)

        @block.gpsimd
        def _(pool):
            pairs = pairs_less_one(pool, s, top_k)
            pool.memset(spare[:, :], 0.0)
            with pool.Fori(0, pairs + 1) as i:
                for v in range(2):
                    n = i * 2 + v
                    pool.wait_ge(tx_done, n + 1)
                    pool.tensor_copy(ids[:, v:v + 1], s.slot_tokens[:, bass.ds(n, 1)]).then_inc(ids_copied, 1)
                    pool.wait_ge(ids_copied, n + 1)
                    pool.tensor_tensor(spare[:, :], spare[:, :], spare[:, :], ALU.add)
                    pool.indirect_dma_start(xg[:, v, :], None, s.xn_rows,
                                            bass.IndirectOffsetOnAxis(ap=ids[:, v:v + 1], axis=0)).then_inc(xg_loaded[v], 16)

        @block.tensor
        def _(pe):
            pe.sem_inc(tx_done, 2)
            pe.sem_inc(u_done, 2)
            pe.sem_inc(th_done, 2)
            pe.sem_inc(y_done, 2)

            def turn_x(n, v, m):
                pe.wait_ge(xg_loaded[v], m * 16 + 16)
                pe.wait_ge(xT_copied, n + 1)
                for k in range(KD):
                    mm = pe.transpose(bank_x[:, k * BLK:(k + 1) * BLK], xg[:, v, k * 128:(k + 1) * 128], s.ident[:, :])
                mm.then_inc(tx_done, 1)

            def look_up(n):
                return (pe.value_load(s.table[0:1, bass.ds(n, 1)], min_val=0, max_val=1),
                        [pe.value_load(s.table[0:1, bass.ds(n + (w + 1) * MAX_BLOCKS, 1)], min_val=1,
                                       max_val=1 + load_inc(layer) * E // 2) for w in range(2)])

            def gate_up(n, v, m, entry):
                at, need = entry
                for w in range(2):
                    pe.wait_ge(w_loaded[w], need[w])
                pe.wait_ge(xT_copied, n + 2)
                pe.wait_ge(h_done, n + 1)
                for j, (w, bank, done) in enumerate(((wg, bank_g[v], g_done), (wu, bank_u[v], u_done))):
                    if bias_rows is not None:
                        pe.matmul(bank[:, 0:width], s.ones[0:1, :], bias_rows[0:1, bass.ds(at, 1), j, :]
                                  .rearrange("p o f -> p (o f)"), start=True, stop=False)
                    for k in range(KD):
                        mm = pe.matmul(bank[:, 0:width], xT[:, v, k, :],
                                       w[:, bass.ds(at, 1), k, :].rearrange("p o f -> p (o f)"),
                                       start=(k == 0 and bias_rows is None), stop=(k == KD - 1))
                    mm.then_inc(done, 1)

            def turn_h(n, v, m):
                pe.wait_ge(h_done, n + 3)
                pe.wait_ge(hT_copied, n + 1)
                for c, (f0, fn) in enumerate(chunks):
                    mm = pe.transpose(bank_h[0:fn, c * BLK:(c + 1) * BLK], h[:, v, f0:f0 + fn], s.ident[:, :])
                mm.then_inc(th_done, 1)

            def down(n, v, m, entry):
                at, need = entry
                for w in range(2):
                    pe.wait_ge(d_loaded[w], need[w])
                pe.wait_ge(hT_copied, n + 2)
                pe.wait_ge(y_copied, n + 1)
                for c, (f0, fn) in enumerate(chunks):
                    mm = pe.matmul(bank_y[v][:, :], hT[0:fn, v, c, :],
                                   wd[0:fn, bass.ds(at, 1), c, :].rearrange("p o f -> p (o f)"),
                                   start=(c == 0), stop=(c == FC - 1))
                mm.then_inc(y_done, 1)

            def first():
                turn_x(0, 0, 0)
                gate_up(0, 0, 0, look_up(0))
                turn_x(1, 1, 0)

            def step(n, v, m):
                now, before = look_up(n), look_up(n - 1)
                turn_h(n - 1, 1 - v, m)
                gate_up(n, v, m, now)
                turn_x(n + 1, 1 - v, m + v)
                down(n - 1, 1 - v, m, before)

            def last(n, v, m):
                now, before = look_up(n), look_up(n - 1)
                turn_h(n - 1, 1 - v, m)
                gate_up(n, v, m, now)
                down(n - 1, 1 - v, m, before)
                turn_h(n, v, m)
                down(n, v, m, now)

            over_blocks(pe, first, step, last)

        @block.scalar
        def _(act):
            act.sem_inc(xT_copied, 1)
            act.sem_inc(stored[0], 1)
            act.sem_inc(stored[1], 1)

            def copy_xT(n, v, m):
                act.wait_ge(tx_done, n + 3)
                act.wait_ge(u_done, n + 1)
                act.activation(xT[:, v, :, :], bank_x[:, :].rearrange("p (k n) -> p k n", k=KD), ACT.Copy)\
                   .then_inc(xT_copied, 1)

            def hidden(n, v, m):
                act.wait_ge(g_done, n + 1)
                act.wait_ge(h_done, n + 1)
                act.activation(acted[:, v, :], bank_g[v][:, 0:width], func).then_inc(act_done, 1)

            def store(n, v, m):
                act.wait_ge(y_copied, n + 3)
                act.dma_start(s.slot_rows[bass.ds(n * BLK, BLK), :], y[:, v, :]).then_inc(stored[v], 16)

            def first():
                copy_xT(0, 0, 0)
                hidden(0, 0, 0)
                copy_xT(1, 1, 0)

            def step(n, v, m):
                hidden(n, v, m)
                copy_xT(n + 1, 1 - v, m + v)
                store(n - 1, 1 - v, m)

            def last(n, v, m):
                hidden(n, v, m)
                store(n - 1, 1 - v, m)
                store(n, v, m)

            over_blocks(act, first, step, last)

        @block.vector
        def _(dve):
            dve.sem_inc(h_done, 2)
            dve.sem_inc(hT_copied, 1)
            dve.sem_inc(y_copied, 2)

            def product(n, v, m):
                dve.wait_ge(u_done, n + 3)
                dve.wait_ge(act_done, n + 1)
                dve.wait_ge(th_done, n + 1)
                dve.tensor_tensor(h[:, v, :], bank_u[v][:, 0:width], acted[:, v, :], ALU.mult).then_inc(h_done, 1)

            def copy_y(n, v, m):
                dve.wait_ge(y_done, n + 3)
                dve.wait_ge(stored[v], m * 16 + 1)
                dve.tensor_copy(y[:, v, :], bank_y[v][:, :]).then_inc(y_copied, 1)

            def copy_hT(n, v, m):
                dve.wait_ge(th_done, n + 3)
                dve.wait_ge(y_done, n + 1)
                whole, rest = width // 128, width % 128
                op = dve.tensor_copy(hT[:, v, 0:whole, :], bank_h[:, 0:whole * BLK].rearrange("p (c n) -> p c n", c=whole))
                if rest:
                    op = dve.tensor_copy(hT[0:rest, v, whole, :], bank_h[0:rest, whole * BLK:(whole + 1) * BLK])
                op.then_inc(hT_copied, 1)

            def first():
                product(0, 0, 0)
                copy_hT(0, 0, 0)

            def step(n, v, m):
                product(n, v, m)
                copy_y(n - 1, 1 - v, m + v - 1)
                copy_hT(n, v, m)

            def last(n, v, m):
                product(n, v, m)
                copy_y(n - 1, 1 - v, m + v - 1)
                copy_hT(n, v, m)
                copy_y(n, v, m)

            over_blocks(dve, first, step, last)


def routed_ffn(nc, s, d, layer, top_k, width, func, softmax, eps, capacity=None):
    dram = tuple(d[f"l{layer}_{n}"] for n in ("wg", "wu", "wd"))
    biases = tuple(d[f"l{layer}_{n}"] for n in ("bg", "bu", "bd")) if layer == 0 else None
    bias_rows = d["l0_bias_rows"] if layer == 0 else None
    with ExitStack() as own:
        shared = Shared(nc, own, s, f"f{layer}", *dram, width, func, biases)
        with ExitStack() as of_ring:
            gate_loaded = s.sems(f"r{layer}", "gate_loaded")[0]
            ring = Ring(nc, of_ring, s, f"f{layer}r", dram, width, bias_rows)

            def loads(sp):
                sp.dma_start(s.gate_w[:, :, :], d[f"l{layer}_router"].rearrange("(k p) e -> p k e", p=128))\
                  .then_inc(gate_loaded, 16)
                load_shared(sp, shared, 0)

            layernorm_stage(nc, s, f"ln{2 * layer + 1}", beside=loads, gate_loaded=gate_loaded)
            router_stage(nc, s, f"r{layer}", top_k, layer, softmax, eps, shared, ring, capacity)
            routed_blocks_stage(nc, s, f"f{layer}b", layer, top_k, ring, shared, width, func)
        combine_stage(nc, s, f"f{layer}c", shared, layer, top_k)


class DecayedSums:

    def __init__(self, nc, ctx, s):
        def sb(n, shape):
            return ctx.enter_context(nc.sbuf_tensor(f"l2s_{n}", shape, F32))

        self.s = s
        self.loaded, self.exp_done, self.step, self.summed = s.sems("l2s", "loaded", "exp_done", "step", "summed")
        self.decay = sb("decay", [128, 1])
        self.decay_exp = sb("decay_exp", [128, 1])
        self.keep = sb("keep", [128, 1])
        self.keeps = sb("keeps", [128, T])
        self.ones = sb("ones", [128, T])
        self.coef = sb("coef", [128, T])
        self.weighted = sb("weighted", [128, 2, T])

    def load(self, sp, d):
        sp.dma_start(self.decay[:, :], d["l2_decay"].partition_broadcast(128)).then_inc(self.loaded, 16)

    def exponential(self, act):
        act.wait_ge(self.loaded, 16)
        act.activation(self.decay_exp[:, :], self.decay[:, :], ACT.Exp, scale=-1.0).then_inc(self.exp_done, 1)

    def coefficients(self, dve):
        s, chain = self.s, [0]

        def then(instruction):
            chain[0] += 1
            instruction.then_inc(self.step, 1)
            dve.wait_ge(self.step, chain[0])

        then(dve.memset(self.ones[:, :], 1.0))
        dve.wait_ge(self.exp_done, 1)
        then(dve.tensor_scalar(self.keep[:, :], self.decay_exp[:, :], 1.0, None, ALU.add))
        then(dve.reciprocal(self.keep[:, :], self.keep[:, :]))
        then(dve.tensor_scalar(self.keeps[:, :], self.ones[:, :], self.keep[:, :], None, ALU.mult))
        then(dve.tensor_tensor_scan(self.coef[:, ::-1], self.keeps[:, :], self.ones[:, :], 0.0, ALU.mult, ALU.add))
        dve.tensor_reduce(s.coef_sum[:, :], self.coef[:, :], AX_X, ALU.add)

    def sum(self, dve, share, shares):
        s = self.s
        for i in range(share * KD * B // shares, (share + 1) * KD * B // shares):
            k, b = i // B, i % B
            if i >= 2:
                dve.wait_ge(self.summed, i - 1)
            dve.tensor_tensor_reduce(out=self.weighted[:, i % 2, :], in0=s.ctxT[:, k, b * T:(b + 1) * T],
                                     in1=self.coef[:, :], scale=1.0, scalar=0.0, op0=ALU.mult, op1=ALU.add,
                                     accum_out=s.ctx_sums[:, k, b:b + 1]).then_inc(self.summed, 1)


class ProjectWeights:

    def __init__(self, nc, ctx, s):
        def sb(n, shape, dt=F32):
            return ctx.enter_context(nc.sbuf_tensor(f"l0w_{n}", shape, dt))

        self.loaded = s.sems("l0w", "loaded")[0]
        self.kvc = sb("kvc", [128, KD, KVC])
        self.kr = sb("kr", [KVC, 2, 128])
        self.dq = sb("dq", [128, KD, QC])
        self.ids = sb("ids", [TOK, B], I32)

    def load(self, sp, d, a):
        for dst, src in ((self.dq[:, :, :], d["l0_w_dq"].rearrange("(k p) n -> p k n", p=128)),
                         (self.kvc[:, :, :], d["l0_w_kvc"].rearrange("(k p) n -> p k n", p=128)),
                         (self.kr[:, :, :], d["l0_w_kr"]), (a.cos[:, :], d["cos"]), (a.sin[:, :], d["sin"]),
                         (self.ids[:, :], d["ids"])):
            sp.dma_start(dst, src).then_inc(self.loaded, 16)


def latent_project_stage(nc, s, d, a, w):
    with ExitStack() as ctx:
        def sb(n, shape, dt=F32):
            return ctx.enter_context(nc.sbuf_tensor(f"l0p_{n}", shape, dt))

        (kv_done, kv_copied, rot_done, rot_mul, rot_added, tr_done, tr_copied, q_done, ids_f) = s.sems(
            "l0p", "kv_done", "kv_copied", "rot_done", "rot_mul", "rot_added", "tr_done",
            "tr_copied", "q_done", "ids_f")
        q_copied = s.sems("l0p", "q_copied")[0]
        masked = a.masked
        w_kvc, w_kr, w_dq, ids_i, loaded = w.kvc, w.kr, w.dq, w.ids, w.loaded
        part = sb("part", [128, 2, 2, T])
        ids = sb("ids", [TOK, B])
        low = sb("low", [TOK, 2, T])
        sums = DecayedSums(nc, ctx, s)
        block = ctx.enter_context(nc.Block())

        @block.sync
        def _(sp):
            sums.load(sp, d)
            a.load_weights(sp, d, 0)
            clear_scratch(sp, s)

        @block.tensor
        def _(pe):
            pe.wait_ge(loaded, 96)
            for q in range(4):
                m, half = q // 2, q % 2
                rows = 128 if m == 0 else QC1
                for k in range(KD):
                    mm = pe.matmul(s.bank[q][0:rows, 0:HALF], w_dq[:, k, m * 128:m * 128 + rows],
                                   s.xnT[:, k, half * HALF:(half + 1) * HALF], start=(k == 0), stop=(k == KD - 1))
                mm.then_inc(q_done, 1)
            pe.wait_ge(s.ctx_loaded, 16 * KD)
            for b in range(B + 1):
                if b < B:
                    if b < 2:
                        pe.wait_ge(q_copied, b + 1)
                    else:
                        pe.wait_ge(kv_copied, b - 1)
                    for k in range(KD):
                        mm = pe.matmul(s.bank[b % 2][:, 0:T], w_kvc[:, k, :], s.ctxT[:, k, b * T:(b + 1) * T],
                                       start=(k == 0), stop=(k == KD - 1))
                    mm.then_inc(kv_done, 1)
                if b >= 1:
                    c = b - 1
                    pe.wait_ge(kv_copied, c + 1)
                    if c == 0:
                        pe.wait_ge(q_copied, 4)
                    if c >= 2:
                        pe.wait_ge(rot_mul, 2 * (c - 1))
                        pe.wait_ge(tr_copied, c - 1)
                    for v in range(2):
                        mm = pe.matmul(s.bank[2 + 2 * (c % 2) + v][:, 0:T], w_kr[:, v, :],
                                       a.kvcT[:, c * T:(c + 1) * T], start=True, stop=True)
                    mm.then_inc(rot_done, 1)
                    for t in range(KT):
                        mm = pe.transpose(s.bank[6 + c % 2][0:TT, t * KVC:(t + 1) * KVC],
                                          a.kvcT[:, c * T + t * TT:c * T + (t + 1) * TT], s.ident[:, :])
                    mm.then_inc(tr_done, 1)

        @block.scalar
        def _(act):
            sums.exponential(act)
            for q in range(4):
                act.wait_ge(q_done, q + 1)
                dst = (a.qcT0, a.qcT1)[q // 2]
                rows = dst.shape[0]
                act.activation(dst[:, (q % 2) * HALF:(q % 2 + 1) * HALF], s.bank[q][0:rows, 0:HALF], ACT.Copy)\
                   .then_inc(q_copied, 1)
            for b in range(B + 1):
                if b < B:
                    act.wait_ge(kv_done, b + 1)
                    act.activation(a.kvcT[:, b * T:(b + 1) * T], s.bank[b % 2][:, 0:T], ACT.Copy).then_inc(kv_copied, 1)
                if b >= 1:
                    c = b - 1
                    act.wait_ge(tr_done, c + 1)
                    act.activation(a.kvc[:, c * KT:(c + 1) * KT, :],
                                   s.bank[6 + c % 2][0:TT, 0:KT * KVC].rearrange("p (t n) -> p t n", t=KT),
                                   ACT.Copy).then_inc(tr_copied, 1)

        @block.vector
        def _(dve):
            sums.coefficients(dve)
            dve.wait_ge(s.ctx_loaded, 16 * KD)
            for b in range(B):
                sums.sum(dve, b, B)
                dve.wait_ge(rot_done, b + 1)
                if b >= 2:
                    dve.wait_ge(rot_added, b - 1)
                for v, table in enumerate((a.cos, a.sin)):
                    dve.tensor_tensor(part[:, b % 2, v, :], s.bank[2 + 2 * (b % 2) + v][:, 0:T], table[:, :],
                                      ALU.mult).then_inc(rot_mul, 1)
                dve.wait_ge(rot_mul, 2 * (b + 1))
                dve.tensor_tensor(a.krT[:, b * T:(b + 1) * T], part[:, b % 2, 0, :], part[:, b % 2, 1, :],
                                  ALU.add).then_inc(rot_added, 1)

        @block.gpsimd
        def _(pool):
            pool.wait_ge(loaded, 96)
            pool.tensor_copy(ids[:, :], ids_i[:, :]).then_inc(ids_f, 1)
            pool.wait_ge(ids_f, 1)
            for b in range(B):
                pool.tensor_scalar(low[:, 0, :], s.key_ids[:, :], ids[:, b:b + 1], -float(LOOKBACK),
                                  ALU.subtract, ALU.is_ge).then_inc(masked, 1)
                pool.tensor_scalar(low[:, 1, :], s.key_ids[:, :], ids[:, b:b + 1], 0.0,
                                  ALU.subtract, ALU.is_le).then_inc(masked, 1)
                pool.wait_ge(masked, 4 * b + 2)
                pool.tensor_tensor(a.mask[:, b, :], low[:, 0, :], low[:, 1, :], ALU.add).then_inc(masked, 1)
                pool.wait_ge(masked, 4 * b + 3)
                pool.tensor_scalar(a.mask[:, b, :], a.mask[:, b, :], -2.0, -NEG / SCALE0, ALU.add, ALU.mult)\
                    .then_inc(masked, 1)


def latent_attention_stage(nc, s, d, a):
    N = B * GH
    BUFS = 5
    with ExitStack() as ctx:
        def sb(n, shape, dt=F32):
            return ctx.enter_context(nc.sbuf_tensor(f"l0a_{n}", shape, dt))

        (w_done, w_copied, qr_done, qr_mul, qr_added, s_done, s_masked, shift, e_done, inv_done, p_done,
         pt_done, pt_copied, z_done, z_copied, y_done, y_added) = s.sems(
            "l0a", "w_done", "w_copied", "qr_done", "qr_mul", "qr_added", "s_done", "s_masked",
            "shift", "e_done", "inv_done", "p_done", "pt_done", "pt_copied", "z_done", "z_copied", "y_done", "y_added")
        w_uq, w_uk, w_uv, w_o, w_qr0, w_qr1, loaded = a.w_uq, a.w_uk, a.w_uv, a.w_o, a.w_qr0, a.w_qr1, a.w_loaded
        qk0 = sb("qk0", [128, GH, KVC])
        qk1 = sb("qk1", [QC1, GH, KVC])
        vo = sb("vo", [KVC, GH, D])
        qT = s.xnT
        qrT = sb("qrT", [128, GH // 2, NT])
        shared = sb("shared", [128, 2 * KT * GH * TOK])
        part = shared[:, 0:4 * HALF].rearrange("p (i v n) -> p i v n", i=2, v=2)
        pT = shared[0:TT, :].rearrange("p (i t h n) -> p i t h n", i=2, t=KT, h=GH)
        p = sb("p", [TOK, BUFS, T])
        top = sb("top", [TOK, BUFS])
        spare = sb("spare", [TOK, 1])
        low = sb("low", [TOK, BUFS])
        total = sb("total", [TOK, BUFS])
        inv = sb("inv", [TOK, BUFS])
        zT = sb("zT", [KVC, 2, GH, TOK])
        block = ctx.enter_context(nc.Block())
        W_COPIES = 2 + GH + 2 * GH
        QR = 2 * 2
        MIXED = 3 + GH
        PROJECTED = MIXED + GH

        @block.sync
        def _(sp):
            with sp.Fori(1, NG) as g:
                sp.wait_ge(qr_done, g * QR + 1)
                a.load_weights(sp, d, g)

        @block.tensor
        def _(pe):
            pe.sem_inc(qr_done, 1)

            def scores(g, n):
                b, j = n // GH, n % GH
                if n >= 3:
                    pe.wait_ge(s_masked, 1 + g * N + n - 2)
                out = s.bank[n % 3][0:TOK, 0:T]
                r = 64 * (j % 2)
                pe.matmul(out, qT[:, j, b * TOK:(b + 1) * TOK], a.kvcT[:, b * T:(b + 1) * T], start=True, stop=False)
                pe.matmul(out, qrT[r:r + R, j // 2, b * TOK:(b + 1) * TOK], a.krT[r:r + R, b * T:(b + 1) * T],
                          start=False, stop=True).then_inc(s_done, 1)

            def turn(g, n):
                pe.wait_ge(p_done, g * N + n + 1)
                if n >= 2:
                    pe.wait_ge(pt_copied, 1 + g * N + n - 1)
                for t in range(KT):
                    mm = pe.transpose(s.bank[3 + n % 2][0:TT, t * TOK:(t + 1) * TOK],
                                      p[:, n % BUFS, t * TT:(t + 1) * TT], s.ident[0:TOK, 0:TOK])
                mm.then_inc(pt_done, 1)

            def mix(g, b, t):
                if t == 0:
                    pe.wait_ge(pt_copied, 1 + g * N + (b + 1) * GH)
                    if b:
                        pe.wait_ge(z_copied, 1 + g * B + b)
                mm = pe.matmul(s.bank[5][:, 0:GH * TOK], a.kvc[:, b * KT + t, :],
                               pT[:, b % 2, t, :, :].rearrange("p h n -> p (h n)"),
                               start=(t == 0), stop=(t == KT - 1))
                if t == KT - 1:
                    mm.then_inc(z_done, 1)

            def project(g, b, j):
                if j == 0:
                    pe.wait_ge(z_copied, 1 + g * B + b + 1)
                    if b >= 2:
                        pe.wait_ge(y_added, 1 + g * B + b - 1)
                mm = pe.matmul(s.bank[6 + b % 2][0:TOK, :], zT[:, b % 2, j, :], vo[:, j, :],
                               start=(j == 0), stop=(j == GH - 1))
                if j == GH - 1:
                    mm.then_inc(y_done, 1)

            with pe.Fori(0, NG) as g:
                pe.wait_ge(loaded, (g + 1) * 96)
                pe.wait_ge(y_added, 1 + g * B)
                for j in range(GH):
                    pe.matmul(s.bank[0][:, j * KVC:(j + 1) * KVC], w_uq[:, j, 0:128], w_uk[:, j, :],
                              start=True, stop=True)
                    mm = pe.matmul(s.bank[1][0:QC1, j * KVC:(j + 1) * KVC], w_uq[:, j, 128:QC], w_uk[:, j, :],
                                   start=True, stop=True)
                mm.then_inc(w_done, 1)
                for j in range(GH):
                    pe.matmul(s.bank[2 + j][:, :], w_uv[:, j, :], w_o[:, j, :], start=True, stop=True).then_inc(w_done, 1)
                for i in range(QR):
                    jj, half = i // 2, i % 2
                    pair = (6, 7) if i % 2 == 0 else (0, 1)
                    if i == 1:
                        pe.wait_ge(w_copied, g * W_COPIES + 2)
                    if i >= 2:
                        pe.wait_ge(qr_mul, g * 2 * QR + 2 * (i - 1))
                    for v in range(2):
                        out = s.bank[pair[v]][:, 0:HALF]
                        cols = slice(jj * 128, jj * 128 + 128)
                        toks = slice(half * HALF, (half + 1) * HALF)
                        pe.matmul(out, w_qr0[:, v, cols], a.qcT0[:, toks], start=True, stop=False)
                        mm = pe.matmul(out, w_qr1[:, v, cols], a.qcT1[:, toks], start=False, stop=True)
                    mm.then_inc(qr_done, 1)
                for i in range(2 * GH):
                    j, half = i // 2, i % 2
                    pe.wait_ge(w_copied, g * W_COPIES + 2 + i % 4 + 1 + (4 if i >= 4 else 0))
                    out = s.bank[2 + i % 4][:, 0:HALF]
                    toks = slice(half * HALF, (half + 1) * HALF)
                    pe.matmul(out, qk0[:, j, :], a.qcT0[:, toks], start=True, stop=False)
                    pe.matmul(out, qk1[:, j, :], a.qcT1[:, toks], start=False, stop=True).then_inc(w_done, 1)
                pe.wait_ge(w_copied, (g + 1) * W_COPIES)
                pe.wait_ge(qr_added, (g + 1) * QR)
                for n in range(PROJECTED + N):
                    if n < N:
                        scores(g, n)
                    if 3 <= n < N + 3:
                        turn(g, n - 3)
                    b, t = (n - MIXED) // GH, (n - MIXED) % GH
                    if 0 <= b < B and t < KT:
                        mix(g, b, t)
                    if n >= PROJECTED:
                        project(g, (n - PROJECTED) // GH, (n - PROJECTED) % GH)

        @block.scalar
        def _(act):
            act.sem_inc(pt_copied, 1)
            with act.Fori(0, NG) as g:
                act.wait_ge(w_done, g * (1 + 3 * GH) + 1)
                act.activation(qk0[:, :, :], s.bank[0][:, 0:GH * KVC].rearrange("p (h n) -> p h n", h=GH),
                               ACT.Copy).then_inc(w_copied, 1)
                act.activation(qk1[:, :, :], s.bank[1][0:QC1, 0:GH * KVC].rearrange("p (h n) -> p h n", h=GH),
                               ACT.Copy).then_inc(w_copied, 1)
                for j in range(GH):
                    act.wait_ge(w_done, g * (1 + 3 * GH) + 2 + j)
                    act.activation(vo[:, j, :], s.bank[2 + j][:, :], ACT.Copy).then_inc(w_copied, 1)
                for i in range(2 * GH):
                    act.wait_ge(w_done, g * (1 + 3 * GH) + 2 + GH + i)
                    act.activation(qT[:, i // 2, (i % 2) * HALF:(i % 2 + 1) * HALF], s.bank[2 + i % 4][:, 0:HALF],
                                   ACT.Copy).then_inc(w_copied, 1)
                for n in range(N + 3):
                    if n < N:
                        act.wait_ge(shift, g * N + n + 1)
                        act.activation(p[:, n % BUFS, :], p[:, n % BUFS, :], ACT.Exp,
                                       bias=low[:, n % BUFS:n % BUFS + 1], scale=SCALE0,
                                       accum_out=total[:, n % BUFS:n % BUFS + 1]).then_inc(e_done, 1)
                    if 1 <= n < N + 1:
                        m = n - 1
                        act.wait_ge(inv_done, g * N + m + 1)
                        act.activation(p[:, m % BUFS, :], p[:, m % BUFS, :], ACT.Copy,
                                       scale=inv[:, m % BUFS:m % BUFS + 1]).then_inc(p_done, 1)
                    if n >= 3 and n - 3 < N:
                        m = n - 3
                        b, j = m // GH, m % GH
                        act.wait_ge(pt_done, g * N + m + 1)
                        if b >= 2 and j == 0:
                            act.wait_ge(z_done, g * B + b - 1)
                        act.activation(pT[:, b % 2, :, j, :],
                                       s.bank[3 + m % 2][0:TT, 0:KT * TOK].rearrange("p (t n) -> p t n", t=KT),
                                       ACT.Copy).then_inc(pt_copied, 1)

        @block.vector
        def _(dve):
            dve.sem_inc(s_masked, 1)
            dve.sem_inc(z_copied, 1)
            dve.sem_inc(y_added, 1)
            with dve.Fori(0, NG) as g:
                for i in range(QR):
                    jj, half = i // 2, i % 2
                    pair = (6, 7) if i % 2 == 0 else (0, 1)
                    dve.wait_ge(qr_done, 1 + g * QR + i + 1)
                    for v, table in enumerate((a.cos, a.sin)):
                        dve.tensor_tensor(part[:, i % 2, v, :].rearrange("p (b t) -> p b t", t=TOK),
                                          s.bank[pair[v]][:, 0:HALF].rearrange("p (b t) -> p b t", t=TOK),
                                          table[:, 0:TOK].unsqueeze(1).to_broadcast([128, B // 2, TOK]),
                                          ALU.mult).then_inc(qr_mul, 1)
                    dve.wait_ge(qr_mul, g * 2 * QR + 2 * (i + 1))
                    dve.tensor_tensor(qrT[:, jj, half * HALF:(half + 1) * HALF], part[:, i % 2, 0, :],
                                      part[:, i % 2, 1, :], ALU.add).then_inc(qr_added, 1)
                for n in range(PROJECTED + N + 1):
                    if n >= MIXED + KT and (n - MIXED - KT) % GH == 0 and (n - MIXED - KT) // GH < B:
                        b = (n - MIXED - KT) // GH
                        dve.wait_ge(z_done, g * B + b + 1)
                        if b >= 2:
                            dve.wait_ge(y_done, g * B + b - 1)
                        dve.tensor_copy(zT[:, b % 2, :, :], s.bank[5][:, 0:GH * TOK].rearrange("p (h n) -> p h n", h=GH))\
                           .then_inc(z_copied, 1)
                    if n < N:
                        b = n // GH
                        dve.wait_ge(a.masked, 4 * B)
                        dve.wait_ge(s_done, g * N + n + 1)
                        if n == 0:
                            dve.memset(spare[:, :], 0.0)
                        if n >= BUFS:
                            dve.wait_ge(pt_done, g * N + n - BUFS + 1)
                        dve.tensor_tensor_reduce(out=p[:, n % BUFS, :], in0=s.bank[n % 3][0:TOK, 0:T],
                                                 in1=a.mask[:, b, :], scale=1.0, scalar=-3.0e38, op0=ALU.add,
                                                 op1=ALU.max, accum_out=top[:, n % BUFS:n % BUFS + 1]).then_inc(s_masked, 1)
                    if 1 <= n < N + 1:
                        m = (n - 1) % BUFS
                        dve.wait_ge(e_done, g * N + n)
                        dve.reciprocal(inv[:, m:m + 1], total[:, m:m + 1]).then_inc(inv_done, 1)
                    if n < N:
                        dve.wait_ge(s_masked, 1 + g * N + n + 1)
                        dve.tensor_scalar(low[:, n % BUFS:n % BUFS + 1], top[:, n % BUFS:n % BUFS + 1], -SCALE0, None,
                                          ALU.mult).then_inc(shift, 1)
                    if n >= PROJECTED + GH and (n - PROJECTED) % GH == 0:
                        b = (n - PROJECTED) // GH - 1
                        dve.wait_ge(y_done, g * B + b + 1)
                        dve.wait_ge(y_added, 1 + g * B + b)
                        dve.scalar_tensor_tensor(out=s.x[:, b, :], in0=s.bank[6 + b % 2][0:TOK, :],
                                                 scalar=s.tanh_g[0:TOK, 0:1], in1=s.x[:, b, :],
                                                 op0=ALU.mult, op1=ALU.add).then_inc(y_added, 1)


class HeadWeights:

    def __init__(self, nc, ctx, s):
        def sb(n, shape):
            return ctx.enter_context(nc.sbuf_tensor(f"l1w_{n}", shape, F32))

        self.loaded, self.o_loaded = s.sems("l1w", "loaded", "o_loaded")
        self.q = sb("q", [128, KD, 128])
        self.k = sb("k", [128, KD, 128])
        self.v = sb("v", [128, KD, 128])
        self.o = sb("o", [128, D])

    def load_projections(self, sp, d, g):
        for dst, src in ((self.q, "l1_w_qT"), (self.k, "l1_w_kT"), (self.v, "l1_w_vT")):
            sp.dma_start(dst[:, :, :], d[src][bass.ds(g, 1)].rearrange("o p k n -> p (o k) n")).then_inc(self.loaded, 16)

    def load_output(self, sp, d, g):
        sp.dma_start(self.o[:, :], d["l1_w_oT"][bass.ds(g, 1)].rearrange("o p n -> p (o n)")).then_inc(self.o_loaded, 16)

    def load_first(self, sp, d):
        self.load_projections(sp, d, 0)
        self.load_output(sp, d, 0)


def heads_attention_stage(nc, s, d, w):
    N = B * GH
    BUFS = 6
    VB = 128
    with ExitStack() as ctx:
        def sb(n, shape, dt=F32):
            return ctx.enter_context(nc.sbuf_tensor(f"l1a_{n}", shape, dt))

        (const, k_done, k_copied, q_done, q_copied, v_done, v_copied, s_done, max_done, shift, e_done,
         inv_done, p_done, pt_done, pt_copied, z_done, zt_copied, y_done, y_added, b_ready) = s.sems(
            "l1a", "const", "k_done", "k_copied", "q_done", "q_copied", "v_done", "v_copied",
            "s_done", "max_done", "shift", "e_done", "inv_done", "p_done", "pt_done", "pt_copied", "z_done",
            "zt_copied", "y_done", "y_added", "b_ready")
        w_q, w_k, w_v, w_o, loaded, o_loaded = w.q, w.k, w.v, w.o, w.loaded, w.o_loaded
        b_q = sb("b_q", [128, NG])
        b_k = sb("b_k", [128, NG])
        b_now = sb("b_now", [128, 2])
        b_v = sb("b_v", [TT, D])
        b_o = sb("b_o", [TOK, D])
        kT = sb("kT", [128, B * T])
        v = sb("v", [TT, B * KT, VB])
        qT = sb("qT", [128, NT])
        p = sb("p", [TOK, BUFS, T])
        top = sb("top", [TOK, BUFS])
        low = sb("low", [TOK, BUFS])
        total = sb("total", [TOK, BUFS])
        inv = sb("inv", [TOK, BUFS])
        pT = sb("pT", [TT, 2, KT, GH, TOK])
        zT = sb("zT", [VB, 2, TOK])
        block = ctx.enter_context(nc.Block())
        VT = B * KT // 4
        MIXED = 3 + GH
        PROJECTED = MIXED + GH + 1

        @block.sync
        def _(sp):
            sp.dma_start(b_q[:, :], d["l1_b_q"]).then_inc(const, 16)
            sp.dma_start(b_k[:, :], d["l1_b_k"]).then_inc(const, 16)
            sp.dma_start(b_v[:, :], d["l1_b_v"].partition_broadcast(TT)).then_inc(const, 16)
            sp.dma_start(b_o[:, :], d["l1_b_o"].partition_broadcast(TOK)).then_inc(const, 16)
            with sp.Fori(1, NG) as g:
                sp.wait_ge(v_done, g * VT + 1)
                w.load_projections(sp, d, g)
                sp.wait_ge(y_done, g * B + 1)
                w.load_output(sp, d, g)

        @block.tensor
        def _(pe):
            pe.sem_inc(v_done, 1)
            pe.sem_inc(y_done, 1)

            def scores(g, n):
                b, r = n // GH, HD1 * (n % GH)
                if n >= 3:
                    pe.wait_ge(e_done, g * N + n - 2)
                pe.matmul(s.bank[n % 3][0:TOK, 0:T], qT[r:r + HD1, b * TOK:(b + 1) * TOK],
                          kT[r:r + HD1, b * T:(b + 1) * T], start=True, stop=True).then_inc(s_done, 1)

            def turn(g, n):
                pe.wait_ge(p_done, g * N + n + 1)
                if n >= 2:
                    pe.wait_ge(pt_copied, 1 + g * N + n - 1)
                for t in range(KT):
                    mm = pe.transpose(s.bank[3 + n % 2][0:TT, t * TOK:(t + 1) * TOK],
                                      p[:, n % BUFS, t * TT:(t + 1) * TT], s.ident[0:TOK, 0:TOK])
                mm.then_inc(pt_done, 1)

            def mix(g, b, t):
                if t == 0:
                    pe.wait_ge(pt_copied, 1 + g * N + (b + 1) * GH)
                    if b >= 2:
                        pe.wait_ge(zt_copied, 1 + g * B + b - 1)
                mm = pe.matmul(s.bank[5 + b % 2][:, 0:GH * TOK], v[:, b * KT + t, :],
                               pT[:, b % 2, t, :, :].rearrange("p h n -> p (h n)"),
                               start=(t == 0), stop=(t == KT - 1))
                if t == KT - 1:
                    mm.then_inc(z_done, 1)

            def project(g, b):
                if b == 0:
                    pe.wait_ge(o_loaded, (g + 1) * 16)
                pe.wait_ge(zt_copied, 1 + g * B + b + 1)
                pe.wait_ge(y_added, g * B + b + 1)
                pe.matmul(s.bank[7][0:TOK, :], zT[:, b % 2, :], w_o[:, :], start=True, stop=True)\
                  .then_inc(y_done, 1)

            with pe.Fori(0, NG) as g:
                pe.wait_ge(loaded, (g + 1) * 48)
                for h in range(2):
                    for k in range(KD):
                        mm = pe.matmul(s.bank[h][:, 0:HALF], w_q[:, k, :], s.xnT[:, k, h * HALF:(h + 1) * HALF],
                                       start=(k == 0), stop=(k == KD - 1))
                    mm.then_inc(q_done, 1)
                for b in range(B):
                    if b >= 2:
                        pe.wait_ge(k_copied, g * B + b - 1)
                    for k in range(KD):
                        mm = pe.matmul(s.bank[2 + b % 2][:, 0:T], w_k[:, k, :], s.ctxT[:, k, b * T:(b + 1) * T],
                                       start=(k == 0), stop=(k == KD - 1))
                    mm.then_inc(k_done, 1)
                for c in range(VT):
                    if c >= 2:
                        pe.wait_ge(v_copied, g * VT + c - 1)
                    for i in range(4):
                        r0 = (c * 4 + i) * TT
                        for k in range(KD):
                            mm = pe.matmul(s.bank[4 + c % 2][0:TT, i * VB:(i + 1) * VB], s.ctxT[:, k, r0:r0 + TT],
                                           w_v[:, k, :], start=(k == 0), stop=(k == KD - 1))
                    mm.then_inc(v_done, 1)
                pe.wait_ge(q_copied, 2 * (g + 1))
                pe.wait_ge(k_copied, B * (g + 1))
                pe.wait_ge(v_copied, VT * (g + 1))
                for n in range(PROJECTED + N - GH + 1):
                    if n < N:
                        scores(g, n)
                    if 3 <= n < N + 3:
                        turn(g, n - 3)
                    b, t = (n - MIXED) // GH, (n - MIXED) % GH
                    if 0 <= b < B and t < KT:
                        mix(g, b, t)
                    if n >= PROJECTED and (n - PROJECTED) % GH == 0:
                        project(g, (n - PROJECTED) // GH)

        @block.scalar
        def _(act):
            act.wait_ge(const, 64)
            act.sem_inc(pt_copied, 1)
            act.sem_inc(zt_copied, 1)
            with act.Fori(0, NG) as g:
                act.copy(b_now[:, 0:1], b_q[:, bass.ds(g, 1)]).then_inc(b_ready, 1)
                act.copy(b_now[:, 1:2], b_k[:, bass.ds(g, 1)]).then_inc(b_ready, 1)
                act.wait_ge(b_ready, 2 * (g + 1))
                for h in range(2):
                    act.wait_ge(q_done, 2 * g + h + 1)
                    act.activation(qT[:, h * HALF:(h + 1) * HALF], s.bank[h][:, 0:HALF], ACT.Identity,
                                   bias=b_now[:, 0:1]).then_inc(q_copied, 1)
                for b in range(B):
                    act.wait_ge(k_done, g * B + b + 1)
                    act.activation(kT[:, b * T:(b + 1) * T], s.bank[2 + b % 2][:, 0:T], ACT.Identity,
                                   bias=b_now[:, 1:2]).then_inc(k_copied, 1)
                for n in range(MIXED + GH + N):
                    if n >= MIXED + KT and (n - MIXED - KT) % GH == 0 and (n - MIXED - KT) // GH < B:
                        b = (n - MIXED - KT) // GH
                        act.wait_ge(z_done, g * B + b + 1)
                        if b >= 2:
                            act.wait_ge(y_done, 1 + g * B + b - 1)
                        for j in range(GH):
                            op = act.activation(zT[j * HD1:(j + 1) * HD1, b % 2, :],
                                                s.bank[5 + b % 2][j * HD1:(j + 1) * HD1, j * TOK:(j + 1) * TOK], ACT.Copy)
                        op.then_inc(zt_copied, 1)
                    if n < N:
                        act.wait_ge(shift, g * N + n + 1)
                        if n >= BUFS:
                            act.wait_ge(pt_done, g * N + n - BUFS + 1)
                        act.activation(p[:, n % BUFS, :], s.bank[n % 3][0:TOK, 0:T], ACT.Exp,
                                       bias=low[:, n % BUFS:n % BUFS + 1], scale=SCALE1,
                                       accum_out=total[:, n % BUFS:n % BUFS + 1]).then_inc(e_done, 1)
                    if n >= 3 and n - 3 < N:
                        m = n - 3
                        b, j = m // GH, m % GH
                        act.wait_ge(pt_done, g * N + m + 1)
                        if b >= 2 and j == 0:
                            act.wait_ge(z_done, g * B + b - 1)
                        act.activation(pT[:, b % 2, :, j, :],
                                       s.bank[3 + m % 2][0:TT, 0:KT * TOK].rearrange("p (t n) -> p t n", t=KT),
                                       ACT.Copy).then_inc(pt_copied, 1)

        @block.vector
        def _(dve):
            dve.wait_ge(const, 64)
            dve.sem_inc(y_added, 1)
            for b in range(B):
                op = dve.scalar_tensor_tensor(out=s.x[:, b, :], in0=b_o[:, :], scalar=s.tanh_g[0:TOK, 1:2],
                                              in1=s.x[:, b, :], op0=ALU.mult, op1=ALU.add)
            op.then_inc(const, 1)
            dve.wait_ge(const, 65)
            with dve.Fori(0, NG) as g:
                for c in range(VT):
                    dve.wait_ge(v_done, 1 + g * VT + c + 1)
                    dve.tensor_tensor(v[:, c * 4:(c + 1) * 4, :],
                                      s.bank[4 + c % 2][0:TT, :].rearrange("p (i n) -> p i n", i=4),
                                      b_v[:, bass.ds(g * VB, VB)].unsqueeze(1).to_broadcast([TT, 4, VB]),
                                      ALU.add).then_inc(v_copied, 1)
                for n in range(PROJECTED + N - GH + 2):
                    now, last = slice(n % BUFS, n % BUFS + 1), slice((n - 1) % BUFS, (n - 1) % BUFS + 1)
                    if n < N:
                        dve.wait_ge(s_done, g * N + n + 1)
                        if n >= BUFS:
                            dve.wait_ge(e_done, g * N + n - BUFS + 1)
                        dve.tensor_reduce(top[:, now], s.bank[n % 3][0:TOK, 0:T], AX_X, ALU.max).then_inc(max_done, 1)
                    if 1 <= n < N + 1:
                        dve.wait_ge(e_done, g * N + n)
                        dve.reciprocal(inv[:, last], total[:, last]).then_inc(inv_done, 1)
                    if n < N:
                        dve.wait_ge(max_done, g * N + n + 1)
                        dve.tensor_scalar(low[:, now], top[:, now], -SCALE1, None, ALU.mult).then_inc(shift, 1)
                    if 1 <= n < N + 1:
                        dve.wait_ge(inv_done, g * N + n)
                        dve.tensor_scalar(p[:, (n - 1) % BUFS, :], p[:, (n - 1) % BUFS, :], inv[:, last], None, ALU.mult)\
                           .then_inc(p_done, 1)
                    if n > PROJECTED and (n - PROJECTED - 1) % GH == 0:
                        b = (n - PROJECTED - 1) // GH
                        dve.wait_ge(y_done, 1 + g * B + b + 1)
                        dve.wait_ge(y_added, 1 + g * B + b)
                        dve.scalar_tensor_tensor(out=s.x[:, b, :], in0=s.bank[7][0:TOK, :],
                                                 scalar=s.tanh_g[0:TOK, 1:2], in1=s.x[:, b, :],
                                                 op0=ALU.mult, op1=ALU.add).then_inc(y_added, 1)


class Recurrence:

    def __init__(self, nc, ctx, s):
        def sb(n, shape):
            return ctx.enter_context(nc.sbuf_tensor(f"l2a_{n}", shape, F32))

        self.loaded = s.sems("l2a", "loaded")[0]
        self.w_in = sb("w_in", [128, KD, D])
        self.w_out = sb("w_out", [128, KD, D])
        self.b_in = sb("b_in", [128, KD])
        self.b_out = sb("b_out", [B, D])
        self.gamma = sb("gamma", [TOK, D])
        self.beta = sb("beta", [TOK, D])

    def load(self, sp, d):
        loads = ((self.w_in[:, :, :], d["l2_w_inT"].rearrange("(k p) n -> p k n", p=128)),
                 (self.w_out[:, :, :], d["l2_w_outT"].rearrange("(k p) n -> p k n", p=128)),
                 (self.b_in[:, :], d["l2_b_in"]),
                 (self.b_out[:, :], d["l2_b_out"].partition_broadcast(B)),
                 (self.gamma[:, :], d["l2_gamma"].partition_broadcast(TOK)),
                 (self.beta[:, :], d["l2_beta"].partition_broadcast(TOK)))
        for dst, src in loads:
            sp.dma_start(dst, src).then_inc(self.loaded, 16)


def recurrence_stage(nc, s, r):
    with ExitStack() as ctx:
        def sb(n, shape):
            return ctx.enter_context(nc.sbuf_tensor(f"l2r_{n}", shape, F32))

        (selected, scaled, state_done, state_copied, rows_done, rows_copied, y_done, y_added, stats_done, mv_done,
         sd_done, rstd_done, weighted, finished) = s.sems(
            "l2r", "selected", "scaled", "state_done", "state_copied", "rows_done", "rows_copied", "y_done", "y_added",
            "stats_done", "mv_done", "sd_done", "rstd_done", "weighted", "finished")
        LOADED = 6 * 16
        state = sb("state", [128, KD, B])
        b_in_sum = sb("b_in_sum", [128, KD])
        rows = sb("rows", [B, D])
        select = sb("select", [B, B, TOK])
        block = ctx.enter_context(nc.Block())

        @block.gpsimd
        def _(pool):
            pool.tensor_copy(select[:, :, :], s.ident[0:B, 0:B].unsqueeze(2).to_broadcast([B, B, TOK])).then_inc(selected, 1)
            pool.wait_ge(r.loaded, LOADED)
            for vector in (r.beta, r.gamma):
                pool.tensor_scalar(vector[:, :], vector[:, :], s.tanh_g[0:TOK, 2:3], None, ALU.mult).then_inc(scaled, 1)
            pool.wait_ge(scaled, 2)
            for b in range(B):
                pool.tensor_tensor(s.x[:, b, :], s.x[:, b, :], r.beta[:, :], ALU.add).then_inc(scaled, 1)

        @block.tensor
        def _(pe):
            pe.wait_ge(r.loaded, LOADED)
            for m in range(KD):
                for k in range(KD):
                    mm = pe.matmul(s.bank[0][:, m * B:(m + 1) * B], r.w_in[:, k, m * 128:(m + 1) * 128], s.ctx_sums[:, k, :],
                                   start=(k == 0), stop=(k == KD - 1))
            mm.then_inc(state_done, 1)
            pe.wait_ge(state_copied, KD + 1)
            for k in range(KD):
                mm = pe.matmul(s.bank[1][0:B, :], state[:, k, :], r.w_out[:, k, :], start=(k == 0), stop=(k == KD - 1))
            mm.then_inc(rows_done, 1)
            pe.wait_ge(rows_copied, 1)
            pe.wait_ge(selected, 1)
            for b in range(B):
                if b >= 4:
                    pe.wait_ge(y_added, b - 3)
                pe.matmul(s.bank[2 + b % 4][0:TOK, :], select[:, b, :], rows[:, :], start=True, stop=True)\
                  .then_inc(y_done, 1)

        @block.scalar
        def _(act):
            for b in range(B):
                act.wait_ge(mv_done, b + 1)
                act.activation(s.sd[:, b:b + 1], s.mv[:, b, 1:2], ACT.Sqrt, bias=s.eps[0:TOK, :]).then_inc(sd_done, 1)

        @block.vector
        def _(dve):
            dve.wait_ge(r.loaded, LOADED)
            dve.tensor_scalar(b_in_sum[:, :], r.b_in[:, :], s.coef_sum[:, :], None, ALU.mult).then_inc(state_copied, 1)
            dve.wait_ge(state_copied, 1)
            dve.wait_ge(state_done, 1)
            for m in range(KD):
                dve.tensor_scalar(state[:, m, :], s.bank[0][:, m * B:(m + 1) * B], b_in_sum[:, m:m + 1], 1.0 / T,
                                  ALU.add, ALU.mult).then_inc(state_copied, 1)
            dve.wait_ge(rows_done, 1)
            dve.tensor_tensor(rows[:, :], s.bank[1][0:B, :], r.b_out[:, :], ALU.add).then_inc(rows_copied, 1)
            for n in range(B + 3):
                if n < B:
                    dve.wait_ge(y_done, n + 1)
                    dve.tensor_tensor(s.xn[:, n, :], s.xn[:, n, :], s.bank[2 + n % 4][0:TOK, :], ALU.add).then_inc(y_added, 1)
                if 1 <= n < B + 1:
                    b = n - 1
                    dve.wait_ge(y_added, b + 1)
                    dve.bn_stats(s.stats[:, b, :], s.xn[:, b, :]).then_inc(stats_done, 1)
                    dve.wait_ge(stats_done, b + 1)
                    dve.bn_aggr(s.mv[:, b, :], s.stats[:, b, :]).then_inc(mv_done, 1)
                if 2 <= n < B + 2:
                    b = n - 2
                    dve.wait_ge(mv_done, b + 1)
                    dve.wait_ge(scaled, 2 + B)
                    dve.scalar_tensor_tensor(out=s.xn[:, b, :], in0=s.xn[:, b, :], scalar=s.mv[:, b, 0:1],
                                             in1=r.gamma[:, :], op0=ALU.subtract, op1=ALU.mult).then_inc(weighted, 1)
                if n >= 3:
                    b = n - 3
                    dve.wait_ge(sd_done, b + 1)
                    dve.reciprocal(s.rstd[:, b:b + 1], s.sd[:, b:b + 1]).then_inc(rstd_done, 1)
                    dve.wait_ge(rstd_done, b + 1)
                    dve.wait_ge(weighted, b + 1)
                    dve.scalar_tensor_tensor(out=s.x[:, b, :], in0=s.xn[:, b, :], scalar=s.rstd[:, b:b + 1],
                                             in1=s.x[:, b, :], op0=ALU.mult, op1=ALU.add).then_inc(finished, 1)


class CacheWeights:

    def __init__(self, nc, ctx, s):
        self.loaded = s.sems("l3w", "loaded")[0]
        self.matrices = [ctx.enter_context(nc.sbuf_tensor(f"l3w_{n}", [128, KD, D], F32)) for n in "qkvo"]

    def load(self, sp, d):
        for dst, n in zip(self.matrices, "qkvo"):
            sp.dma_start(dst[:, :, :], d[f"l3_w_{n}T"].rearrange("(k p) n -> p k n", p=128)).then_inc(self.loaded, 16)


def cache_attention_stage(nc, s, d, w, t):
    with ExitStack() as ctx:
        def sb(n, shape, dt=F32):
            return ctx.enter_context(nc.sbuf_tensor(f"l3a_{n}", shape, dt))

        (v_loaded0, v_loaded1, qk_done, qk_copied, vn_done, vn_copied, s_done, max_done, shift, e_done,
         inv_done, pt_done, pt_copied, z_done, z_scaled, zt_done, zt_copied, y_done, y_added) = s.sems(
            "l3a", "v_loaded0", "v_loaded1", "qk_done", "qk_copied", "vn_done", "vn_copied",
            "s_done", "max_done", "shift", "e_done", "inv_done", "pt_done", "pt_copied", "z_done", "z_scaled",
            "zt_done", "zt_copied", "y_done", "y_added")
        ALL = T + TOK
        w_v, w_o = w.matrices[2:]
        qkT = [sb("qT", [128, KD, NT]), sb("kT", [128, KD, NT])]
        vn = sb("vn", [TOK, B, D])
        vc = sb("vc", [TT, 2, KT, D])
        p = sb("p", [TOK, 2, ALL])
        top = sb("top", [TOK, 2])
        low = sb("low", [TOK, 2])
        total = sb("total", [TOK, 2])
        inv = sb("inv", [TOK, 2])
        pT = sb("pT", [TT, 2, KT + 1, TOK])
        z = sb("z", [TOK, 2, D])
        zT = sb("zT", [128, 2, KD, TOK])
        v_loaded = (v_loaded0, v_loaded1)
        stage = s.xn_buffer[:, 0:6, :].rearrange("p (i m) n -> p i m n", i=2)
        size = s.xn_buffer[:, 6, :]
        staged = s.sems("l3a", "staged0", "staged1")
        sized, summed, sum_done, scaled = s.sems("l3a", "sized", "summed", "sum_done", "scaled")
        QK = 2 * KD * 2
        block = ctx.enter_context(nc.Block())

        @block.sync
        def _(sp):
            for c in range(L3_CHUNKS):
                if c >= 2:
                    sp.wait_ge(sized, 3 * (c - 1))
                sp.dma_start(stage[:, c % 2, :, :], d["l3_w_ffn"][c]).then_inc(staged[c % 2], 16)
            for b in range(B):
                if b >= 2:
                    sp.wait_ge(z_done, b - 1)
                sp.dma_start(vc[:, b % 2, :, :], d["ctx"][b].rearrange("(t p) n -> p t n", p=TT))\
                  .then_inc(v_loaded[b % 2], 16)

        @block.tensor
        def _(pe):
            pe.wait_ge(w.loaded, 64)
            for i in range(QK):
                m, h = (i // 2) % KD, i % 2
                if i >= 4:
                    pe.wait_ge(qk_copied, i - 3)
                for k in range(KD):
                    mm = pe.matmul(s.bank[i % 4][:, 0:HALF], w.matrices[i // (2 * KD)][:, k, m * 128:(m + 1) * 128],
                                   s.xnT[:, k, h * HALF:(h + 1) * HALF], start=(k == 0), stop=(k == KD - 1))
                mm.then_inc(qk_done, 1)
            for b in range(B):
                if b >= 4:
                    pe.wait_ge(vn_copied, b - 3)
                for k in range(KD):
                    mm = pe.matmul(s.bank[4 + b % 4][0:TOK, :], s.xnT[:, k, b * TOK:(b + 1) * TOK], w_v[:, k, :],
                                   start=(k == 0), stop=(k == KD - 1))
                mm.then_inc(vn_done, 1)

            def scores(b):
                if b >= 2:
                    pe.wait_ge(e_done, b - 1)
                toks = slice(b * TOK, (b + 1) * TOK)
                for k in range(KD):
                    pe.matmul(s.bank[b % 2][0:TOK, 0:T], qkT[0][:, k, toks], s.ctxT[:, k, b * T:(b + 1) * T],
                              start=(k == 0), stop=(k == KD - 1))
                for k in range(KD):
                    mm = pe.matmul(s.bank[b % 2][0:TOK, T:ALL], qkT[0][:, k, toks], qkT[1][:, k, toks],
                                   start=(k == 0), stop=(k == KD - 1))
                mm.then_inc(s_done, 1)

            def turn(b):
                pe.wait_ge(e_done, b + 1)
                if b >= 2:
                    pe.wait_ge(pt_copied, 2 * (b - 1))
                for t in range(KT + 1):
                    rows = TT if t < KT else TOK
                    mm = pe.transpose(s.bank[2 + b % 2][0:rows, t * TOK:(t + 1) * TOK],
                                      p[:, b % 2, t * TT:t * TT + rows], s.ident[0:TOK, 0:TOK])
                mm.then_inc(pt_done, 1)

            def mix(b):
                pe.wait_ge(pt_copied, 2 * (b + 1))
                pe.wait_ge(v_loaded[b % 2], 16 * (b // 2 + 1))
                if b >= 2:
                    pe.wait_ge(z_scaled, b - 1)
                for t in range(KT):
                    pe.matmul(s.bank[4 + b % 2][0:TOK, :], pT[:, b % 2, t, :], vc[:, b % 2, t, :],
                              start=(t == 0), stop=False)
                pe.matmul(s.bank[4 + b % 2][0:TOK, :], pT[0:TOK, b % 2, KT, :], vn[:, b, :],
                          start=False, stop=True).then_inc(z_done, 1)

            def turn_mix(b):
                pe.wait_ge(z_scaled, b + 1)
                if b:
                    pe.wait_ge(zt_copied, b)
                for k in range(KD):
                    mm = pe.transpose(s.bank[6][:, k * TOK:(k + 1) * TOK], z[:, b % 2, k * 128:(k + 1) * 128],
                                      s.ident[0:TOK, 0:TOK])
                mm.then_inc(zt_done, 1)

            def project(b):
                pe.wait_ge(zt_copied, b + 1)
                if b:
                    pe.wait_ge(y_added, b)
                for k in range(KD):
                    mm = pe.matmul(s.bank[7][0:TOK, :], zT[:, b % 2, k, :], w_o[:, k, :],
                                   start=(k == 0), stop=(k == KD - 1))
                mm.then_inc(y_done, 1)

            pe.wait_ge(qk_copied, QK)
            pe.wait_ge(summed, 1)
            pe.matmul(s.bank[3][:, 0:3], s.ones[:, :], t.total[:, :], start=True, stop=True).then_inc(sum_done, 1)
            pe.wait_ge(scaled, 1)
            pe.wait_ge(vn_copied, B)
            for n in range(B + 4):
                for lag, step in enumerate((scores, turn, mix, turn_mix, project)):
                    if 0 <= n - lag < B:
                        step(n - lag)

        @block.scalar
        def _(act):
            for i in range(QK):
                act.wait_ge(qk_done, i + 1)
                m, h = (i // 2) % KD, i % 2
                act.activation(qkT[i // (2 * KD)][:, m, h * HALF:(h + 1) * HALF], s.bank[i % 4][:, 0:HALF],
                               ACT.Copy).then_inc(qk_copied, 1)
                if 2 <= i < 2 + L3_CHUNKS:
                    c = i - 2
                    act.wait_ge(staged[c % 2], 16 * (c // 2 + 1))
                    for m in range(3):
                        if c or m:
                            act.wait_ge(sized, 3 * c + m)
                        act.activation(size, stage[:, c % 2, m, :], ACT.Abs,
                                       accum_out=t.magnitudes[:, m, c:c + 1]).then_inc(sized, 1)
            for n in range(B + 3):
                if n < B:
                    act.wait_ge(shift, n + 1)
                    if n >= 2:
                        act.wait_ge(pt_done, n - 1)
                        act.wait_ge(inv_done, n - 1)
                    act.activation(p[:, n % 2, :], s.bank[n % 2][0:TOK, 0:ALL], ACT.Exp, bias=low[:, n % 2:n % 2 + 1],
                                   scale=SCALE3, accum_out=total[:, n % 2:n % 2 + 1]).then_inc(e_done, 1)
                if 0 <= n - 1 < B:
                    b = n - 1
                    act.wait_ge(pt_done, b + 1)
                    if b >= 2:
                        act.wait_ge(z_done, b - 1)
                    act.activation(pT[:, b % 2, 0:KT, :],
                                   s.bank[2 + b % 2][0:TT, 0:KT * TOK].rearrange("p (t n) -> p t n", t=KT),
                                   ACT.Copy).then_inc(pt_copied, 1)
                    act.activation(pT[0:TOK, b % 2, KT, :], s.bank[2 + b % 2][0:TOK, KT * TOK:(KT + 1) * TOK],
                                   ACT.Copy).then_inc(pt_copied, 1)
                if 0 <= n - 3 < B:
                    b = n - 3
                    act.wait_ge(zt_done, b + 1)
                    if b >= 2:
                        act.wait_ge(y_done, b - 1)
                    act.activation(zT[:, b % 2, :, :], s.bank[6][:, 0:KD * TOK].rearrange("p (k n) -> p k n", k=KD),
                                   ACT.Copy).then_inc(zt_copied, 1)

        @block.vector
        def _(dve):
            for b in range(B):
                dve.wait_ge(vn_done, b + 1)
                dve.tensor_copy(vn[:, b, :], s.bank[4 + b % 4][0:TOK, :]).then_inc(vn_copied, 1)
            dve.wait_ge(sized, 3 * L3_CHUNKS)
            dve.tensor_reduce(t.total[:, :], t.magnitudes[:, :, :], AX_X, ALU.add).then_inc(summed, 1)
            dve.wait_ge(sum_done, 1)
            dve.tensor_scalar(t.scale[:, :], s.bank[3][:, 0:3], 1.0 / float(L3_HIDDEN * D), None, ALU.mult)\
               .then_inc(scaled, 1)
            dve.wait_ge(scaled, 1)
            for i, sign in enumerate((0.5, -0.5)):
                dve.tensor_scalar(t.half[:, 3 * i:3 * i + 3], t.scale[:, :], sign, None, ALU.mult)
            dve.tensor_tensor(t.output_scale[:, :], t.scale[:, 2:3], s.tanh_g[:, 7:8], ALU.mult)
            for n in range(B + 5):
                if n < B:
                    m = slice(n % 2, n % 2 + 1)
                    dve.wait_ge(s_done, n + 1)
                    if n >= 2:
                        dve.wait_ge(e_done, n - 1)
                    dve.tensor_reduce(top[:, m], s.bank[n % 2][0:TOK, 0:ALL], AX_X, ALU.max).then_inc(max_done, 1)
                    dve.wait_ge(max_done, n + 1)
                    dve.tensor_scalar(low[:, m], top[:, m], -SCALE3, None, ALU.mult).then_inc(shift, 1)
                if 0 <= n - 2 < B:
                    b = n - 2
                    dve.wait_ge(e_done, b + 1)
                    dve.reciprocal(inv[:, b % 2:b % 2 + 1], total[:, b % 2:b % 2 + 1]).then_inc(inv_done, 1)
                    dve.wait_ge(inv_done, b + 1)
                    dve.wait_ge(z_done, b + 1)
                    if b >= 2:
                        dve.wait_ge(zt_done, b - 1)
                    dve.tensor_scalar(z[:, b % 2, :], s.bank[4 + b % 2][0:TOK, :], inv[:, b % 2:b % 2 + 1], None,
                                      ALU.mult).then_inc(z_scaled, 1)
                if 0 <= n - 4 < B:
                    b = n - 4
                    dve.wait_ge(y_done, b + 1)
                    dve.scalar_tensor_tensor(out=s.x[:, b, :], in0=s.bank[7][0:TOK, :], scalar=s.tanh_g[0:TOK, 3:4],
                                             in1=s.x[:, b, :], op0=ALU.mult, op1=ALU.add).then_inc(y_added, 1)


def ternary_ffn_stage(nc, s, d, t):
    UNIT = 3
    TERNS = 2 * UNIT
    unit_of = [c // UNIT for c in range(L3_CHUNKS)]
    units = unit_of[-1] + 1
    PIECES = 2 * L3_CHUNKS
    with ExitStack() as ctx:
        def sb(n, shape, dt=F32):
            return ctx.enter_context(nc.sbuf_tensor(f"f3_{n}", shape, dt))

        below_done, tern_done, xhi_done, xlo_done, g_done, u_done, act_done, h_done, hi_done, lo_done, y_done, y_added = s.sems(
            "f3", "below_done", "tern_done", "xhi_done", "xlo_done", "g_done", "u_done", "act_done", "h_done", "hi_done",
            "lo_done", "y_done", "y_added")
        below = sb("below", [128, 2, D])
        tern = sb("tern", [128, TERNS, 3, D], F32R)
        xr = sb("xr", [128, 2, KD, NT], F32R)
        acted = sb("acted", [128, 2, HALF])
        h = sb("h", [128, 2, HALF])
        hT = sb("hT", [128, 2, 2, UNIT, NT], F32R)
        block = ctx.enter_context(nc.Block())

        def halves(half):
            return slice(half * HALF, (half + 1) * HALF)

        @block.sync
        def _(sp):
            for c in range(RAWS, L3_CHUNKS):
                sp.wait_ge(tern_done, 3 * (c - RAWS + 1))
                t.load(sp, d, c)

        @block.gpsimd
        def _(pool):
            for i in range(3 * L3_CHUNKS):
                c, m = i // 3, i % 3
                if m == 0:
                    pool.wait_ge(t.loaded[c % RAWS], 16 * (c // RAWS + 1))
                if i >= 2:
                    pool.wait_ge(tern_done, i - 1)
                pool.tensor_scalar(below[:, i % 2, :], t.raw[:, c % RAWS, m, :], t.half[:, 3 + m:4 + m], None,
                                   ALU.is_lt).then_inc(below_done, 1)

        @block.tensor
        def _(pe):
            def piece(n):
                c, half = n // 2, n % 2
                pe.wait_ge(tern_done, 3 * c + 2)
                if n >= 2:
                    pe.wait_ge(h_done, n - 1)
                for m, done in ((0, g_done), (1, u_done)):
                    for part in range(2):
                        if n < 2 and m == 0:
                            pe.wait_ge((xhi_done, xlo_done)[part], half + 1)
                        for k in range(KD):
                            mm = pe.matmul(s.bank[2 * (n % 2) + m][:, 0:HALF],
                                           tern[:, c % TERNS, m, k * 128:(k + 1) * 128],
                                           xr[:, part, k, halves(half)],
                                           start=(part == 0 and k == 0), stop=(part == 1 and k == KD - 1))
                    mm.then_inc(done, 1)

            def output(u):
                chunks = [c for c in range(L3_CHUNKS) if unit_of[c] == u]
                pe.wait_ge(tern_done, 3 * chunks[-1] + 3)
                pe.wait_ge(lo_done, 2 * chunks[-1] + 2)
                for b in range(B):
                    if u * B + b >= 4:
                        pe.wait_ge(y_added, u * B + b - 3)
                    for c in chunks:
                        for part in range(2):
                            mm = pe.matmul(s.bank[4 + b % 4][0:TOK, :],
                                           hT[:, u % 2, part, c % UNIT, b * TOK:(b + 1) * TOK],
                                           tern[:, c % TERNS, 2, :],
                                           start=(c == chunks[0] and part == 0), stop=(c == chunks[-1] and part == 1))
                    mm.then_inc(y_done, 1)

            for n in range(PIECES):
                piece(n)
                if n > 1 and n % (2 * UNIT) == 1:
                    output(unit_of[n // 2] - 1)
            output(units - 1)

        @block.scalar
        def _(act):
            for half in range(2):
                act.activation(xr[:, 0, :, halves(half)], s.xnT[:, :, halves(half)], ACT.Copy).then_inc(xhi_done, 1)
            for n in range(PIECES + 1):
                if n < PIECES:
                    act.wait_ge(g_done, n + 1)
                    if n >= 2:
                        act.wait_ge(h_done, n - 1)
                    act.activation(acted[:, n % 2, :], s.bank[2 * (n % 2)][:, 0:HALF], ACT.Silu,
                                   scale=t.scale[:, 0:1]).then_inc(act_done, 1)
                if n >= 1:
                    c, half = (n - 1) // 2, (n - 1) % 2
                    u = unit_of[c]
                    act.wait_ge(h_done, n)
                    if u >= 2:
                        act.wait_ge(y_done, (u - 1) * B)
                    act.activation(hT[:, u % 2, 0, c % UNIT, halves(half)], h[:, (n - 1) % 2, :], ACT.Copy)\
                       .then_inc(hi_done, 1)

        @block.vector
        def _(dve):
            def make_ternary(c, rows):
                for m in rows:
                    i = 3 * c + m
                    dve.wait_ge(below_done, i + 1)
                    if c >= TERNS:
                        dve.wait_ge(y_done, (unit_of[c - TERNS] + 1) * B)
                    dve.scalar_tensor_tensor(out=tern[:, c % TERNS, m, :], in0=t.raw[:, c % RAWS, m, :],
                                             scalar=t.half[:, m:m + 1], in1=below[:, i % 2, :],
                                             op0=ALU.is_gt, op1=ALU.subtract).then_inc(tern_done, 1)

            def rest_of_xnT(half):
                dve.wait_ge(xhi_done, half + 1)
                dve.tensor_tensor(xr[:, 1, :, halves(half)], s.xnT[:, :, halves(half)],
                                  xr[:, 0, :, halves(half)].bitcast(F32), ALU.subtract).then_inc(xlo_done, 1)

            def hidden(n):
                dve.wait_ge(u_done, n + 1)
                dve.wait_ge(act_done, n + 1)
                if n >= 2:
                    dve.wait_ge(hi_done, n - 1)
                    dve.wait_ge(lo_done, n - 1)
                dve.scalar_tensor_tensor(out=h[:, n % 2, :], in0=s.bank[2 * (n % 2) + 1][:, 0:HALF],
                                         scalar=t.scale[:, 1:2], in1=acted[:, n % 2, :],
                                         op0=ALU.mult, op1=ALU.mult).then_inc(h_done, 1)

            def rest_of_hidden(n):
                c, half = n // 2, n % 2
                u = unit_of[c]
                dve.wait_ge(hi_done, n + 1)
                dve.tensor_tensor(hT[:, u % 2, 1, c % UNIT, halves(half)], h[:, n % 2, :],
                                  hT[:, u % 2, 0, c % UNIT, halves(half)].bitcast(F32), ALU.subtract).then_inc(lo_done, 1)

            def add(u):
                for b in range(B):
                    dve.wait_ge(y_done, u * B + b + 1)
                    if u:
                        dve.wait_ge(y_added, (u - 1) * B + b + 1)
                    dve.scalar_tensor_tensor(out=s.x[:, b, :], in0=s.bank[4 + b % 4][0:TOK, :],
                                             scalar=t.output_scale[0:TOK, :], in1=s.x[:, b, :],
                                             op0=ALU.mult, op1=ALU.add).then_inc(y_added, 1)

            make_ternary(0, (0, 1))
            rest_of_xnT(0)
            rest_of_xnT(1)
            make_ternary(0, (2,))
            for n in range(PIECES):
                if n % 2 == 0 and n // 2 + 1 < L3_CHUNKS:
                    make_ternary(n // 2 + 1, range(3))
                hidden(n)
                if n:
                    rest_of_hidden(n - 1)
                if n > 1 and n % (2 * UNIT) == 1:
                    add(unit_of[n // 2] - 1)
            rest_of_hidden(PIECES - 1)
            add(units - 1)


def store_stage(nc, s, out):
    with ExitStack() as ctx:
        (stored,) = s.sems("store", "stored")
        block = ctx.enter_context(nc.Block())

        @block.sync
        def _(sp):
            sp.dma_start(out.rearrange("b p d -> p b d"), s.x[:, :, :]).then_inc(stored, 16)
            sp.wait_ge(stored, 16)


class Latent:

    def __init__(self, nc, ctx, s):
        def sb(name, shape):
            return ctx.enter_context(nc.sbuf_tensor(f"l0_{name}", shape, F32))

        self.kvcT = sb("kvcT", [KVC, B * T])
        self.kvc = sb("kvc", [TT, B * KT, KVC])
        self.krT = sb("krT", [128, B * T])
        self.qcT0 = sb("qcT0", [128, NT])
        self.qcT1 = sb("qcT1", [QC1, NT])
        self.mask = s.xn[:, :, :].rearrange("p b d -> p (b d)")[:, 0:B * T].rearrange("p (b t) -> p b t", b=B)
        self.masked, self.w_loaded = s.sems("l0", "masked", "w_loaded")
        self.w_uq = sb("w_uq", [HD, GH, QC])
        self.w_uk = sb("w_uk", [HD, GH, KVC])
        self.w_uv = sb("w_uv", [HD, GH, KVC])
        self.w_o = sb("w_o", [HD, GH, D])
        self.w_qr0 = sb("w_qr0", [128, 2, GH * R])
        self.w_qr1 = sb("w_qr1", [QC1, 2, GH * R])
        self.cos = sb("cos", [128, T])
        self.sin = sb("sin", [128, T])

    def load_weights(self, sp, d, g):
        one = bass.ds(g, 1)
        loads = ((self.w_uq, d["l0_w_uqT"][one].rearrange("o h p n -> p (o h) n")),
                 (self.w_uk, d["l0_w_ukT"][one].rearrange("o h p n -> p (o h) n")),
                 (self.w_uv, d["l0_w_uvT"][one].rearrange("o h p n -> p (o h) n")),
                 (self.w_o, d["l0_w_o"][one].rearrange("o h p n -> p (o h) n")),
                 (self.w_qr0, d["l0_w_qr"][one, :, 0:128].rearrange("o v p n -> p (o v) n")),
                 (self.w_qr1, d["l0_w_qr"][one, :, 128:QC].rearrange("o v p n -> p (o v) n")))
        for dst, src in loads:
            sp.dma_start(dst[:, :, :], src).then_inc(self.w_loaded, 16)


class Ternary:

    def __init__(self, nc, ctx):
        def sb(name, shape):
            return ctx.enter_context(nc.sbuf_tensor(f"l3_{name}", shape, F32))

        self.magnitudes = sb("magnitudes", [128, 3, L3_CHUNKS])
        self.total = sb("total", [128, 3])
        self.scale = sb("scale", [128, 3])
        self.half = sb("half", [128, 6])
        self.output_scale = sb("output_scale", [128, 1])

    def raws(self, nc, ctx, s):
        self.raw = ctx.enter_context(nc.sbuf_tensor("l3_raw", [128, RAWS, 3, D], F32))
        self.loaded = s.sems("l3", *[f"raw_loaded{j}" for j in range(RAWS)])

    def load(self, sp, d, c):
        sp.dma_start(self.raw[:, c % RAWS, :, :], d["l3_w_ffn"][c]).then_inc(self.loaded[c % RAWS], 16)


def build(nc, d, out, parts=range(8)):
    with ExitStack() as ctx:
        s = Chip(nc, ctx)
        t = s.ternary
        if 0 in parts:
            with ExitStack() as own:
                a = Latent(nc, own, s)
                with ExitStack() as of_projections:
                    w = ProjectWeights(nc, of_projections, s)
                    setup_stage(nc, s, d, beside=lambda sp: w.load(sp, d, a))
                    layernorm_stage(nc, s, "ln0")
                    latent_project_stage(nc, s, d, a, w)
                latent_attention_stage(nc, s, d, a)
        else:
            setup_stage(nc, s, d)
        if 1 in parts:
            routed_ffn(nc, s, d, 0, 2, 256, ACT.Gelu, softmax=False, eps=0.0)
        if 2 in parts:
            s.clear_semaphores()
            with ExitStack() as own:
                w = HeadWeights(nc, own, s)
                layernorm_stage(nc, s, "ln2", beside=lambda sp: w.load_first(sp, d))
                heads_attention_stage(nc, s, d, w)
        if 3 in parts:
            routed_ffn(nc, s, d, 1, 4, 352, ACT.Silu, softmax=True, eps=1e-20, capacity=CAP)
        if 4 in parts:
            s.clear_semaphores()
            with ExitStack() as own:
                r = Recurrence(nc, own, s)
                layernorm_stage(nc, s, "ln4", beside=lambda sp: r.load(sp, d))
                recurrence_stage(nc, s, r)
        if 5 in parts:
            routed_ffn(nc, s, d, 2, 6, 352, ACT.Silu, softmax=True, eps=1e-20)
        if 6 in parts or 7 in parts:
            s.clear_semaphores()
        if 6 in parts:
            with ExitStack() as own:
                w = CacheWeights(nc, own, s)
                layernorm_stage(nc, s, "ln6", beside=lambda sp: w.load(sp, d))
                cache_attention_stage(nc, s, d, w, t)
        s.context_life.close()
        if 7 in parts:
            with ExitStack() as own:
                t.raws(nc, own, s)
                layernorm_stage(nc, s, "ln7", beside=lambda sp: [t.load(sp, d, c) for c in range(RAWS)])
                ternary_ffn_stage(nc, s, d, t)
        store_stage(nc, s, out)


def halves_swapped(w, width):
    n = w.shape[-1] // width
    return np.ascontiguousarray(w.reshape(w.shape[0], n, 2, width // 2)[:, :, ::-1].reshape(w.shape))


def lay_out(i):
    f = {k: np.asarray(v) for k, v in i.items()}
    c = np.ascontiguousarray
    d = {"x": f["x"], "g_xattn": f["g_xattn"], "g_ffn": f["g_ffn"], "ids": c(f["itok_BxS_0_1023"].T)}
    d["ctx"] = f["ctx_2048"]
    d["ctxT"] = c(f["ctx_2048"].reshape(B * T, KD, 128).transpose(2, 1, 0))
    half = R // 2
    freq = (np.float32(1.0) / np.power(np.float32(10000.0), np.arange(half, dtype=np.float32) / np.float32(half)))
    ang = (np.arange(T, dtype=np.float32)[:, None] * freq.astype(np.float32)).astype(np.float32)
    d["cos"] = c(np.tile(np.cos(ang).T, (4, 1)).astype(np.float32))
    sin = np.sin(ang).T.astype(np.float32)
    d["sin"] = c(np.concatenate([-sin, sin, -sin, sin], axis=0))
    d["l0_w_kvc"] = f["L0_xattn_W_kvc"]
    kr = f["L0_xattn_W_kr"]
    d["l0_w_kr"] = c(np.stack([np.tile(kr, (1, 2)), np.tile(halves_swapped(kr, R), (1, 2))], axis=1))
    d["l0_w_dq"] = f["L0_xattn_W_dq"]
    d["l0_w_uqT"] = c(f["L0_xattn_W_uq"].T.reshape(NG, GH, HD, QC))
    d["l0_w_ukT"] = c(f["L0_xattn_W_uk"].T.reshape(NG, GH, HD, KVC))
    d["l0_w_uvT"] = c(f["L0_xattn_W_uv"].T.reshape(NG, GH, HD, KVC))
    d["l0_w_o"] = c(f["L0_xattn_W_o"].reshape(NG, GH, HD, D))
    qr = f["L0_xattn_W_qr"]
    both = np.stack([qr, halves_swapped(qr, R)])
    d["l0_w_qr"] = c(both.reshape(2, QC, NG, GH * R).transpose(2, 0, 1, 3))
    d["l0_router"] = f["L0_ffn_wa"]
    for name, routed, shared in (("wg", "rg", "sg"), ("wu", "rw1", "sw1"), ("wd", "rw2", "sw2")):
        d["l0_" + name] = c(np.concatenate([f["L0_ffn_" + routed], f["L0_ffn_" + shared]]))
    for name, routed, shared in (("bg", "rgb", "sgb"), ("bu", "rb1", "sb1")):
        d["l0_" + name] = c(np.concatenate([f["L0_ffn_" + routed], f["L0_ffn_" + shared]])
                            .reshape(E + 2, 2, 128).transpose(2, 0, 1))
    d["l0_bias_rows"] = c(np.stack([f["L0_ffn_rgb"], f["L0_ffn_rb1"]], axis=1))
    d["l0_bd"] = c(np.concatenate([f["L0_ffn_rb2"], f["L0_ffn_sb2"]]))
    for n in "qkv":
        w = f["L1_xattn_W" + n].T
        d[f"l1_w_{n}T"] = c(w.reshape(KD, 128, NG, 128).transpose(2, 1, 0, 3))
        d[f"l1_b_{n}"] = f["L1_xattn_b" + n] if n == "v" else c(f["L1_xattn_b" + n].reshape(NG, 128).T)
    d["l1_w_oT"] = c(f["L1_xattn_Wo"].T.reshape(NG, 128, D))
    d["l1_b_o"] = f["L1_xattn_bo"]
    d["l1_router"] = c(f["L1_ffn_gate_w"].T)
    for name, routed, shared in (("wg", "w_gate", "sw_gate"), ("wu", "w_up", "sw_up")):
        d["l1_" + name] = c(np.concatenate([f["L1_ffn_" + routed],
                                            f["L1_ffn_" + shared].reshape(D, 2, 352).transpose(1, 0, 2)]))
    d["l1_wd"] = c(np.concatenate([f["L1_ffn_w_down"], f["L1_ffn_sw_down"].reshape(2, 352, D)]))
    d["l2_router"] = c(f["L2_ffn_gate_w"].T)
    w13 = f["L2_ffn_w13"].reshape(E, 2, 352, D).transpose(1, 0, 3, 2)
    s13 = f["L2_ffn_sw13"].reshape(2, 2, 352, D).transpose(0, 1, 3, 2)
    d["l2_wg"], d["l2_wu"] = c(np.concatenate([w13[0], s13[0]])), c(np.concatenate([w13[1], s13[1]]))
    d["l2_wd"] = c(np.concatenate([f["L2_ffn_w2"].transpose(0, 2, 1), f["L2_ffn_sw2"].T.reshape(2, 352, D)]))
    d["l2_decay"] = f["L2_xattn_decay"].reshape(1)
    d["l2_w_inT"], d["l2_w_outT"] = c(f["L2_xattn_W_in"].T), c(f["L2_xattn_W_out"].T)
    d["l2_b_in"] = c(f["L2_xattn_b_in"].reshape(KD, 128).T)
    for n in ("b_out", "gamma", "beta"):
        d["l2_" + n] = f["L2_xattn_" + n]
    for n in "qkvo":
        d[f"l3_w_{n}T"] = c(f["L3_xattn_w" + n].T)
    pad = L3_CHUNKS * 128 - L3_HIDDEN
    w1, w3 = (np.pad(f["L3_ffn_w" + n].T, ((0, 0), (0, pad))).reshape(KD, 128, L3_CHUNKS, 128).transpose(2, 1, 0, 3)
              .reshape(L3_CHUNKS, 128, D) for n in "13")
    w2 = np.pad(f["L3_ffn_w2"].T, ((0, pad), (0, 0))).reshape(L3_CHUNKS, 128, D)
    d["l3_w_ffn"] = c(np.stack([w1, w3, w2], axis=2))
    return d


def kernel(**inputs):
    from concourse import bacc
    from concourse.bass_utils import run_bass_kernel_spmd

    nc = bacc.Bacc("TRN2", target_bir_lowering=False, num_devices=1)
    arrays = {f"in_{k}": v for k, v in lay_out(inputs).items()}
    dram = {k[3:]: nc.dram_tensor(k, v.shape, mybir.dt.from_np(v.dtype), kind="ExternalInput").ap()
            for k, v in arrays.items()}
    out = nc.dram_tensor("out_x", (B, TOK, D), F32, kind="ExternalOutput").ap()
    build(nc, dram, out)
    return run_bass_kernel_spmd(nc, [arrays], core_ids=[0]).results[0]["out_x"]
```
